# Optimizing a Trainium2 kernel written in Bass

```python
import numpy as np
import jax
import jax.numpy as jnp

def _softmax(x, axis=-1):
    return jax.nn.softmax(x, axis=axis)

def _gelu(x):
    return jax.nn.gelu(x, approximate=True)

def _silu(x):
    return jax.nn.silu(x)

def _sigmoid(x):
    return jax.nn.sigmoid(x)

def _layernorm(x, axis=-1, eps=1e-05):
    m = jnp.mean(x, axis=axis, keepdims=True)
    v = jnp.var(x, axis=axis, keepdims=True)
    return (x - m) / jnp.sqrt(v + eps)

def _scatter_add(tgt, idx, src, axis=0):
    return tgt.at[idx].add(src)

def _segment_sum(src, seg, n):
    return jax.ops.segment_sum(src, seg, n)
kernel_name = 'mk_audio_tower_d1_tok_aud1d768_r4_552327'

def setup_inputs(seed: int=0):
    np.random.seed(seed)
    _w = jnp.asarray

    def _rec_inputs():
        import jax
        import jax.numpy as jnp
        _rk = jax.random.key(seed)
        x = 8.9527e-05 + 1.00009 * jax.random.normal(jax.random.fold_in(_rk, 1), (4, 120000), jnp.float32)
        return x
    x = _rec_inputs()

    def _L0_tok_setup():
        import jax, jax.numpy as jnp
        import numpy as np
        from jax import lax
        CONV_LAYERS = [(128, 10, 5), (128, 3, 2), (128, 3, 2), (128, 3, 2), (128, 3, 2), (128, 2, 2)]
        NUM_GROUPS = 32
        EPS = 1e-05
        EMBED_DIM = 192

        def _block(x, cw, cb, gw, gb, stride):
            y = lax.conv_general_dilated(x, cw, (stride,), 'VALID', dimension_numbers=('NCH', 'OIH', 'NCH'))
            y = y + cb[None, :, None]
            B, C, T = y.shape
            yg = y.reshape(B, NUM_GROUPS, C // NUM_GROUPS * T)
            mu = yg.mean(axis=-1, keepdims=True)
            var = yg.var(axis=-1, keepdims=True)
            yn = ((yg - mu) * lax.rsqrt(var + EPS)).reshape(B, C, T)
            yn = yn * gw[None, :, None] + gb[None, :, None]
            return jax.nn.gelu(yn)

        def _forward(x, conv_params, pw, pb):
            h = x[:, None, :]
            for (cw, cb, gw, gb), (_, _, s) in zip(conv_params, CONV_LAYERS):
                h = _block(h, cw, cb, gw, gb, s)
            h = jnp.transpose(h, (0, 2, 1))
            return jnp.einsum('bfc,ec->bfe', h, pw) + pb
        key = jax.random.key(seed)
        ks = jax.random.split(key, 16)
        inp = {'x': jax.random.normal(ks[0], (2, 80000), dtype=jnp.float32)}
        in_c = 1
        for li, (oc, k, s) in enumerate(CONV_LAYERS):
            lim = 1.0 / np.sqrt(in_c * k)
            inp[f'cw{li}'] = jax.random.uniform(jax.random.fold_in(ks[1], li), (oc, in_c, k), jnp.float32, -lim, lim)
            inp[f'cb{li}'] = jax.random.uniform(jax.random.fold_in(ks[2], li), (oc,), jnp.float32, -lim, lim)
            inp[f'gw{li}'] = jnp.ones((oc,), jnp.float32)
            inp[f'gb{li}'] = jnp.zeros((oc,), jnp.float32)
            in_c = oc
        lim = 1.0 / np.sqrt(128)
        inp['pw'] = jax.random.uniform(ks[3], (EMBED_DIM, 128), jnp.float32, -lim, lim)
        inp['pb'] = jax.random.uniform(ks[4], (EMBED_DIM,), jnp.float32, -lim, lim)
        return inp
    _L0_tok_all = _L0_tok_setup()
    _L0_tok_in = {k: v for k, v in _L0_tok_all.items() if k in ('cw0', 'cb0', 'gw0', 'gb0', 'cw1', 'cb1', 'gw1', 'gb1', 'cw2', 'cb2', 'gw2', 'gb2', 'cw3', 'cb3', 'gw3', 'gb3', 'cw4', 'cb4', 'gw4', 'gb4', 'cw5', 'cb5', 'gw5', 'gb5', 'pw', 'pb')}
    del _L0_tok_all

    def _L0_attn_setup():
        import math
        import jax, jax.numpy as jnp
        import numpy as np
        NUM_HEADS = 12
        EPS = 0.0001

        def softmax_kernel_features(data, proj, is_query):
            d = data.shape[-1]
            data_normalizer = 1.0 / math.sqrt(math.sqrt(d))
            ratio = 1.0 / math.sqrt(proj.shape[0])
            data_dash = jnp.einsum('bhnd,md->bhnm', data_normalizer * data, proj)
            diag_data = jnp.sum(jnp.square(data), axis=-1, keepdims=True) * 0.5 * data_normalizer * data_normalizer
            if is_query:
                stab = jnp.max(data_dash, axis=-1, keepdims=True)
            else:
                stab = jnp.max(data_dash)
            return ratio * (jnp.exp(data_dash - diag_data - stab) + EPS)
        key = jax.random.key(seed)
        k0, k1, k2, k3, k4 = jax.random.split(key, 5)
        B, N, C, H = (8, 1024, 192, NUM_HEADS)
        hd = C // H
        m = int(hd * math.log(hd))
        x = jax.random.normal(k0, (B, N, C), dtype=jnp.float32)
        W_qkv = jax.random.normal(k1, (C, 3 * C), dtype=jnp.float32) / math.sqrt(C)
        W_proj = jax.random.normal(k2, (C, C), dtype=jnp.float32) / math.sqrt(C)
        b_proj = jnp.zeros((C,), dtype=jnp.float32)
        proj_mat = jax.random.normal(k3, (m, hd), dtype=jnp.float32)
        return {'x': x, 'W_qkv': W_qkv, 'W_proj': W_proj, 'b_proj': b_proj, 'proj_mat': proj_mat}
    _L0_attn_all = _L0_attn_setup()
    _L0_attn_in = {k: v for k, v in _L0_attn_all.items() if k in ('W_qkv', 'W_proj', 'b_proj', 'proj_mat')}
    del _L0_attn_all

    def _L0_ffn_setup():
        import math
        import jax, jax.numpy as jnp
        import numpy as np
        EMBED_CHOICES = [96, 144, 192]
        RATIO_CHOICES = [2, 3, 4]
        E_MAX = 192
        H_MAX = 768

        def new_gelu(x):
            c = math.sqrt(2.0 / math.pi)
            return 0.5 * x * (1.0 + jnp.tanh(c * (x + 0.044715 * x * x * x)))

        def _mixed_coeffs(alpha_e, alpha_r):
            h_idx = jnp.arange(H_MAX)
            d_idx = jnp.arange(E_MAX)
            C0 = jnp.zeros((H_MAX, E_MAX), jnp.float32)
            c0b = jnp.zeros((H_MAX,), jnp.float32)
            C1 = jnp.zeros((E_MAX, H_MAX), jnp.float32)
            c1b = jnp.zeros((E_MAX,), jnp.float32)
            for i, e in enumerate(EMBED_CHOICES):
                m_in = (d_idx < e).astype(jnp.float32)
                for j, r in enumerate(RATIO_CHOICES):
                    a = alpha_e[i] * alpha_r[j]
                    m_out = (h_idx < r * e).astype(jnp.float32)
                    C0 = C0 + a * (m_out[:, None] * m_in[None, :])
                    c0b = c0b + a * m_out
                    C1 = C1 + a * (m_in[:, None] * m_out[None, :])
                    c1b = c1b + a * m_in
            return (C0, c0b, C1, c1b)
        key = jax.random.key(seed)
        ks = jax.random.split(key, 6)
        x = jax.random.normal(ks[0], (8, 512, E_MAX), jnp.float32)
        w_fc = jax.random.normal(ks[1], (H_MAX, E_MAX), jnp.float32) * 0.02
        b_fc = jnp.zeros((H_MAX,), jnp.float32)
        w_proj = jax.random.normal(ks[2], (E_MAX, H_MAX), jnp.float32) * 0.02
        b_proj = jnp.zeros((E_MAX,), jnp.float32)
        alpha_e = jax.nn.softmax(jax.random.normal(ks[3], (3,), jnp.float32))
        alpha_r = jax.nn.softmax(jax.random.normal(ks[4], (3,), jnp.float32))
        return {'x': x, 'w_fc': w_fc, 'b_fc': b_fc, 'w_proj': w_proj, 'b_proj': b_proj, 'alpha_e': alpha_e, 'alpha_r': alpha_r}
    _L0_ffn_all = _L0_ffn_setup()
    _L0_ffn_in = {k: v for k, v in _L0_ffn_all.items() if k in ('w_fc', 'b_fc', 'w_proj', 'b_proj', 'alpha_e', 'alpha_r')}
    del _L0_ffn_all
    return {'x': x, 'L0_tok_cw0': _L0_tok_in['cw0'], 'L0_tok_cb0': _L0_tok_in['cb0'], 'L0_tok_gw0': _L0_tok_in['gw0'], 'L0_tok_gb0': _L0_tok_in['gb0'], 'L0_tok_cw1': _L0_tok_in['cw1'], 'L0_tok_cb1': _L0_tok_in['cb1'], 'L0_tok_gw1': _L0_tok_in['gw1'], 'L0_tok_gb1': _L0_tok_in['gb1'], 'L0_tok_cw2': _L0_tok_in['cw2'], 'L0_tok_cb2': _L0_tok_in['cb2'], 'L0_tok_gw2': _L0_tok_in['gw2'], 'L0_tok_gb2': _L0_tok_in['gb2'], 'L0_tok_cw3': _L0_tok_in['cw3'], 'L0_tok_cb3': _L0_tok_in['cb3'], 'L0_tok_gw3': _L0_tok_in['gw3'], 'L0_tok_gb3': _L0_tok_in['gb3'], 'L0_tok_cw4': _L0_tok_in['cw4'], 'L0_tok_cb4': _L0_tok_in['cb4'], 'L0_tok_gw4': _L0_tok_in['gw4'], 'L0_tok_gb4': _L0_tok_in['gb4'], 'L0_tok_cw5': _L0_tok_in['cw5'], 'L0_tok_cb5': _L0_tok_in['cb5'], 'L0_tok_gw5': _L0_tok_in['gw5'], 'L0_tok_gb5': _L0_tok_in['gb5'], 'L0_tok_pw': _L0_tok_in['pw'], 'L0_tok_pb': _L0_tok_in['pb'], 'L0_attn_W_qkv': _L0_attn_in['W_qkv'], 'L0_attn_W_proj': _L0_attn_in['W_proj'], 'L0_attn_b_proj': _L0_attn_in['b_proj'], 'L0_attn_proj_mat': _L0_attn_in['proj_mat'], 'L0_ffn_w_fc': _L0_ffn_in['w_fc'], 'L0_ffn_b_fc': _L0_ffn_in['b_fc'], 'L0_ffn_w_proj': _L0_ffn_in['w_proj'], 'L0_ffn_b_proj': _L0_ffn_in['b_proj'], 'L0_ffn_alpha_e': _L0_ffn_in['alpha_e'], 'L0_ffn_alpha_r': _L0_ffn_in['alpha_r']}

def reference(x, L0_tok_cw0, L0_tok_cb0, L0_tok_gw0, L0_tok_gb0, L0_tok_cw1, L0_tok_cb1, L0_tok_gw1, L0_tok_gb1, L0_tok_cw2, L0_tok_cb2, L0_tok_gw2, L0_tok_gb2, L0_tok_cw3, L0_tok_cb3, L0_tok_gw3, L0_tok_gb3, L0_tok_cw4, L0_tok_cb4, L0_tok_gw4, L0_tok_gb4, L0_tok_cw5, L0_tok_cb5, L0_tok_gw5, L0_tok_gb5, L0_tok_pw, L0_tok_pb, L0_attn_W_qkv, L0_attn_W_proj, L0_attn_b_proj, L0_attn_proj_mat, L0_ffn_w_fc, L0_ffn_b_fc, L0_ffn_w_proj, L0_ffn_b_proj, L0_ffn_alpha_e, L0_ffn_alpha_r):
    import jax
    import jax.numpy as jnp

    def _L0_tok_ref(x, cw0, cb0, gw0, gb0, cw1, cb1, gw1, gb1, cw2, cb2, gw2, gb2, cw3, cb3, gw3, gb3, cw4, cb4, gw4, gb4, cw5, cb5, gw5, gb5, pw, pb):
        import jax, jax.numpy as jnp
        import numpy as np
        from jax import lax
        CONV_LAYERS = [(128, 10, 5), (128, 3, 2), (128, 3, 2), (128, 3, 2), (128, 3, 2), (128, 2, 2)]
        NUM_GROUPS = 32
        EPS = 1e-05
        EMBED_DIM = 192

        def _block(x, cw, cb, gw, gb, stride):
            y = lax.conv_general_dilated(x, cw, (stride,), 'VALID', dimension_numbers=('NCH', 'OIH', 'NCH'))
            y = y + cb[None, :, None]
            B, C, T = y.shape
            yg = y.reshape(B, NUM_GROUPS, C // NUM_GROUPS * T)
            mu = yg.mean(axis=-1, keepdims=True)
            var = yg.var(axis=-1, keepdims=True)
            yn = ((yg - mu) * lax.rsqrt(var + EPS)).reshape(B, C, T)
            yn = yn * gw[None, :, None] + gb[None, :, None]
            return jax.nn.gelu(yn)

        def _forward(x, conv_params, pw, pb):
            h = x[:, None, :]
            for (cw, cb, gw, gb), (_, _, s) in zip(conv_params, CONV_LAYERS):
                h = _block(h, cw, cb, gw, gb, s)
            h = jnp.transpose(h, (0, 2, 1))
            return jnp.einsum('bfc,ec->bfe', h, pw) + pb
        conv_params = [(cw0, cb0, gw0, gb0), (cw1, cb1, gw1, gb1), (cw2, cb2, gw2, gb2), (cw3, cb3, gw3, gb3), (cw4, cb4, gw4, gb4), (cw5, cb5, gw5, gb5)]
        return _forward(x, conv_params, pw, pb)

    def _L0_attn_ref(x, W_qkv, W_proj, b_proj, proj_mat):
        import math
        import jax, jax.numpy as jnp
        import numpy as np
        NUM_HEADS = 12
        EPS = 0.0001

        def softmax_kernel_features(data, proj, is_query):
            d = data.shape[-1]
            data_normalizer = 1.0 / math.sqrt(math.sqrt(d))
            ratio = 1.0 / math.sqrt(proj.shape[0])
            data_dash = jnp.einsum('bhnd,md->bhnm', data_normalizer * data, proj)
            diag_data = jnp.sum(jnp.square(data), axis=-1, keepdims=True) * 0.5 * data_normalizer * data_normalizer
            if is_query:
                stab = jnp.max(data_dash, axis=-1, keepdims=True)
            else:
                stab = jnp.max(data_dash)
            return ratio * (jnp.exp(data_dash - diag_data - stab) + EPS)
        B, N, C = x.shape
        H = NUM_HEADS
        hd = C // H
        qkv = (x @ W_qkv).reshape(B, N, 3, H, hd)
        qkv = jnp.transpose(qkv, (2, 0, 3, 1, 4))
        q, k, v = (qkv[0], qkv[1], qkv[2])
        q1 = softmax_kernel_features(q, proj_mat, is_query=True)
        k1 = softmax_kernel_features(k, proj_mat, is_query=False)
        kv = jnp.einsum('bhnm,bhnd->bhmd', k1, v)
        ksum = jnp.sum(k1, axis=2)
        z = 1.0 / jnp.einsum('bhnm,bhm->bhn', q1, ksum)
        out = jnp.einsum('bhnm,bhmd->bhnd', q1, kv) * z[..., None]
        out = jnp.transpose(out, (0, 2, 1, 3)).reshape(B, N, C)
        return out @ W_proj + b_proj

    def _L0_ffn_ref(x, w_fc, b_fc, w_proj, b_proj, alpha_e, alpha_r):
        import math
        import jax, jax.numpy as jnp
        import numpy as np
        EMBED_CHOICES = [96, 144, 192]
        RATIO_CHOICES = [2, 3, 4]
        E_MAX = 192
        H_MAX = 768

        def new_gelu(x):
            c = math.sqrt(2.0 / math.pi)
            return 0.5 * x * (1.0 + jnp.tanh(c * (x + 0.044715 * x * x * x)))

        def _mixed_coeffs(alpha_e, alpha_r):
            h_idx = jnp.arange(H_MAX)
            d_idx = jnp.arange(E_MAX)
            C0 = jnp.zeros((H_MAX, E_MAX), jnp.float32)
            c0b = jnp.zeros((H_MAX,), jnp.float32)
            C1 = jnp.zeros((E_MAX, H_MAX), jnp.float32)
            c1b = jnp.zeros((E_MAX,), jnp.float32)
            for i, e in enumerate(EMBED_CHOICES):
                m_in = (d_idx < e).astype(jnp.float32)
                for j, r in enumerate(RATIO_CHOICES):
                    a = alpha_e[i] * alpha_r[j]
                    m_out = (h_idx < r * e).astype(jnp.float32)
                    C0 = C0 + a * (m_out[:, None] * m_in[None, :])
                    c0b = c0b + a * m_out
                    C1 = C1 + a * (m_in[:, None] * m_out[None, :])
                    c1b = c1b + a * m_in
            return (C0, c0b, C1, c1b)
        C0, c0b, C1, c1b = _mixed_coeffs(alpha_e, alpha_r)
        W0 = w_fc * C0
        b0 = b_fc * c0b
        h = jnp.einsum('bte,he->bth', x, W0) + b0
        h = new_gelu(h)
        W1 = w_proj * C1
        b1 = b_proj * c1b
        out = jnp.einsum('bth,eh->bte', h, W1) + b1
        return out
    h = _L0_tok_ref(x, L0_tok_cw0, L0_tok_cb0, L0_tok_gw0, L0_tok_gb0, L0_tok_cw1, L0_tok_cb1, L0_tok_gw1, L0_tok_gb1, L0_tok_cw2, L0_tok_cb2, L0_tok_gw2, L0_tok_gb2, L0_tok_cw3, L0_tok_cb3, L0_tok_gw3, L0_tok_gb3, L0_tok_cw4, L0_tok_cb4, L0_tok_gw4, L0_tok_gb4, L0_tok_cw5, L0_tok_cb5, L0_tok_gw5, L0_tok_gb5, L0_tok_pw, L0_tok_pb)
    h = h + _L0_attn_ref(_layernorm(h, axis=-1), L0_attn_W_qkv, L0_attn_W_proj, L0_attn_b_proj, L0_attn_proj_mat)
    h = h + _L0_ffn_ref(_layernorm(h, axis=-1), L0_ffn_w_fc, L0_ffn_b_fc, L0_ffn_w_proj, L0_ffn_b_proj, L0_ffn_alpha_e, L0_ffn_alpha_r)
    return h

_drawn_inputs = setup_inputs


def setup_inputs(seed=0):
    import zlib

    import numpy as np

    out = dict(_drawn_inputs(seed))
    spreads = {'L0_tok_gw0': (1.0, 0.2),
     'L0_tok_gb0': (0.0, 0.1),
     'L0_tok_gw1': (1.0, 0.2),
     'L0_tok_gb1': (0.0, 0.1),
     'L0_tok_gw2': (1.0, 0.2),
     'L0_tok_gb2': (0.0, 0.1),
     'L0_tok_gw3': (1.0, 0.2),
     'L0_tok_gb3': (0.0, 0.1),
     'L0_tok_gw4': (1.0, 0.2),
     'L0_tok_gb4': (0.0, 0.1),
     'L0_tok_gw5': (1.0, 0.2),
     'L0_tok_gb5': (0.0, 0.1),
     'L0_attn_b_proj': (0.0, 0.1),
     'L0_ffn_b_fc': (0.0, 0.297),
     'L0_ffn_b_proj': (0.0, 0.1)}
    factors = {'L0_ffn_alpha_r': 3.466}
    for name, (base, spread) in spreads.items():
        noise = np.random.default_rng([zlib.crc32(name.encode()), seed]).standard_normal(out[name].shape)
        drawn = base * np.exp(spread * noise) if base else spread * noise
        out[name] = jnp.asarray(drawn.astype(out[name].dtype))
    for name, factor in factors.items():
        out[name] = (out[name] * factor).astype(out[name].dtype)
    return out
```

```python
import math
from contextlib import ExitStack

import numpy as np
import concourse.bass as bass
from concourse import mybir

ALU = mybir.AluOpType
ACT = mybir.ActivationFunctionType
AX_X = mybir.AxisListType.X
F32 = mybir.dt.float32
F16 = mybir.dt.float16
I32 = mybir.dt.int32
GELU = ACT.Gelu_apprx_tanh

B = 4
L = 120000
C = 128
P = 125
SP = L // P
K0, S0 = 10, 5
ROWS = [SP // S0 >> n for n in range(6)]
VALID = [P * r - 1 for r in ROWS]
XW = SP + S0
CH = 4
CS = CH * S0
CW = CS + S0
NCH = SP // CS
TK = 4 * CW
UR = 8
UC = UR * P
OC = UC // 2
TAPS = [K0, 3, 3, 3, 3, 2]
EPS = 1e-5
BUFR = UR + 2
PL = BUFR * P


R = ROWS[5]
E = 192
E1 = E - C
HEADS, HD, M = 12, 16, 44
FE = HEADS * M
FA = 8 * M
GR = HEADS // 2
VW = HD + 1
HID = 768
HT = HID // C
HALF = R * P // 2
NORM = 1.0 / math.sqrt(math.sqrt(HD))
RATIO = 1.0 / math.sqrt(M)
FEPS = 1e-4
EMBEDS, RATIOS = (96, 144, 192), (2, 3, 4)
SEG = ((0, 96), (96, 144), (144, 192))


class Slot:

    def __init__(self, stream, layer, batch, j, rows=UR, final=False):
        self.stream, self.layer, self.batch, self.j, self.rows, self.final = stream, layer, batch, j, rows, final
        self.par = j % 2


def plan():
    slots, loops = [], []

    def a(b, j):
        return Slot("A", 1, b, j)

    def layer_b(n, b):
        return [Slot("B", n, b, j) for j in range(ROWS[n - 1] // UR)] + [Slot("B", n, b, ROWS[n - 1] // UR, final=True)]

    def a_end(b):
        return Slot("A", 1, b, ROWS[0] // UR, final=True)

    def loop(body, times):
        first = len(slots)
        for i in range(times):
            slots.extend(body(i))
        size = (len(slots) - first) // times
        if times > 3:
            loops.append((first + size, size, times - 2))

    na = ROWS[0] // UR
    loop(lambda i: [a(0, 2 * i), a(0, 2 * i + 1)], na // 2)
    slots.append(a_end(0))
    for b in range(1, B):
        l2, l3, l4 = (layer_b(n, b - 1) for n in (2, 3, 4))
        loop(lambda i: [a(b, 2 * i), l2[2 * i], a(b, 2 * i + 1), l2[2 * i + 1]], 6)
        slots.extend([l2[12], a(b, 12)])
        loop(lambda i: [l3[2 * i], a(b, 13 + 2 * i), l3[2 * i + 1], a(b, 14 + 2 * i)], 3)
        slots.extend([l3[6], a(b, 19), l4[0], a(b, 20), l4[1], a(b, 21), l4[2], a(b, 22), l4[3], a(b, 23)])
        slots.extend([Slot("B", 5, b - 1, 0), Slot("B", 5, b - 1, 1, rows=4), a_end(b)])
    l2, l3, l4 = (layer_b(n, B - 1) for n in (2, 3, 4))
    loop(lambda i: l2[2 * i:2 * i + 2], 6)
    slots.append(l2[12])
    loop(lambda i: l3[2 * i:2 * i + 2], 3)
    slots.append(l3[6])
    slots.extend(l4)
    slots.extend([Slot("B", 5, B - 1, 0), Slot("B", 5, B - 1, 1, rows=4)])
    return slots, loops


def number(slots):
    g = h = l0 = gn = 0
    last = {}
    finals = {}
    for s, u in enumerate(slots):
        u.c = s
        u.g, u.l0, u.nxt, u.bank = 0, 0, None, s % 2
        if not u.final:
            u.g = g
            u.slot_g = g % 2
            g += 1
        if u.stream == "A" and not u.final:
            u.l0 = l0
            l0 += 1
        u.head = not u.final and u.j == 0
        u.last_of_layer = u.final or (u.layer == 5 and u.j == 1)
        u.size = P if u.final else u.rows * P // 2
    by = {"A": [u for u in slots if u.stream == "A"], "B": [u for u in slots if u.stream == "B"]}
    for st in by.values():
        units = [u for u in st if not u.final]
        for n, u in enumerate(units):
            u.nxt = units[n + 1] if n + 1 < len(units) and units[n + 1].j == u.j + 1 and u.layer != 5 else None
            prev = [v for v in st if v.c < u.c]
            same = [v for v in prev if (not v.final and v.par == u.par)]
            u.buf_free = same[-1].c + 1 if same else 0
            if same:
                for v in prev:
                    if v.final and v.c > same[-1].c and (v.j - 1) % 2 == u.par:
                        u.buf_free = max(u.buf_free, v.c + 1)
            u.all_before = prev[-1].c + 1 if prev else 0
            u.nxt_g = u.nxt.g + 1 if u.nxt is not None else 0
            u.l0_wait = units[n - 2].g + 1 if u.stream == "A" and n >= 2 else 0
    ends = {(u.layer, u.batch): u for u in slots if u.last_of_layer}
    for u in slots:
        u.before, u.after, u.gn, u.tail = [], [], None, 0
    for u in slots:
        if u.last_of_layer:
            u.gn = gn
            gn += 1
        u.need_halo = 0
    lead = slots[:2]
    for u in slots:
        u.coef_need = 1 if u.layer == 1 else ends[(u.layer - 1, u.batch)].gn + 2
        u.n_stats = u.j + 1
    for u in slots:
        if u.final or u in lead:
            continue
        at = u.c - 2
        dep = ends.get((u.layer - 1, u.batch)) if u.layer > 1 else None
        if dep is not None and dep.c >= at:
            slots[dep.c].after.append(u)
        else:
            slots[at].before.append(u)
    issued = len(lead)
    for u in slots:
        issued += len(u.before)
        u.read = issued - 1
        issued += len(u.after)
    for u in slots:
        u.tails = []
    for u in slots:
        if not u.final and u.nxt is not None:
            slots[max(u.c, u.nxt.c - 2)].tails.append(u)
    order = []
    for u in lead:
        order.append(("head", u)) if u.head else None
    for u in slots:
        for v in u.before:
            if v.head and v.layer != 5:
                order.append(("head", v))
        for v in u.tails:
            order.append(("tail", v))
        for v in u.after:
            if v.head and v.layer != 5:
                order.append(("head", v))
    for n, (kind, u) in enumerate(order):
        if kind == "head":
            u.head_copy = n + 1
        else:
            u.tail = n + 1
    for st in by.values():
        units = [u for u in st if not u.final]
        for n, u in enumerate(units):
            u.need_halo = 0
            if u.layer != 5 and u.j == 1:
                u.need_halo = units[n - 1].head_copy
            elif u.layer != 5 and u.j >= 2:
                u.need_halo = units[n - 2].tail
            u.halo_read = 0
            same = [v for v in units[:n] if v.par == u.par]
            if same:
                v = same[-1]
                m = units.index(v)
                reads = []
                if v.head and v.layer != 5:
                    reads.append(v.head_copy)
                if m >= 1 and units[m - 1].nxt is v:
                    reads.append(units[m - 1].tail)
                u.halo_read = max(reads, default=0)
    return lead, gn


def moved(u, i, later):
    v = Slot(u.stream, u.layer, u.batch, u.j + i * (later.j - u.j), u.rows, u.final)
    v.par, v.size, v.head, v.nxt, v.last_of_layer = u.par, u.size, u.head, u.nxt, u.last_of_layer
    v.bank, v.slot_g = u.c % 2, u.g % 2
    v.c = u.c + i * (later.c - u.c)
    v.g = u.g + i * (later.g - u.g)
    v.buf_free = u.buf_free + i * (later.buf_free - u.buf_free)
    v.need_halo = u.need_halo + i * (later.need_halo - u.need_halo)
    v.halo_read = u.halo_read + i * (later.halo_read - u.halo_read)
    v.nxt_g = u.nxt_g + i * (later.nxt_g - u.nxt_g)
    v.l0 = u.l0 + i * (later.l0 - u.l0)
    v.l0_wait = u.l0_wait + i * (later.l0_wait - u.l0_wait)
    v.read = u.read + i * (later.read - u.read)
    v.gn, v.tails = None, [v]
    return v


def take(eng, slots, loops, work):
    s = 0
    spans = {first: (size, times) for first, size, times in loops}
    while s < len(slots):
        if s in spans:
            size, times = spans[s]
            with eng.Fori(0, times) as i:
                for k in range(size):
                    t, later = slots[s + k], slots[s + size + k]
                    work(moved(t, i, later), [moved(x, i, y) for x, y in zip(t.before, later.before)], [])
            s += size * times
        else:
            t = slots[s]
            work(t, t.before, t.after)
            s += 1


def is_zero(n):
    return isinstance(n, int) and n == 0


def is_low(n, least):
    return isinstance(n, int) and n < least


def needs(t, p):
    return not t.final and t.layer == p.layer + 1 and t.batch == p.batch and t.head


def audio_tower(nc, x, w, par, t_in, out):
    slots, loops = plan()
    lead, n_gn = number(slots)
    outer, ctx = ExitStack(), ExitStack()
    h5 = outer.enter_context(nc.sbuf_tensor("h5", [C, B, R * P], F32))
    sb = lambda name, shape, dt=F32: ctx.enter_context(nc.sbuf_tensor(name, shape, dt))
    psum = lambda name, shape, dt=F32: ctx.enter_context(nc.psum_tensor(name, shape, dt))
    sem = lambda name: ctx.enter_context(nc.semaphore(name))

    y = [None] + [sb(f"y{n}", [C, (ROWS[n] + (n < 5)) * P]) for n in range(1, 6)]
    place = [0]

    def early(words):
        place[0] += words
        return y[1][:, place[0] - words:place[0]]

    wn = [early(C * TAPS[n] if n else K0 + 2) for n in range(6)]
    wn[0] = wn[0][:, 0:K0]
    wh = early(C * 3 // 2).bitcast(F16)
    wl = early(C * 3 // 2).bitcast(F16)
    w0h = sb("w0h", [C, K0], F16)
    w0l = sb("w0l", [C, K0], F16)
    w0pad = sb("w0pad", [C, CH, CW])
    w0pad16 = sb("w0pad16", [C, CH, TK], F16)
    w0T = sb("w0T", [CW, CH, C])
    w0T16 = sb("w0T16", [TK, CH, C], F16)
    wT = [None] + [sb(f"wT{n}", [C, 2, TAPS[n], C], F16) for n in range(1, 6)]
    pars = sb("pars", [C, 6, 3])
    big = sb("big", [C, 6 + B])
    bigall = sb("bigall", [C, 6 + B])
    pow2 = sb("pow2", [C, 6 + B])
    inv2 = sb("inv2", [C, 6 + B])
    up = sb("up", [C, 6 + B])
    down = sb("down", [C, 6])
    unscale = sb("unscale", [C, 6 + B])
    unscale2 = sb("unscale2", [C, 6])
    ident = sb("ident", [C, C])
    ident16 = sb("ident16", [C, C], F16)
    quad = sb("quad", [C, C])
    ones = sb("ones", [C, C])
    mhalf = sb("mhalf", [C, B])
    x16 = sb("x16", [P, B, XW, 4], F16)
    xlast = sb("xlast", [C, B, S0])
    gram = sb("gram", [CW, B, CW])
    xsum = early(B * CW)[0:P, :].rearrange("p (b s) -> p b s", b=B)
    energy = early(B * CH * CW).rearrange("p (b s) -> p b s", b=B)
    acc = sb("acc", [C, 4, B])
    stat0 = sb("stat0", [C, B, 2])
    x0T = sb("x0T", [TK, 2, NCH, P], F16)
    xs = y[2][0:P, 0:B * XW].rearrange("p (b s) -> p b s", b=B)
    geluf = sb("geluf", [C, 2, UC])
    ring = {s: sb(f"ring{s}", [C, 2, 2, PL], F16) for s in "AB"}
    wrap = {s: sb(f"wrap{s}", [C, 2, P], F16) for s in "AB"}
    bst = {s: sb(f"bst{s}", [C, 25 * 6]) for s in "AB"}
    mv = sb("mv", [C, 2])
    gs = sb("gs", [C, 16])
    coef0 = sb("coef0", [C, B, 2])
    coef = sb("coef", [C, 6, 2])

    p_l0 = psum("p_l0", [C, 4, 512])
    p_y = psum("p_y", [C, 2, 512])
    p_t = psum("p_t", [C, 512])
    p_m = psum("p_m", [C, 512])
    p_m16 = p_m[:, :].bitcast(F16)

    loaded_x, loaded_w, loaded_p = sem("loaded_x"), [sem(f"loaded_w{n}") for n in range(6)], sem("loaded_p")
    zeroed, halo0 = sem("zeroed"), sem("halo0")
    made_ident, made_quad, made_big = sem("made_ident"), sem("made_quad"), sem("made_big")
    all_big = sem("all_big")
    dve = sem("dve")
    w_split, w_turned, w_kept = sem("w_split"), sem("w_turned"), sem("w_kept")
    g_done, g_kept, u_done = sem("g_done"), sem("g_kept"), sem("u_done")
    x_split = sem("x_split")
    t_mm, t_kept = sem("t_mm"), sem("t_kept")
    l0_done, gelu_done, hi_done, lo_done, halo_done = sem("l0_done"), sem("gelu_done"), sem("hi_done"), sem("lo_done"), sem("halo_done")
    conv_done, evac_done = sem("conv_done"), sem("evac_done")
    gn_stat, gn_group, gn_var, gn_pow, gn_coef = sem("gn_stat"), sem("gn_group"), sem("gn_var"), sem("gn_pow"), sem("gn_coef")
    emb_done = sem("emb_done")

    block = ctx.enter_context(nc.Block())

    def buf(t, parts, ap, off=0):
        row = 1
        for d in t.shape[1:]:
            row *= d
        return bass.AP(t, off, [[row, parts]] + ap)

    def ring_rows(u, plane, row, ap):
        return buf(ring[u.stream], C, ap, off=(u.par * 2 + plane) * PL + row * P)

    def first_row(u):
        return [[P, CH], [CH * P, 2], [1, P]] if u.stream == "A" else [[1, u.rows * P]]

    def split_ap(t, u):
        return buf(t, C, [[2 * P, CH], [P, 2], [1, P]] if u.stream == "A" else [[1, u.rows * P]], off=u.slot_g * UC)

    def y_out(u):
        return y[u.layer][:, bass.ds(u.j * OC, u.size)]

    @block.sync
    def _(sp):
        sp.wait_ge(halo0, 1)
        for b in range(B):
            for p0, p1, n in ((0, 112, XW), (112, P - 1, XW), (P - 1, P, SP)):
                sp.dma_start(xs[p0:p1, b, 0:n], bass.AP(x.tensor, b * L + p0 * SP, [[SP, p1 - p0], [1, n]])).then_inc(loaded_x, 16)
        sp.dma_start(xlast[:, :, :], bass.AP(x.tensor, L - S0, [[0, C], [L, B], [1, S0]])).then_inc(loaded_x, 16)

    @block.gpsimd
    def _(pool):
        pool.memset(ident[:, :], 0.0).then_inc(zeroed, 1)
        pool.memset(ident16[:, :], 0.0).then_inc(zeroed, 1)
        pool.memset(quad[:, :], 0.25).then_inc(zeroed, 1)
        pool.memset(mhalf[:, :], -0.5).then_inc(zeroed, 1)
        for s in "AB":
            pool.memset(ring[s][:, :, :, :], 0.0).then_inc(zeroed, 1)
        pool.wait_ge(zeroed, 6)
        for m in (ident, ident16):
            pool.affine_select(out=m[:, :], in_=m[:, :], compare_op=ALU.not_equal, fill=1.0, base=0,
                               pattern=[[-1, C]], channel_multiplier=1).then_inc(made_ident, 1)
        q = quad[:, :].rearrange("p (g c) -> p g c", c=4)
        pool.affine_select(out=q, in_=q, compare_op=ALU.is_ge, fill=0.0, base=0,
                           pattern=[[-4, 32], [0, 4]], channel_multiplier=1).then_inc(made_quad, 1)
        pool.wait_ge(made_quad, 1)
        pool.affine_select(out=q, in_=q, compare_op=ALU.is_ge, fill=0.0, base=3,
                           pattern=[[4, 32], [0, 4]], channel_multiplier=-1).then_inc(made_quad, 1)
        pool.wait_ge(made_big, 1)
        pool.partition_all_reduce(bigall[:, 6:6 + B], big[:, 6:6 + B], C, bass.bass_isa.ReduceOp.max).then_inc(all_big, 1)

        def power(n, v):
            pool.wait_ge(gn_var, n)
            pool.tensor_tensor(v, v, mhalf[:, 0:v.shape[1]], ALU.pow).then_inc(gn_pow, 1)

        power(1, gs[:, 0:B])

        for t in slots:
            if t.gn is not None:
                power(t.gn + 2, gs[:, 0:1])

    @block.scalar
    def _(act):
        for n in range(6):
            act.dma_start(wn[n][:, :], w[n]).then_inc(loaded_w[n], 16)
        for n in range(6):
            for k in range(3):
                act.dma_start(pars[:, n, k:k + 1], par[n][k].rearrange("(c o) -> c o", o=1)).then_inc(loaded_p, 16)
        for n in range(6):
            act.wait_ge(w_turned, n + 1)
            if n == 0:
                nc.scalar.copy(w0T16[:, :, :], p_m16[0:TK, 0:CH * C].rearrange("p (i c) -> p i c", i=CH)).then_inc(w_kept, 1)
            else:
                nc.scalar.copy(wT[n][:, :, :, :], p_m16[:, 0:2 * TAPS[n] * C]
                         .rearrange("p (s k c) -> p s k c", s=2, k=TAPS[n])).then_inc(w_kept, 1)
        act.wait_ge(w_turned, 7)
        nc.scalar.copy(w0T[:, :, :], p_m[0:CW, 0:CH * C].rearrange("p (i c) -> p i c", i=CH)).then_inc(w_kept, 1)

        def gelu(u):
            if u.head:
                act.wait_ge(gn_coef, u.coef_need)
            if u.stream == "A":
                act.wait_ge(l0_done, u.l0 + 1)
                src = p_l0[:, 2 * u.par:2 * u.par + 2, 0:2 * CH * P // 2]
                cf = coef0[:, u.batch, :]
                dst = buf(geluf, C, [[UC // 2, 2], [1, UC // 2]], off=u.slot_g * UC)
            else:
                src = y[u.layer - 1][:, bass.ds(u.j * UC + P, u.rows * P)]
                cf = coef[:, u.layer - 1, :]
                dst = geluf[:, u.slot_g, 0:u.rows * P]
            if not is_low(u.g, 2):
                act.wait_ge(hi_done, u.g - 1)
                act.wait_ge(lo_done, u.g - 1)
            nc.scalar.activation(dst, src, GELU, bias=cf[:, 1:2], scale=cf[:, 0:1]).then_inc(gelu_done, 1)
            if not is_zero(u.buf_free):
                act.wait_ge(conv_done, u.buf_free)
            if not is_zero(u.halo_read):
                act.wait_ge(halo_done, u.halo_read)
            act.wait_ge(gelu_done, u.g + 1)
            nc.scalar.copy(ring_rows(u, 0, 2, first_row(u)), split_ap(geluf, u)).then_inc(hi_done, 1)

        for u in lead:
            gelu(u)

        def work(t, before, after):
            for u in before:
                gelu(u)
            act.wait_ge(conv_done, t.c + 1)
            act.wait_ge(gelu_done, t.read)
            if t.layer == 5 and t.head and t.batch:
                act.wait_ge(emb_done, t.batch)
            nc.scalar.copy(y_out(t), p_y[:, t.bank, 0:t.size]).then_inc(evac_done, 1)
            if t.layer == 5 and t.last_of_layer:
                act.wait_ge(gn_coef, t.gn + 2)
                nc.scalar.activation(h5[:, t.batch, :], y[5][:, :], GELU, bias=coef[:, 5, 1:2], scale=coef[:, 5, 0:1]).then_inc(emb_done, 1)
            for u in after:
                gelu(u)

        take(act, slots, loops, work)

    @block.vector
    def _(v):
        chain = [0]

        def link(ins):
            chain[0] += 1
            ins.then_inc(dve, 1)
            v.wait_ge(dve, chain[0])

        v.memset(xs[:, :, SP:XW], 0.0).then_inc(halo0, 1)
        v.memset(ones[:, :], 1.0).then_inc(made_ident, 1)
        v.memset(big[:, :], 0.0)
        v.memset(w0pad[:, :, :], 0.0)
        link(v.memset(w0pad16[:, :, :], 0.0))
        for n in range(6):
            v.wait_ge(loaded_w[n], 16)
            v.tensor_reduce(big[:, n:n + 1], wn[n][:, :], AX_X, ALU.max, apply_absolute_value=True)
        v.wait_ge(loaded_x, 16 * (3 * B + 1))
        link(v.tensor_reduce(big[0:P, 6:6 + B], xs, AX_X, ALU.max, apply_absolute_value=True))
        v.tensor_copy(bigall[:, 0:6], big[:, 0:6]).then_inc(made_big, 1)
        v.wait_ge(made_big, 1)
        v.wait_ge(all_big, 1)
        link(v.tensor_scalar(bigall[:, :], bigall[:, :], 1e-30, None, ALU.max))
        link(v.tensor_scalar(pow2[:, :].bitcast(I32), bigall[:, :].bitcast(I32), 0x7F800000, None, ALU.bitwise_and))
        link(v.reciprocal(inv2[:, :], pow2[:, :]))
        v.tensor_scalar(up[:, 0:6], inv2[:, 0:6], 16.0, None, ALU.mult)
        v.tensor_scalar(up[:, 6:6 + B], inv2[:, 6:6 + B], 64.0, None, ALU.mult)
        v.tensor_scalar(unscale[:, 6:6 + B], pow2[:, 6:6 + B], 1.0 / 64, None, ALU.mult)
        link(v.tensor_scalar(unscale[:, 0:6], pow2[:, 0:6], 1.0 / 16, None, ALU.mult))
        v.tensor_tensor(unscale2[:, :], unscale[:, 0:6], unscale[:, 0:6], ALU.mult)
        link(v.tensor_scalar(unscale[:, 6:6 + B], unscale[:, 6:6 + B], unscale[:, 0:1], None, ALU.mult))
        link(v.tensor_scalar(w0h[:, :], wn[0][:, :], up[:, 0:1], None, ALU.mult))
        link(v.scalar_tensor_tensor(out=w0l[:, :], in0=wn[0][:, :], scalar=up[:, 0:1], in1=w0h[:, :], op0=ALU.mult, op1=ALU.subtract))
        for part, t in ((0, w0h), (1, w0l)):
            for s in range(2):
                v.tensor_copy(buf(w0pad16, C, [[TK + 4 * S0, CH], [4, K0]], off=2 * part + s),
                              buf(t, C, [[0, CH], [1, K0]]))
        v.tensor_copy(buf(w0pad, C, [[CW + S0, CH], [1, K0]]), buf(y[1], C, [[0, CH], [1, K0]])).then_inc(w_split, 1)
        for b in range(B):
            link(v.tensor_scalar(x16[:, b, :, 0], xs[:, b, :], up[0:P, 6 + b:7 + b], None, ALU.mult))
            link(v.scalar_tensor_tensor(out=x16[:, b, :, 1], in0=xs[:, b, :], scalar=up[0:P, 6 + b:7 + b], in1=x16[:, b, :, 0],
                                        op0=ALU.mult, op1=ALU.subtract))
            v.tensor_copy(x16[:, b, :, 2:4].bitcast(I32), x16[:, b, :, 0:2].bitcast(I32)).then_inc(x_split, 1)
            v.tensor_reduce(xsum[:, b, :], buf(y[2], P, [[1, CW], [CS, NCH]], off=b * XW), AX_X, ALU.add).then_inc(x_split, 1)
        for n in range(1, 6):
            w_n = C * TAPS[n]
            if n > 1:
                v.wait_ge(w_turned, n)
            link(v.tensor_scalar(wh[:, 0:w_n], wn[n][:, :], up[:, n:n + 1], None, ALU.mult))
            v.scalar_tensor_tensor(out=wl[:, 0:w_n], in0=wn[n][:, :], scalar=up[:, n:n + 1], in1=wh[:, 0:w_n],
                                   op0=ALU.mult, op1=ALU.subtract).then_inc(w_split, 1)
        v.wait_ge(g_done, 1)
        v.tensor_copy(gram[:, :, :], p_t[0:CW, 0:B * CW].rearrange("p (b s) -> p b s", b=B)).then_inc(g_kept, 1)
        v.wait_ge(u_done, 1)
        for b in range(B):
            last = v.tensor_tensor_reduce(out=energy[:, b, :], in0=w0pad[:, :, :].rearrange("p i s -> p (i s)"), in1=p_y[:, 0, b * CH * CW:(b + 1) * CH * CW],
                                   scale=1.0, scalar=0.0, op0=ALU.mult, op1=ALU.add, accum_out=acc[:, 0, b:b + 1])
        link(last)
        v.wait_ge(u_done, 2)
        for b in range(B):
            v.tensor_tensor_reduce(out=energy[:, b, :].rearrange("p (i s) -> p i s", i=CH), in0=w0pad[:, :, :],
                                   in1=bass.AP(p_m, b * CW, [[512, C], [0, CH], [1, CW]]),
                                   scale=1.0, scalar=0.0, op0=ALU.mult, op1=ALU.add, accum_out=acc[:, 1, b:b + 1])
            last = v.tensor_tensor_reduce(out=xlast[:, b, :], in0=wn[0][:, 0:S0], in1=xlast[:, b, :],
                                          scale=1.0, scalar=0.0, op0=ALU.mult, op1=ALU.add, accum_out=acc[:, 2, b:b + 1])
        link(last)
        link(v.tensor_tensor(acc[:, 3, :], acc[:, 2, :], acc[:, 2, :], ALU.mult))
        v.tensor_tensor(acc[:, 0, :], acc[:, 0, :], acc[:, 3, :], ALU.subtract)
        link(v.tensor_tensor(acc[:, 1, :], acc[:, 1, :], acc[:, 2, :], ALU.subtract))
        v.wait_ge(loaded_p, 16 * 18)
        link(v.tensor_scalar(acc[:, 2, :], acc[:, 1, :], 1.0 / VALID[0], None, ALU.mult))
        link(v.tensor_tensor(acc[:, 3, :], acc[:, 2, :], acc[:, 2, :], ALU.mult))
        link(v.scalar_tensor_tensor(out=acc[:, 3, :], in0=acc[:, 0, :], scalar=1.0 / VALID[0], in1=acc[:, 3, :], op0=ALU.mult, op1=ALU.subtract))
        v.tensor_scalar(stat0[:, :, 0], acc[:, 2, :], pars[:, 0, 0:1], None, ALU.add)
        link(v.tensor_scalar(acc[:, 2, :], acc[:, 2, :], pars[:, 0, 0:1], None, ALU.add))
        link(v.tensor_tensor(acc[:, 2, :], acc[:, 2, :], acc[:, 2, :], ALU.mult))
        v.tensor_tensor(stat0[:, :, 1], acc[:, 2, :], acc[:, 3, :], ALU.add).then_inc(gn_stat, 1)

        def coefs(n, cnt, layer, group, out_scale, out_bias, un):
            a, t, m = gs[:, 0:cnt], gs[:, 4:4 + cnt], gs[:, 8:8 + 2 * cnt]
            mean, square = m[:, 0:2 * cnt:2], m[:, 1:2 * cnt:2]
            v.wait_ge(gn_group, n)
            link(v.tensor_copy(m, group))
            link(v.tensor_tensor(t, mean, mean, ALU.mult))
            link(v.tensor_tensor(t, square, t, ALU.subtract))
            v.tensor_scalar(a, t, 0.0, EPS, ALU.max, ALU.add).then_inc(gn_var, 1)
            v.wait_ge(gn_pow, n)
            link(v.tensor_scalar(a, a, pars[:, layer, 1:2], None, ALU.mult))
            link(v.tensor_tensor(t, mean, a, ALU.mult))
            link(v.tensor_scalar(t, t, -1.0, pars[:, layer, 2:3], ALU.mult, ALU.add))
            v.tensor_tensor(out_scale, a, un, ALU.mult)
            v.scalar_tensor_tensor(out=out_bias, in0=a, scalar=pars[:, layer, 0:1], in1=t, op0=ALU.mult, op1=ALU.add).then_inc(gn_coef, 1)
            v.wait_ge(gn_coef, n)

        coefs(1, B, 0, p_m[:, 128:128 + 2 * B], coef0[:, :, 0], coef0[:, :, 1], unscale[:, 6:6 + B])

        def keep_chunks(k, b):
            v.wait_ge(t_mm, b * NCH // 2 + k + 1)
            v.tensor_copy(buf(x0T, TK, [[1, 2 * P]], off=(b % 2) * NCH * P + k * 2 * P), p_t[0:TK, 0:2 * P]).then_inc(t_kept, 1)

        with v.Fori(0, NCH // 2) as k:
            keep_chunks(k, 0)

        def low(u):
            v.wait_ge(hi_done, u.g + 1)
            v.wait_ge(gelu_done, u.g + 1)
            nc.vector.tensor_tensor(ring_rows(u, 1, 2, first_row(u)), split_ap(geluf, u),
                                    ring_rows(u, 0, 2, first_row(u)), ALU.subtract).then_inc(lo_done, 1)
            if u.head and u.layer != 5:
                v.wait_ge(lo_done, u.g + 1)
                if u.all_before:
                    v.wait_ge(conv_done, u.all_before)
                src = ring[u.stream]
                nc.vector.tensor_copy(wrap[u.stream][:, :, :], buf(src, C, [[PL, 2], [1, P]], off=u.par * 2 * PL + 2 * P))
                nc.vector.tensor_copy(buf(src, C, [[PL, 2], [1, 2 * P]], off=(1 - u.par) * 2 * PL),
                                      buf(src, C, [[PL, 2], [1, 2 * P]], off=u.par * 2 * PL + UR * P)).then_inc(halo_done, 1)

        for u in lead:
            low(u)

        def work(t, before, after):
            for u in before:
                low(u)
            for m in t.tails:
                v.wait_ge(conv_done, m.c + 1)
                v.wait_ge(lo_done, m.nxt_g)
                src = ring[m.stream]
                nc.vector.tensor_copy(buf(src, C, [[PL, 2], [1, 2 * P]], off=m.par * 2 * PL),
                                      buf(src, C, [[PL, 2], [1, 2 * P]], off=(1 - m.par) * 2 * PL + UR * P)).then_inc(halo_done, 1)
            v.wait_ge(evac_done, t.c + 1)
            skip = P if (t.head and t.layer != 5) else 0
            size = t.size - (1 if t.last_of_layer else 0)
            stats = nc.vector.bn_stats(bst[t.stream][:, bass.ds(t.j * 6, 6)], y[t.layer][:, bass.ds(t.j * OC + skip, size - skip)])
            if t.stream == "A" and not t.final and t.batch + 1 < B:
                keep_chunks(t.j, t.batch + 1)
            if t.gn is not None:
                n = t.layer
                link(stats)
                link(v.bn_aggr(mv[:, :], bst[t.stream][:, 0:6 * (t.n_stats)]))
                link(v.tensor_scalar(gs[:, 0:1], mv[:, 0:1], unscale[:, n:n + 1], pars[:, n, 0:1], ALU.mult, ALU.add))
                link(v.tensor_tensor(gs[:, 4:5], gs[:, 0:1], gs[:, 0:1], ALU.mult))
                v.scalar_tensor_tensor(out=gs[:, 1:2], in0=mv[:, 1:2], scalar=unscale2[:, n:n + 1], in1=gs[:, 4:5],
                                       op0=ALU.mult, op1=ALU.add).then_inc(gn_stat, 1)
                coefs(t.gn + 2, 1, n, p_m[:, 0:2], coef[:, n, 0:1], coef[:, n, 1:2], unscale[:, n:n + 1])
            for u in after:
                low(u)

        take(v, slots, loops, work)

    @block.tensor
    def _(pe):
        pe.wait_ge(made_ident, 3)
        pe.wait_ge(w_split, 1)
        for i in range(CH):
            last = pe.transpose(p_m16[0:TK, i * C:(i + 1) * C], w0pad16[:, i, :], ident16[:, :])
        last.then_inc(w_turned, 1)
        for n in range(1, 6):
            pe.wait_ge(w_split, n + 1)
            pe.wait_ge(w_kept, n)
            for s, t in enumerate((wh, wl)):
                for k in range(TAPS[n]):
                    at = (s * TAPS[n] + k) * C
                    last = pe.transpose(p_m16[:, at:at + C], t[:, k:TAPS[n] * C:TAPS[n]], ident16[:, :])
            last.then_inc(w_turned, 1)
        pe.wait_ge(w_kept, 6)
        for i in range(CH):
            last = pe.transpose(p_m[0:CW, i * C:(i + 1) * C], w0pad[:, i, :], ident[:, :])
        last.then_inc(w_turned, 1)
        pe.wait_ge(x_split, 2 * B)
        for b in range(B):
            for c in range(NCH):
                xc = xs[:, b, c * CS:c * CS + CW]
                last = pe.matmul(p_t[0:CW, b * CW:(b + 1) * CW], xc, xc, start=(c == 0), stop=(c == NCH - 1))
        last.then_inc(g_done, 1)
        pe.wait_ge(g_kept, 1)
        pe.wait_ge(w_kept, 7)
        for b in range(B):
            for i in range(CH):
                at = (b * CH + i) * CW
                last = pe.matmul(p_y[:, 0, at:at + CW], w0T[:, i, :], gram[:, b, :], start=True, stop=True)
        last.then_inc(u_done, 1)
        pe.matmul(p_m[:, 0:B * CW], ones[0:P, :], xsum[:, :, :].rearrange("p b s -> p (b s)"), start=True, stop=True).then_inc(u_done, 1)
        pe.wait_ge(gn_stat, 1)
        pe.wait_ge(made_quad, 2)
        pe.matmul(p_m[:, 128:128 + 2 * B], quad[:, :], stat0[:, :, :].rearrange("p b s -> p (b s)"), start=True, stop=True).then_inc(gn_group, 1)

        def turn_chunks(k, b):
            n = b * NCH // 2 + k
            pe.wait_ge(t_kept, n) if not is_zero(n) else None
            for c in range(2):
                last = pe.matmul(p_t[0:TK, c * P:(c + 1) * P],
                                 buf(x16, P, [[1, TK]], off=b * 4 * XW + k * (8 * CS) + c * 4 * CS),
                                 ident16[0:P, 0:P], start=True, stop=True)
            last.then_inc(t_mm, 1)

        turn_chunks(0, 0)
        with pe.Fori(1, NCH // 2) as k:
            turn_chunks(k, 0)

        def first(u):
            pe.wait_ge(t_kept, u.batch * NCH // 2 + u.j + 1)
            if not is_zero(u.l0_wait):
                pe.wait_ge(gelu_done, u.l0_wait)
            for i in range(CH):
                last = pe.matmul(p_l0[:, 2 * u.par + i // 2, (i % 2) * 2 * P:(i % 2 + 1) * 2 * P], w0T16[:, i, :],
                                 buf(x0T, TK, [[1, 2 * P]], off=(u.batch % 2) * NCH * P + u.j * 2 * P), start=True, stop=True)
            last.then_inc(l0_done, 1)

        for u in lead:
            first(u)

        def conv(t):
            n = t.layer
            if not t.final:
                pe.wait_ge(lo_done, t.g + 1)
            if not is_zero(t.need_halo):
                pe.wait_ge(halo_done, t.need_halo)
            if not is_low(t.c, 2):
                pe.wait_ge(evac_done, t.c - 1)
            out = p_y[:, t.bank, 0:t.size]
            if t.final:
                src, q = ring[t.stream], (t.j - 1) % 2
                ops = []
                for k in range(3):
                    for wp, xp in ((0, 0), (0, 1), (1, 0)):
                        if k < 2:
                            rhs, o = buf(src, C, [[1, P]], off=(q * 2 + xp) * PL + (UR + k) * P), p_y[:, t.bank, 0:P]
                        else:
                            rhs, o = wrap[t.stream][:, xp, 1:P], p_y[:, t.bank, 0:P - 1]
                        ops.append((o, wT[n][:, wp, k, :], rhs))
            else:
                half = t.rows // 2
                base = 2 if n == 5 else 0
                ops = [(out, wT[n][:, wp, k, :], ring_rows(t, xp, base + k, [[2 * P, half], [1, P]]))
                       for k in range(TAPS[n]) for wp, xp in ((0, 0), (0, 1), (1, 0))]
            for m, (o, lhs, rhs) in enumerate(ops):
                last = pe.matmul(o, lhs, rhs, start=(m == 0), stop=(m == len(ops) - 1))
            last.then_inc(conv_done, 1)

        def group(t):
            pe.wait_ge(gn_stat, t.gn + 2)
            pe.matmul(p_m[:, 0:2], quad[:, :], gs[:, 0:2], start=True, stop=True).then_inc(gn_group, 1)

        pending = []

        def work(t, before, after):
            for u in before:
                if u.stream == "A":
                    first(u)
            if pending and needs(t, pending[0]):
                group(pending.pop())
            conv(t)
            if t.stream == "A" and not t.final and t.batch + 1 < B:
                turn_chunks(t.j, t.batch + 1)
            if pending:
                group(pending.pop())
            if t.gn is not None:
                pending.append(t)
            for u in after:
                if u.stream == "A":
                    first(u)

        take(pe, slots, loops, work)
        if pending:
            group(pending.pop())

    ctx.close()
    with ExitStack() as ctx:
        transformer(nc, ctx, h5, t_in, out)
    outer.close()

class Tick:

    def __init__(self, sem, per, base=0):
        self.sem, self.per, self.base, self.at = sem, per, base, 0

    def wait(self, eng, b, n):
        eng.wait_ge(self.sem, b * self.per + (self.base + n))


def transformer(nc, ctx, h5, w, out):
    sb = lambda name, shape, dt=F32: ctx.enter_context(nc.sbuf_tensor(name, shape, dt))
    sem = lambda name: ctx.enter_context(nc.semaphore(name))
    bank = ctx.enter_context(nc.psum_tensor("bank", [C, 8, 512], F32))

    pwn = [sb("pwn0", [C, C]), sb("pwn1", [E1, C])]
    pwT = sb("pwT", [C, E])
    wqkv = [sb("wqkv0", [C, 3 * E]), sb("wqkv1", [E1, 3 * E])]
    wpr = [sb("wpr0", [C, E]), sb("wpr1", [E1, E])]
    fcn = sb("fcn", [C, HT, E])
    w0T = [sb("w0Ta", [C, HID]), sb("w0Tb", [E1, HID])]
    w1all = sb("w1all", [C, 2 * HID])
    w1n = [w1all[:, 0:HID], w1all[0:E1, HID:2 * HID]]
    w1T = sb("w1T", [C, HT, E])
    rows = sb("rows", [P, 3, E])
    bfc = sb("bfc", [C, HT])
    alpha = sb("alpha", [C, 6])
    hnum = sb("hnum", [C, HT])
    hnum_i = sb("hnum_i", [C, HT], I32)
    mix = sb("mix", [C, 3, HT])
    tmp = sb("tmp", [C, 3, HT])
    sums = sb("sums", [C, 4])
    pmn = sb("pmn", [M, HD])
    pmT = sb("pmT", [HD, M])
    spread = sb("spread", [HD, 8, HD])
    own = sb("own", [C, 8])
    feat = [sb("feat0", [C, 8, M]), sb("feat1", [E1, 4, M])]
    diag = [sb("diag0", [C, HEADS]), sb("diag1", [E1, HEADS])]
    kvmask = sb("kvmask", [2 * M, GR, 2 * VW])
    ident = sb("identt", [C, C])
    mhalf = sb("mhalft", [P, R])
    feps = sb("feps", [C, 1])
    hcur = sb("hcur", [C, R * P])
    res = sb("res", [P, B, R, E])
    xn = sb("xn", [P, R, E])
    xc = [sb("xc0", [C, R * P]), sb("xc1", [E1, R * P])]
    xt = [sb("xt0", [C, B, R * P]), sb("xt1", [E1, B, R * P])]
    ft = [sb("ft0", [C, R * P]), sb("ft1", [E1, R * P])]
    sq = [sb("sq0", [C, R * P]), sb("sq1", [E1, R * P])]
    dk = sb("dk", [P, B, R, FE])
    vals = sb("vals", [P, B * R * HEADS, VW])
    kmax = sb("kmax", [C, B, 2 * R])
    kmin = sb("kmin", [C, 2])
    dg = sb("dg", [P, 2, HEADS])
    mq = sb("mq", [P, 2, HEADS])
    st = sb("st", [P, R, 6])
    mv = sb("mvt", [P, R, 2])
    rs = sb("rs", [P, R])
    hid = sb("hid", [C, HT, R * P])
    hflat = hid[0:P, :, :].rearrange("p t n -> p (t n)")
    ek = hflat[:, 0:R * FE].rearrange("p (r f) -> p r f", f=FE)
    dq = hflat[:, R * FE:(R + 2) * FE].rearrange("p (r f) -> p r f", f=FE)
    q1T = w1all[0:2 * M, 0:2 * GR * P].rearrange("p (a g t) -> p a g t", a=2, g=GR)
    kvm = sb("kvm", [2 * M, GR, 2 * VW])
    zr = sb("zr", [P, 2, HEADS])
    at = sb("at", [P, 2, E])
    atT = [sb("atT0", [C, 2, P]), sb("atT1", [E1, 2, P])]
    osb = fcn[0:P, :, :]

    loads = [sem(f"load{n}") for n in range(12)]
    made = sem("made")
    tw, twk = sem("tw"), sem("twk")
    ch = sem("ch")
    ready = sem("ready")
    passed = sem("passed")
    iter_done, iter2 = sem("iter_done"), sem("iter2")
    gmax, gmax_all, gmax_neg = sem("gmax"), sem("gmax_all"), sem("gmax_neg")
    out_done = sem("out_done")
    T = lambda name, per: Tick(sem(name), per)
    hc, h_mm, var_t, pow_t, xn_t, xt_mm, xt_k = T("hc", 1), T("h_mm", 6), T("var_t", 1), T("pow_t", 1), T("xn_t", 6), T("xt_mm", 2), T("xt_k", 4)
    k_mm, k_k, v_mm, v_k, dk_mm, dk_k = T("k_mm", 4), T("k_k", 8), T("v_mm", 6), T("v_k", 6), T("dk_mm", 6), T("dk_k", 6)
    dg_t = T("dg_t", 6)
    q_mm, q_k, ek_t, k1_t, kv_mm, kv_k = T("q_mm", 4), T("q_k", 8), T("ek_t", 6), T("k1_t", 6), T("kv_mm", 1), T("kv_k", 1)
    dq_mm, dq_t, eq_t, qt_mm, qt_k = T("dq_mm", 6), T("dq_t", 6), T("eq_t", 6), T("qt_mm", 6), T("qt_k", 12)
    o_mm, at_t, at_mm, at_k, pr_mm, pr_k = T("o_mm", 6), T("at_t", 6), T("at_mm", 6), T("at_k", 12), T("pr_mm", 6), T("pr_k", 6)
    var2, pow2, x2_t, x2_mm, x2_k = T("var2", 1), T("pow2t", 1), T("x2_t", 6), T("x2_mm", 2), T("x2_k", 4)
    f_mm, f_k, y_mm, y_k, stored = T("f_mm", 12), T("f_k", 12), T("y_mm", 6), T("y_k", 6), T("stored", 32)

    block = ctx.enter_context(nc.Block())

    def tile_(t, r):
        return t[:, r * P:(r + 1) * P]

    ops = {"pw": (0, 2), "rows": (1, 3), "qkv": (2, 2), "pr": (3, 2), "fc": (4, 1), "w1": (5, 2), "bfc": (6, 1), "alpha": (7, 2), "pm": (8, 1)}

    def loaded(eng, what):
        n, times = ops[what]
        eng.wait_ge(loads[n], 16 * times)

    @block.sync
    def _(sp):
        def load(what, dst, src, slow=False):
            sp.dma_start(dst, src, allow_slow_non_contiguous=slow).then_inc(loads[ops[what][0]], 16)

        load("pw", pwn[0][:, :], w["tok_pw"][0:C, :])
        load("pw", pwn[1][:, :], w["tok_pw"][C:E, :])
        load("pm", pmn[:, :], w["attn_proj_mat"])
        for n, name in enumerate(("tok_pb", "attn_b_proj", "ffn_b_proj")):
            load("rows", rows[:, n, :], bass.AP(w[name].tensor, 0, [[0, P], [1, E]]))
        for n in range(2):
            load("qkv", wqkv[n][:, :], w["attn_W_qkv"][n * C:n * C + (C, E1)[n], :])
            load("pr", wpr[n][:, :], w["attn_W_proj"][n * C:n * C + (C, E1)[n], :])
            load("w1", w1n[n][:, :], w["ffn_w_proj"][n * C:n * C + (C, E1)[n], :])
        load("fc", fcn[:, :, :], w["ffn_w_fc"].rearrange("(t p) e -> p t e", p=C))
        load("bfc", bfc[:, :], w["ffn_b_fc"].rearrange("(t p) -> p t", p=C), slow=True)
        for n, name in enumerate(("ffn_alpha_e", "ffn_alpha_r")):
            load("alpha", alpha[:, 3 * n:3 * n + 3], bass.AP(w[name].tensor, 0, [[0, C], [1, 3]]))
        sp.sem_inc(stored.sem, 32)
        with sp.Fori(0, B) as b:
            y_k.wait(sp, b, R)
            row = b * (E * (R * P - 1))
            sp.dma_start(bass.AP(out.tensor, row, [[R * E, P - 1], [1, R * E]]), osb[0:P - 1, :, :].rearrange("p r e -> p (r e)")).then_inc(stored.sem, 16)
            sp.dma_start(bass.AP(out.tensor, row + (P - 1) * R * E, [[R * E, 1], [1, (R - 1) * E]]),
                         osb[P - 1:P, 0:R - 1, :].rearrange("p r e -> p (r e)")).then_inc(stored.sem, 16)
        sp.wait_ge(stored.sem, 32 * B + 32)

    @block.gpsimd
    def _(pool):
        def step(ins, n):
            ins.then_inc(made, 1)
            pool.wait_ge(made, n)

        pool.memset(ident[:, :], 0.0).then_inc(made, 1)
        pool.memset(spread[:, :, :], 0.0).then_inc(made, 1)
        pool.memset(own[:, :], 1.0).then_inc(made, 1)
        step(pool.memset(kvmask[:, :, :], 1.0), 4)
        pool.iota(hnum_i[:, :], pattern=[[C, HT]], base=0, channel_multiplier=1).then_inc(made, 1)
        pool.affine_select(out=ident[:, :], in_=ident[:, :], compare_op=ALU.not_equal, fill=1.0, base=0,
                           pattern=[[-1, C]], channel_multiplier=1).then_inc(made, 1)
        pool.affine_select(out=spread[:, :, :], in_=spread[:, :, :], compare_op=ALU.not_equal, fill=1.0, base=0,
                           pattern=[[0, 8], [-1, HD]], channel_multiplier=1).then_inc(made, 1)
        pool.affine_select(out=own[:, :], in_=own[:, :], compare_op=ALU.is_ge, fill=0.0, base=0,
                           pattern=[[-HD, 8]], channel_multiplier=1).then_inc(made, 1)
        m = kvmask[:, :, :].rearrange("p g (a v) -> p g a v", a=2)
        step(pool.affine_select(out=m, in_=m, compare_op=ALU.is_ge, fill=0.0, base=0,
                                pattern=[[0, GR], [-M, 2], [0, VW]], channel_multiplier=1), 9)
        pool.affine_select(out=own[:, :], in_=own[:, :], compare_op=ALU.is_ge, fill=0.0, base=HD - 1,
                           pattern=[[HD, 8]], channel_multiplier=-1).then_inc(made, 1)
        pool.affine_select(out=m, in_=m, compare_op=ALU.is_ge, fill=0.0, base=M - 1,
                           pattern=[[0, GR], [M, 2], [0, VW]], channel_multiplier=-1).then_inc(made, 1)
        pool.memset(mhalf[:, :], -0.5).then_inc(made, 1)
        pool.memset(vals[:, :, :], 1.0).then_inc(made, 1)
        pool.memset(kmax[:, :, :], -3e38).then_inc(made, 1)
        pool.memset(feps[:, :], FEPS * RATIO).then_inc(made, 1)
        with pool.Fori(0, B) as b:
            var_t.wait(pool, b, 1)
            pool.tensor_tensor(rs[:, :], rs[:, :], mhalf[:, :], ALU.pow).then_inc(pow_t.sem, 1)
        pool.wait_ge(gmax, 1)
        pool.partition_all_reduce(kmin[:, 1:2], kmin[:, 0:1], C, bass.bass_isa.ReduceOp.max).then_inc(gmax_all, 1)
        with pool.Fori(0, B) as b:
            var2.wait(pool, b, 1)
            pool.tensor_tensor(rs[:, :], rs[:, :], mhalf[:, :], ALU.pow).then_inc(pow2.sem, 1)

    @block.scalar
    def _(act):
        S = nc.scalar

        def turned(b, mm, kept, banks):
            for half in range(2):
                mm.wait(act, b, half + 1)
                for n, rowsn in enumerate((C, E1)):
                    S.copy(xc[n][:, half * HALF:(half + 1) * HALF], bank[0:rowsn, banks[half][n], 0:HALF]).then_inc(kept.sem, 1)

        def project(b, mm, kept):
            for half in range(2):
                for n, rowsn in enumerate((C, E1)):
                    mm.wait(act, b, 2 * half + n + 1)
                    src = bank[0:rowsn, 2 + 2 * n + half, 0:HALF]
                    S.copy(ft[n][:, half * HALF:(half + 1) * HALF], src).then_inc(kept.sem, 1)
                    S.activation(sq[n][:, half * HALF:(half + 1) * HALF], src, ACT.Square).then_inc(kept.sem, 1)

        with act.Fori(0, B) as b:
            act.wait_ge(iter_done, b * 3 + 1)
            turned(b, xt_mm, xt_k, ((6, 0), (7, 1)))
            project(b, k_mm, k_k)
        act.wait_ge(gmax_neg, 1)
        with act.Fori(0, B) as b:
            act.wait_ge(iter2, b * 2 + 1)
            project(b, q_mm, q_k)
            for r in range(R):
                S.activation(ek[:, r, :], dk[:, b, r, :], ACT.Exp, bias=kmin[0:P, 0:1]).then_inc(ek_t.sem, 1)
            for s in range(R + 3):
                if s < R:
                    r = s
                    dq_t.wait(act, b, r + 1)
                    S.activation(dq[:, r % 2, :], dq[:, r % 2, :], ACT.Exp).then_inc(eq_t.sem, 1)
                if 0 <= s - 1 < R:
                    r = s - 1
                    qt_mm.wait(act, b, r + 1)
                    if r >= 2:
                        o_mm.wait(act, b, r - 1)
                    S.activation(q1T[:, r % 2, 0:4, :], bank[0:2 * M, 4, 0:4 * P].rearrange("p (g t) -> p g t", g=4), ACT.Identity,
                                 bias=feps[0:2 * M, :], scale=RATIO).then_inc(qt_k.sem, 1)
                    S.activation(q1T[:, r % 2, 4:6, :], bank[0:2 * M, 5, 0:2 * P].rearrange("p (g t) -> p g t", g=2), ACT.Identity,
                                 bias=feps[0:2 * M, :], scale=RATIO).then_inc(qt_k.sem, 1)
                if 0 <= s - 3 < R:
                    r = s - 3
                    at_mm.wait(act, b, r + 1)
                    if r >= 2:
                        pr_mm.wait(act, b, r - 1)
                    S.copy(atT[0][:, r % 2, :], bank[0:C, 6, 0:P]).then_inc(at_k.sem, 1)
                    S.copy(atT[1][:, r % 2, :], bank[0:E1, 6, 128:128 + P]).then_inc(at_k.sem, 1)
            turned(b, x2_mm, x2_k, ((0, 1), (2, 3)))
            for n in range(2 * HT):
                t, half = n // 2, n % 2
                f_mm.wait(act, b, n + 1)
                S.activation(hid[:, t, half * HALF:(half + 1) * HALF], bank[:, 4 + n % 4, 0:HALF], GELU,
                             bias=bfc[:, t:t + 1]).then_inc(f_k.sem, 1)

    LINKS1, LINKS2 = 3, 22

    @block.vector
    def _(v):
        chain = [0]
        body = [None, 0, 0]

        def link(ins):
            ins.then_inc(ch, 1)
            if body[0] is None:
                chain[0] += 1
                v.wait_ge(ch, chain[0])
            else:
                body[1] += 1
                v.wait_ge(ch, body[0] * body[2] + (chain[0] + body[1]))

        v.wait_ge(made, 15)
        v.wait_ge(tw, 1)
        v.tensor_copy(pmT[:, :], bank[0:HD, 0, 0:M]).then_inc(twk, 1)
        v.tensor_copy(pwT[:, :], bank[:, 1, 0:E]).then_inc(twk, 1)
        v.wait_ge(tw, 2)
        for n, (rn, hn) in enumerate(((C, 8), (E1, 4))):
            v.scalar_tensor_tensor(out=feat[n][:, :, :], in0=bass.AP(bank, 2 * 512, [[8 * 512, rn], [0, hn], [1, M]]), scalar=NORM,
                                   in1=bass.AP(own, 0, [[8, rn], [1, hn], [0, M]]), op0=ALU.mult, op1=ALU.mult)
        v.memset(diag[0][:, 8:12], 0.0)
        v.memset(diag[1][:, 0:8], 0.0)
        v.tensor_scalar(diag[0][:, 0:8], own[:, :], 0.5 * NORM * NORM, None, ALU.mult)
        v.tensor_scalar(diag[1][:, 8:12], own[0:E1, 0:4], 0.5 * NORM * NORM, None, ALU.mult)
        loaded(v, "alpha")
        link(v.tensor_copy(hnum[:, :], hnum_i[:, :]))
        for i in range(3):
            for j in range(3):
                link(v.tensor_scalar(tmp[:, j, :], hnum[:, :], float(RATIOS[j] * EMBEDS[i]), alpha[:, 3 + j:4 + j], ALU.is_lt, ALU.mult))
            link(v.tensor_tensor(tmp[:, 0, :], tmp[:, 0, :], tmp[:, 1, :], ALU.add))
            link(v.tensor_tensor(tmp[:, 0, :], tmp[:, 0, :], tmp[:, 2, :], ALU.add))
            link(v.tensor_scalar(mix[:, i, :], tmp[:, 0, :], alpha[:, i:i + 1], None, ALU.mult))
        link(v.tensor_tensor(mix[:, 1, :], mix[:, 1, :], mix[:, 2, :], ALU.add))
        link(v.tensor_tensor(mix[:, 0, :], mix[:, 0, :], mix[:, 1, :], ALU.add))
        link(v.tensor_tensor(sums[:, 3:4], alpha[:, 3:4], alpha[:, 4:5], ALU.add))
        link(v.tensor_tensor(sums[:, 3:4], sums[:, 3:4], alpha[:, 5:6], ALU.add))
        link(v.tensor_tensor(sums[:, 1:2], alpha[:, 1:2], alpha[:, 2:3], ALU.add))
        link(v.tensor_tensor(sums[:, 0:1], alpha[:, 0:1], sums[:, 1:2], ALU.add))
        v.tensor_scalar(sums[:, 0:2], sums[:, 0:2], sums[:, 3:4], None, ALU.mult)
        link(v.tensor_scalar(sums[:, 2:3], alpha[:, 2:3], sums[:, 3:4], None, ALU.mult))
        loaded(v, "rows")
        loaded(v, "bfc")
        loaded(v, "fc")
        for s, (e0, e1) in enumerate(SEG):
            v.tensor_scalar(rows[:, 2, e0:e1], rows[:, 2, e0:e1], sums[0:P, s:s + 1], None, ALU.mult)
            last = v.tensor_tensor(fcn[:, :, e0:e1], fcn[:, :, e0:e1], bass.AP(mix, s * HT, [[3 * HT, C], [1, HT], [0, e1 - e0]]), ALU.mult)
        last.then_inc(twk, 1)
        v.tensor_tensor(bfc[:, :], bfc[:, :], mix[:, 0, :], ALU.mult)
        v.wait_ge(tw, 3)
        v.tensor_copy(w0T[0][:, 0:512], bank[:, 3, :])
        v.tensor_copy(w0T[0][:, 512:768], bank[:, 4, 0:256])
        v.tensor_copy(w0T[1][:, 0:512], bank[0:E1, 5, :])
        v.tensor_copy(w0T[1][:, 512:768], bank[0:E1, 6, 0:256]).then_inc(twk, 1)
        v.wait_ge(tw, 4)
        for p in range(3):
            for s, (e0, e1) in enumerate(SEG):
                last = v.tensor_tensor(w1T[:, 2 * p:2 * p + 2, e0:e1], bass.AP(bank, (3 + p) * 512 + e0, [[8 * 512, C], [E, 2], [1, e1 - e0]]),
                                       bass.AP(mix, s * HT + 2 * p, [[3 * HT, C], [1, 2], [0, e1 - e0]]), ALU.mult)
        last.then_inc(twk, 1)
        v.wait_ge(twk, 5)
        v.sem_inc(ready, 1)
        v.sem_inc(iter_done, 1)

        def normed(b, src, var, powed, done):
            v.sem_inc(passed, 1)
            for r in range(R):
                last = v.bn_stats(st[:, r, :], src(r))
            link(last)
            v.sem_inc(passed, 1)
            for r in range(R):
                last = v.bn_aggr(mv[:, r, :], st[:, r, :])
            link(last)
            v.tensor_scalar(rs[:, :], mv[:, :, 1], EPS, None, ALU.add).then_inc(var.sem, 1)
            powed.wait(v, b, 1)
            for r in range(R):
                v.tensor_scalar(xn[:, r, :], src(r), mv[:, r, 0:1], rs[:, r:r + 1], ALU.subtract, ALU.mult).then_inc(done.sem, 1)

        def wide(k, n0, n):
            return bass.AP(k[0], k[1] + n0, [[2 * HEADS, P], [1, n], [0, M]])

        body[2] = LINKS1
        with v.Fori(0, B) as b:
            body[0], body[1] = b, 0
            v.tensor_copy(hcur[:, :], h5[:, b, :]).then_inc(hc.sem, 1)
            for r in range(R):
                h_mm.wait(v, b, r + 1)
                last = v.tensor_tensor(res[:, b, r, :], bank[0:P, r, 0:E], rows[:, 0, :], ALU.add)
            link(last)
            normed(b, lambda r: res[:, b, r, :], var_t, pow_t, xn_t)
            vb = (6, 7, 0, 1, 2, 3)
            for r in range(R):
                v_mm.wait(v, b, r + 1)
                v.tensor_copy(bass.AP(vals, b * (R * HEADS * VW) + r * HEADS * VW, [[B * R * HEADS * VW, P], [VW, HEADS], [1, HD]]),
                              bank[0:P, vb[r], 0:E].rearrange("p (h d) -> p h d", d=HD)).then_inc(v_k.sem, 1)
            pairs = ((4, 5), (6, 7), (0, 1))
            xt_k.wait(v, b, 4)
            v.tensor_copy(xt[0][:, b, :], xc[0][:, :])
            v.tensor_copy(xt[1][:, b, :], xc[1][:, :])
            for r in range(R):
                a, c = pairs[r % 3]
                dk_mm.wait(v, b, r + 1)
                pn = P - 1 if r == R - 1 else P
                v.tensor_reduce(kmax[0:pn, b, 2 * r:2 * r + 1], bank[0:pn, a, 0:FA], AX_X, ALU.max)
                v.tensor_reduce(kmax[0:pn, b, 2 * r + 1:2 * r + 2], bank[0:pn, c, 0:FE - FA], AX_X, ALU.max)
                if r >= 2:
                    dk_k.wait(v, b, r - 1)
                v.tensor_copy(dg[:, r % 2, :], bank[0:P, a, FA:FA + HEADS]).then_inc(dg_t.sem, 1)
                dg_t.wait(v, b, r + 1)
                k = (dg, r % 2 * HEADS)
                v.tensor_tensor(dk[:, b, r, 0:FA].rearrange("p (h m) -> p h m", m=M), bank[0:P, a, 0:FA].rearrange("p (h m) -> p h m", m=M), wide(k, 0, 8), ALU.subtract)
                last = v.tensor_tensor(dk[:, b, r, FA:FE].rearrange("p (h m) -> p h m", m=M), bank[0:P, c, 0:FE - FA].rearrange("p (h m) -> p h m", m=M), wide(k, 8, 4), ALU.subtract)
                last.then_inc(dk_k.sem, 1)
            dk_k.wait(v, b, R)
            k_k.wait(v, b, 8)
            v.sem_inc(iter_done, 3)
        assert body[1] == LINKS1, body[1]
        chain[0] += LINKS1 * B
        body[0] = None
        v.tensor_reduce(kmin[:, 0:1], kmax[:, :, :].rearrange("p b r -> p (b r)"), AX_X, ALU.max).then_inc(gmax, 1)
        v.wait_ge(gmax_all, 1)
        v.tensor_scalar(kmin[:, 0:1], kmin[:, 1:2], -1.0, None, ALU.mult).then_inc(gmax_neg, 1)
        v.wait_ge(gmax_neg, 1)
        v.sem_inc(iter2, 1)

        body[2] = LINKS2
        with v.Fori(0, B) as b:
            body[0], body[1] = b, 0
            for r in range(R):
                ek_t.wait(v, b, r + 1)
                v.tensor_scalar(ek[:, r, :], ek[:, r, :], FEPS, RATIO, ALU.add, ALU.mult).then_inc(k1_t.sem, 1)
            kv_mm.wait(v, b, 1)
            v.tensor_tensor(kvm[:, :, :], bank[0:2 * M, 6, 0:GR * 2 * VW].rearrange("p (g c) -> p g c", g=GR), kvmask[:, :, :], ALU.mult).then_inc(kv_k.sem, 1)
            for s in range(R + 4):
                if s < R:
                    r = s
                    a, c = ((0, 1), (2, 3))[r % 2]
                    dq_mm.wait(v, b, r + 1)
                    if r >= 2:
                        qt_mm.wait(v, b, r - 1)
                    v.tensor_reduce(mq[:, r % 2, 0:8], bank[0:P, a, 0:FA].rearrange("p (h m) -> p h m", m=M), AX_X, ALU.max)
                    link(v.tensor_reduce(mq[:, r % 2, 8:12], bank[0:P, c, 0:FE - FA].rearrange("p (h m) -> p h m", m=M), AX_X, ALU.max))
                    link(v.tensor_tensor(mq[:, r % 2, :], bank[0:P, a, FA:FA + HEADS], mq[:, r % 2, :], ALU.add))
                    k = (mq, r % 2 * HEADS)
                    v.tensor_tensor(dq[:, r % 2, 0:FA].rearrange("p (h m) -> p h m", m=M), bank[0:P, a, 0:FA].rearrange("p (h m) -> p h m", m=M), wide(k, 0, 8), ALU.subtract)
                    v.tensor_tensor(dq[:, r % 2, FA:FE].rearrange("p (h m) -> p h m", m=M), bank[0:P, c, 0:FE - FA].rearrange("p (h m) -> p h m", m=M), wide(k, 8, 4), ALU.subtract).then_inc(dq_t.sem, 1)
                if 0 <= s - 2 < R:
                    r = s - 2
                    o_mm.wait(v, b, r + 1)
                    if r >= 2:
                        at_mm.wait(v, b, r - 1)
                    o = bank[0:P, 7, 0:HEADS * VW].rearrange("p (h c) -> p h c", c=VW)
                    link(v.reciprocal(zr[:, r % 2, :], o[:, :, HD]))
                    v.tensor_tensor(at[:, r % 2, :].rearrange("p (h d) -> p h d", d=HD), o[:, :, 0:HD],
                                    bass.AP(zr, r % 2 * HEADS, [[2 * HEADS, P], [1, HEADS], [0, HD]]), ALU.mult).then_inc(at_t.sem, 1)
                if 0 <= s - 4 < R:
                    r = s - 4
                    pr_mm.wait(v, b, r + 1)
                    v.tensor_tensor(xn[:, r, :], bank[0:P, 7, 256:256 + E], rows[:, 1, :], ALU.add).then_inc(pr_k.sem, 1)
                    pr_k.wait(v, b, r + 1)
                    last = v.tensor_tensor(res[:, b, r, :], res[:, b, r, :], xn[:, r, :], ALU.add)
            link(last)
            normed(b, lambda r: res[:, b, r, :], var2, pow2, x2_t)
            for r in range(R):
                y_mm.wait(v, b, r + 1)
                last = v.tensor_tensor(xn[:, r, :], bank[0:P, r, 0:E], rows[:, 2, :], ALU.add)
            link(last)
            v.wait_ge(stored.sem, b * 32 + 32)
            for r in range(R):
                v.tensor_tensor(osb[:, r, :], xn[:, r, :], res[:, b, r, :], ALU.add).then_inc(y_k.sem, 1)
            y_k.wait(v, b, R)
            f_k.wait(v, b, 12)
            v.sem_inc(iter2, 2)
        assert body[1] == LINKS2, body[1]

    @block.tensor
    def _(pe):
        pe.wait_ge(made, 15)
        loaded(pe, "pm")
        loaded(pe, "pw")
        pe.transpose(bank[0:HD, 0, 0:M], pmn[:, :], ident[0:M, 0:M])
        pe.transpose(bank[:, 1, 0:C], pwn[0][:, :], ident[:, :])
        pe.transpose(bank[:, 1, C:E], pwn[1][:, :], ident[0:E1, 0:E1]).then_inc(tw, 1)
        pe.wait_ge(twk, 2)
        pe.matmul(bank[:, 2, 0:M], spread[:, :, :].rearrange("p h d -> p (h d)"), pmT[:, :], start=True, stop=True).then_inc(tw, 1)
        pe.wait_ge(twk, 3)
        for t in range(HT):
            pe.transpose(bank[:, 3 + t // 4, t % 4 * C:t % 4 * C + C], fcn[:, t, 0:C], ident[:, :])
            last = pe.transpose(bank[0:E1, 5 + t // 4, t % 4 * C:t % 4 * C + C], fcn[:, t, C:E], ident[:, :])
        last.then_inc(tw, 1)
        loaded(pe, "w1")
        pe.wait_ge(twk, 4)
        for t in range(HT):
            a = t % 2 * E
            pe.transpose(bank[:, 3 + t // 2, a:a + C], w1n[0][:, t * C:t * C + C], ident[:, :])
            last = pe.transpose(bank[:, 3 + t // 2, a + C:a + E], w1n[1][:, t * C:t * C + C], ident[0:E1, 0:E1])
        last.then_inc(tw, 1)
        pe.wait_ge(ready, 1)
        loaded(pe, "qkv")
        loaded(pe, "pr")

        def mm(out, pairs, inc=None):
            for n, (lhs, rhs) in enumerate(pairs):
                last = pe.matmul(out, lhs, rhs, start=(n == 0), stop=(n == len(pairs) - 1))
            if inc:
                last.then_inc(inc.sem, 1)

        def turn(b, need, done, banks):
            for r in range(R):
                need.wait(pe, b, r + 1)
                half, k = r // 3, r % 3
                pe.transpose(bank[0:C, banks[half][0], k * P:(k + 1) * P], xn[:, r, 0:C], ident[0:P, 0:P])
                last = pe.transpose(bank[0:E1, banks[half][1], k * P:(k + 1) * P], xn[:, r, C:E], ident[0:P, 0:P])
                if k == 2:
                    last.then_inc(done.sem, 1)

        def project(src, col, done):
            for half in range(2):
                for n, rn in enumerate((C, E1)):
                    c0 = col + n * C
                    mm(bank[:, 2 + 2 * n + half, 0:HALF],
                       [(wqkv[k][:, c0:c0 + C], src(k, half)) for k in range(2)], done)

        def features(r, a, c, done):
            mm(bank[0:P, a, 0:FA], [(tile_(ft[0], r), feat[0][:, :, :].rearrange("p h m -> p (h m)"))])
            mm(bank[0:P, a, FA:FA + HEADS], [(tile_(sq[n], r), diag[n][:, :]) for n in range(2)])
            mm(bank[0:P, c, 0:FE - FA], [(tile_(ft[1], r), feat[1][:, :, :].rearrange("p h m -> p (h m)"))], done)

        with pe.Fori(0, B) as b:
            hc.wait(pe, b, 1)
            for r in range(R):
                mm(bank[0:P, r, 0:E], [(tile_(hcur, r), pwT[:, :])], h_mm)
            turn(b, xn_t, xt_mm, ((6, 0), (7, 1)))
            xt_k.wait(pe, b, 4)
            project(lambda k, half: xc[k][:, half * HALF:(half + 1) * HALF], E, k_mm)
            for r, a in enumerate((6, 7, 0, 1, 2, 3)):
                if r == 4:
                    k_k.wait(pe, b, 8)
                mm(bank[0:P, a, 0:E], [(tile_(xc[k], r), wqkv[k][:, 2 * E:3 * E]) for k in range(2)], v_mm)
            k_k.wait(pe, b, 8)
            v_k.wait(pe, b, 4)
            for r in range(R):
                if r >= 3:
                    dk_k.wait(pe, b, r - 2)
                features(r, *((4, 5), (6, 7), (0, 1))[r % 3], dk_mm)

        with pe.Fori(0, B) as b:
            pe.wait_ge(iter2, b * 2 + 1)
            project(lambda k, half: xt[k][:, b, half * HALF:(half + 1) * HALF], 0, q_mm)
            q_k.wait(pe, b, 8)
            k1_t.wait(pe, b, R)
            for g in range(GR):
                for r in range(R):
                    pn = P - 1 if r == R - 1 else P
                    last = pe.matmul(bank[0:2 * M, 6, g * 2 * VW:(g + 1) * 2 * VW], ek[0:pn, r, g * 2 * M:(g + 1) * 2 * M],
                                     bass.AP(vals, b * (R * HEADS * VW) + (r * HEADS + 2 * g) * VW, [[B * R * HEADS * VW, pn], [1, 2 * VW]]),
                                     start=(r == 0), stop=(r == R - 1))
            last.then_inc(kv_mm.sem, 1)
            for s in range(R + 4):
                if s < R:
                    if s >= 2:
                        dq_t.wait(pe, b, s - 1)
                    features(s, *((0, 1), (2, 3))[s % 2], dq_mm)
                if 0 <= s - 1 < R:
                    r = s - 1
                    eq_t.wait(pe, b, r + 1)
                    if r >= 1:
                        qt_k.wait(pe, b, 2 * r)
                    for g in range(GR):
                        last = pe.transpose(bank[0:2 * M, 4 + g // 4, g % 4 * P:g % 4 * P + P], dq[:, r % 2, g * 2 * M:(g + 1) * 2 * M], ident[0:P, 0:P])
                    last.then_inc(qt_mm.sem, 1)
                if 0 <= s - 2 < R:
                    r = s - 2
                    qt_k.wait(pe, b, 2 * r + 2)
                    kv_k.wait(pe, b, 1)
                    if r >= 3:
                        pr_k.wait(pe, b, r - 2)
                    if r >= 1:
                        at_t.wait(pe, b, r)
                    for g in range(GR):
                        last = pe.matmul(bank[0:P, 7, g * 2 * VW:(g + 1) * 2 * VW], q1T[:, r % 2, g, :], kvm[:, g, :], start=True, stop=True)
                    last.then_inc(o_mm.sem, 1)
                if 0 <= s - 3 < R:
                    r = s - 3
                    at_t.wait(pe, b, r + 1)
                    if r >= 1:
                        at_k.wait(pe, b, 2 * r)
                    pe.transpose(bank[0:C, 6, 0:P], at[:, r % 2, 0:C], ident[0:P, 0:P])
                    pe.transpose(bank[0:E1, 6, 128:128 + P], at[:, r % 2, C:E], ident[0:P, 0:P]).then_inc(at_mm.sem, 1)
                if 0 <= s - 4 < R:
                    r = s - 4
                    at_k.wait(pe, b, 2 * r + 2)
                    at_t.wait(pe, b, min(R, r + 3))
                    if r >= 1:
                        pr_k.wait(pe, b, r)
                    mm(bank[0:P, 7, 256:256 + E], [(atT[k][:, r % 2, :], wpr[k][:, :]) for k in range(2)], pr_mm)
            turn(b, x2_t, x2_mm, ((0, 1), (2, 3)))
            x2_k.wait(pe, b, 4)
            for n in range(2 * HT):
                t, half = n // 2, n % 2
                if n >= 4:
                    f_k.wait(pe, b, n - 3)
                mm(bank[:, 4 + n % 4, 0:HALF], [(w0T[k][:, t * C:(t + 1) * C], xc[k][:, half * HALF:(half + 1) * HALF]) for k in range(2)], f_mm)
            f_k.wait(pe, b, 12)
            for r in range(R):
                mm(bank[0:P, r, 0:E], [(hid[:, t, r * P:(r + 1) * P], w1T[:, t, :]) for t in range(HT)], y_mm)


_CONV = [f"L0_tok_{k}{n}" for n in range(6) for k in ("cw", "cb", "gw", "gb")]
_REST = ["tok_pw", "tok_pb", "attn_W_qkv", "attn_W_proj", "attn_b_proj", "attn_proj_mat", "ffn_w_fc", "ffn_b_fc",
         "ffn_w_proj", "ffn_b_proj", "ffn_alpha_e", "ffn_alpha_r"]


def kernel(**inputs):
    import numpy as _np
    import concourse.bacc as _bacc
    from concourse import mybir as _mybir
    from concourse.bass_utils import run_bass_kernel_spmd as _run

    nc = _bacc.Bacc("TRN2", target_bir_lowering=False, num_devices=1)
    arrays, args = {}, {}
    for name in ["x"] + _CONV + ["L0_" + n for n in _REST]:
        a = _np.ascontiguousarray(inputs[name])
        if name.startswith("L0_tok_cw"):
            a = a.reshape(a.shape[0], -1)
        arrays[f"in_{name}"] = a
        args[name] = nc.dram_tensor(f"in_{name}", a.shape, _mybir.dt.from_np(a.dtype), kind="ExternalInput").ap()
    out = nc.dram_tensor("out", (B, R * P - 1, E), _mybir.dt.float32, kind="ExternalOutput").ap()
    audio_tower(nc, args["x"], [args[f"L0_tok_cw{n}"] for n in range(6)],
                [[args[f"L0_tok_{k}{n}"] for k in ("cb", "gw", "gb")] for n in range(6)],
                {n: args["L0_" + n] for n in _REST}, out)
    r = _run(nc, [arrays], core_ids=[0])
    return r.results[0]["out"]
```

```python
import math
from contextlib import ExitStack

import numpy as np
import concourse.bass as bass
from concourse import mybir

ALU = mybir.AluOpType
ACT = mybir.ActivationFunctionType
AX_X = mybir.AxisListType.X
F32 = mybir.dt.float32
F16 = mybir.dt.float16
I32 = mybir.dt.int32
GELU = ACT.Gelu_apprx_tanh

B = 4
L = 120000
C = 128
P = 125
SP = L // P
K0, S0 = 10, 5
ROWS = [SP // S0 >> n for n in range(6)]
VALID = [P * r - 1 for r in ROWS]
XW = SP + S0
CH = 4
CS = CH * S0
CW = CS + S0
NCH = SP // CS
TK = 4 * CW
UR = 8
UC = UR * P
OC = UC // 2
TAPS = [K0, 3, 3, 3, 3, 2]
EPS = 1e-5
BUFR = UR + 2
PL = BUFR * P


R = ROWS[5]
E = 192
E1 = E - C
HEADS, HD, M = 12, 16, 44
FE = HEADS * M
FA = 8 * M
GR = HEADS // 2
VW = HD + 1
HID = 768
HT = HID // C
HALF = R * P // 2
NORM = 1.0 / math.sqrt(math.sqrt(HD))
RATIO = 1.0 / math.sqrt(M)
FEPS = 1e-4
EMBEDS, RATIOS = (96, 144, 192), (2, 3, 4)
SEG = ((0, 96), (96, 144), (144, 192))


class Slot:

    def __init__(self, stream, layer, batch, j, rows=UR, final=False):
        self.stream, self.layer, self.batch, self.j, self.rows, self.final = stream, layer, batch, j, rows, final
        self.par = j % 2


def plan():
    slots, loops = [], []

    def a(b, j):
        return Slot("A", 1, b, j)

    def layer_b(n, b):
        return [Slot("B", n, b, j) for j in range(ROWS[n - 1] // UR)] + [Slot("B", n, b, ROWS[n - 1] // UR, final=True)]

    def a_end(b):
        return Slot("A", 1, b, ROWS[0] // UR, final=True)

    def loop(body, times):
        first = len(slots)
        for i in range(times):
            slots.extend(body(i))
        size = (len(slots) - first) // times
        if times > 3:
            loops.append((first + size, size, times - 2))

    na = ROWS[0] // UR
    loop(lambda i: [a(0, 2 * i), a(0, 2 * i + 1)], na // 2)
    slots.append(a_end(0))
    for b in range(1, B):
        l2, l3, l4 = (layer_b(n, b - 1) for n in (2, 3, 4))
        loop(lambda i: [l2[2 * i], a(b, 2 * i), l2[2 * i + 1], a(b, 2 * i + 1)], 5)
        slots.extend([l2[10], l2[11], a(b, 10), l2[12], a(b, 11), a(b, 12), a(b, 13)])
        slots.extend([l3[0], l3[1], l3[2], a(b, 14), l3[3], l3[4], a(b, 15), l3[5], l3[6], a(b, 16), a(b, 17), a(b, 18)])
        slots.extend([l4[0], a(b, 19), l4[1], a(b, 20), l4[2], l4[3], a(b, 21), a(b, 22), a(b, 23), a_end(b)])
        slots.extend([Slot("B", 5, b - 1, 0), Slot("B", 5, b - 1, 1, rows=4)])
    l2, l3, l4 = (layer_b(n, B - 1) for n in (2, 3, 4))
    loop(lambda i: l2[2 * i:2 * i + 2], 6)
    slots.append(l2[12])
    loop(lambda i: l3[2 * i:2 * i + 2], 3)
    slots.append(l3[6])
    slots.extend(l4)
    slots.extend([Slot("B", 5, B - 1, 0), Slot("B", 5, B - 1, 1, rows=4)])
    return slots, loops


def number(slots):
    for s, u in enumerate(slots):
        u.c = s
        u.g, u.l0, u.nxt, u.bank = 0, 0, None, s % 2
        u.head = not u.final and u.j == 0
        u.last_of_layer = u.final or (u.layer == 5 and u.j == 1)
        u.size = P if u.final else u.rows * P // 2
        u.before, u.after, u.gn, u.tail, u.tails, u.ends, u.need_halo = [], [], None, 0, [], None, 0
        u.n_stats = u.j + 1
    taken = {"act": 0, "dve": 0}
    for u in slots:
        u.by = "dve" if 0 < u.batch and u.stream == "A" and u.j % 2 == 0 and not u.final else "act"
        u.taken = taken[u.by]
        taken[u.by] += 1
    for u in slots:
        before = slots[u.c - 2] if u.c >= 2 else None
        u.free_by, u.free = (before.by, before.taken + 1) if before is not None else ("act", 0)
    gn = 0
    for u in slots:
        if u.last_of_layer:
            u.gn = gn
            gn += 1
    ends = {(u.layer, u.batch): u for u in slots if u.last_of_layer}
    lead = slots[:2]
    for u in slots:
        u.coef_need = 1 if u.layer == 1 else ends[(u.layer - 1, u.batch)].gn + 2
        if u.final or u in lead:
            continue
        at = u.c - 2
        dep = ends.get((u.layer - 1, u.batch)) if u.layer > 1 else None
        if dep is not None and dep.c >= at:
            slots[dep.c].after.append(u)
        else:
            slots[at].before.append(u)
    g = l0 = 0
    for u in lead + [v for t in slots for v in t.before + t.after]:
        u.g, u.slot_g = g, g % 2
        g += 1
        if u.stream == "A":
            u.l0 = l0
            l0 += 1
    by = {"A": [u for u in slots if u.stream == "A"], "B": [u for u in slots if u.stream == "B"]}
    for st in by.values():
        units = [u for u in st if not u.final]
        for n, u in enumerate(units):
            u.nxt = units[n + 1] if n + 1 < len(units) and units[n + 1].j == u.j + 1 and u.layer != 5 else None
            prev = [v for v in st if v.c < u.c]
            same = [v for v in prev if (not v.final and v.par == u.par)]
            u.buf_free = same[-1].c + 1 if same else 0
            if same:
                for v in prev:
                    if v.final and v.c > same[-1].c and (v.j - 1) % 2 == u.par:
                        u.buf_free = max(u.buf_free, v.c + 1)
            u.all_before = prev[-1].c + 1 if prev else 0
            u.nxt_g = u.nxt.g + 1 if u.nxt is not None else 0
            u.l0_wait = units[n - 2].g + 1 if u.stream == "A" and n >= 2 else 0
    issued = len(lead)
    for u in slots:
        issued += len(u.before)
        u.read = issued - 1
        issued += len(u.after)
    for u in slots:
        if not u.final and u.nxt is not None:
            slots[max(u.c, u.nxt.c - 2)].tails.append(u)
    for u in slots:
        if u.layer == 5 and u.last_of_layer:
            slots[min(u.c + 2, len(slots) - 1)].ends = u
    order = []
    for u in lead:
        order.append(("head", u)) if u.head else None
    for u in slots:
        for v in u.before:
            if v.head and v.layer != 5:
                order.append(("head", v))
        for v in u.tails:
            order.append(("tail", v))
        for v in u.after:
            if v.head and v.layer != 5:
                order.append(("head", v))
    for n, (kind, u) in enumerate(order):
        if kind == "head":
            u.head_copy = n + 1
        else:
            u.tail = n + 1
    for st in by.values():
        units = [u for u in st if not u.final]
        for n, u in enumerate(units):
            u.need_halo = 0
            if u.layer != 5 and u.j == 1:
                u.need_halo = units[n - 1].head_copy
            elif u.layer != 5 and u.j >= 2:
                u.need_halo = units[n - 2].tail
            u.halo_read = 0
            same = [v for v in units[:n] if v.par == u.par]
            if same:
                v = same[-1]
                m = units.index(v)
                reads = []
                if v.head and v.layer != 5:
                    reads.append(v.head_copy)
                if m >= 1 and units[m - 1].nxt is v:
                    reads.append(units[m - 1].tail)
                u.halo_read = max(reads, default=0)
    return lead, gn


def moved(u, i, later):
    v = Slot(u.stream, u.layer, u.batch, u.j + i * (later.j - u.j), u.rows, u.final)
    v.par, v.size, v.head, v.nxt, v.last_of_layer = u.par, u.size, u.head, u.nxt, u.last_of_layer
    v.bank, v.slot_g = u.c % 2, u.g % 2
    v.by, v.free_by = u.by, u.free_by
    v.taken = u.taken + i * (later.taken - u.taken)
    v.free = u.free + i * (later.free - u.free)
    v.c = u.c + i * (later.c - u.c)
    v.g = u.g + i * (later.g - u.g)
    v.buf_free = u.buf_free + i * (later.buf_free - u.buf_free)
    v.need_halo = u.need_halo + i * (later.need_halo - u.need_halo)
    v.halo_read = u.halo_read + i * (later.halo_read - u.halo_read)
    v.nxt_g = u.nxt_g + i * (later.nxt_g - u.nxt_g)
    v.l0 = u.l0 + i * (later.l0 - u.l0)
    v.l0_wait = u.l0_wait + i * (later.l0_wait - u.l0_wait)
    v.read = u.read + i * (later.read - u.read)
    v.gn, v.tails, v.ends = None, [v], None
    return v


def take(eng, slots, loops, work):
    s = 0
    spans = {first: (size, times) for first, size, times in loops}
    while s < len(slots):
        if s in spans:
            size, times = spans[s]
            with eng.Fori(0, times) as i:
                for k in range(size):
                    t, later = slots[s + k], slots[s + size + k]
                    work(moved(t, i, later), [moved(x, i, y) for x, y in zip(t.before, later.before)], [])
            s += size * times
        else:
            t = slots[s]
            work(t, t.before, t.after)
            s += 1


def is_zero(n):
    return isinstance(n, int) and n == 0


def is_low(n, least):
    return isinstance(n, int) and n < least


def needs(t, p):
    return not t.final and t.layer == p.layer + 1 and t.batch == p.batch and t.head


def audio_tower(nc, x, w, par, t_in, out):
    slots, loops = plan()
    lead, n_gn = number(slots)
    outer, ctx = ExitStack(), ExitStack()
    kept = outer.enter_context(nc.sbuf_tensor("kept", [C, R * FE], F32))
    h5 = kept[:, 0:B * R * P].rearrange("c (b t) -> c b t", b=B)
    sb = lambda name, shape, dt=F32: ctx.enter_context(nc.sbuf_tensor(name, shape, dt))
    psum = lambda name, shape, dt=F32: ctx.enter_context(nc.psum_tensor(name, shape, dt))
    sem = lambda name: ctx.enter_context(nc.semaphore(name))

    y = [None] + [sb(f"y{n}", [C, (ROWS[n] + (n < 5)) * P]) for n in range(1, 6)]
    place = [0]

    def early(words):
        place[0] += words
        return y[1][:, place[0] - words:place[0]]

    wn = [early(C * TAPS[n] if n else K0 + 2) for n in range(6)]
    wn[0] = wn[0][:, 0:K0]
    wh = [early(C * 3 // 2).bitcast(F16) for _ in range(2)]
    wl = [early(C * 3 // 2).bitcast(F16) for _ in range(2)]
    w0h = sb("w0h", [C, K0], F16)
    w0l = sb("w0l", [C, K0], F16)
    w0pad = sb("w0pad", [C, CH, CW])
    w0pad16 = sb("w0pad16", [C, CH, TK], F16)
    w0T = sb("w0T", [CW, CH, C])
    w0T16 = sb("w0T16", [TK, CH, C], F16)
    wT = [None] + [sb(f"wT{n}", [C, 2, TAPS[n], C], F16) for n in range(1, 6)]
    pars = sb("pars", [C, 6, 3])
    big = sb("big", [C, 6 + B])
    bigall = sb("bigall", [C, 6 + B])
    pow2 = sb("pow2", [C, 6 + B])
    inv2 = sb("inv2", [C, 6 + B])
    up = sb("up", [C, 6 + B])
    down = sb("down", [C, 6])
    unscale = sb("unscale", [C, 6 + B])
    unscale2 = sb("unscale2", [C, 6])
    ident = sb("ident", [C, C])
    ident16 = sb("ident16", [C, C], F16)
    quad = sb("quad", [C, C])
    ones = sb("ones", [C, C])
    mhalf = sb("mhalf", [C, B])
    x16 = sb("x16", [P, B, XW, 4], F16)
    xlast = sb("xlast", [C, B, S0])
    gram = sb("gram", [CW, B, CW])
    xsum = early(B * CW)[0:P, :].rearrange("p (b s) -> p b s", b=B)
    energy = early(B * CH * CW).rearrange("p (b s) -> p b s", b=B)
    acc = sb("acc", [C, 4, B])
    stat0 = sb("stat0", [C, B, 2])
    x0T = sb("x0T", [TK, 2, NCH, P], F16)
    xs = y[2][0:P, 0:B * XW].rearrange("p (b s) -> p b s", b=B)
    geluf = sb("geluf", [C, 2, UC])
    ring = {s: sb(f"ring{s}", [C, 2, 2, PL], F16) for s in "AB"}
    wrap = {s: sb(f"wrap{s}", [C, 2, P], F16) for s in "AB"}
    bst = {s: sb(f"bst{s}", [C, 25 * 6]) for s in "AB"}
    mv = sb("mv", [C, 2])
    gs = sb("gs", [C, 16])
    coef0 = sb("coef0", [C, B, 2])
    coef = sb("coef", [C, 6, 2])

    p_l0 = psum("p_l0", [C, 4, 512])
    p_y = psum("p_y", [C, 2, 512])
    p_t = psum("p_t", [C, 512])
    p_m = psum("p_m", [C, 512])
    p_w16 = [p_m[:, :].bitcast(F16), p_l0[:, 3, :].bitcast(F16)]

    loaded_x, loaded_w, loaded_p, loaded_xl = [sem(f"loaded_x{n}") for n in range(2)], [sem(f"loaded_w{n}") for n in range(6)], sem("loaded_p"), sem("loaded_xl")
    zeroed, halo0 = sem("zeroed"), sem("halo0")
    made_ident, made_quad, made_big = sem("made_ident"), sem("made_quad"), sem("made_big")
    all_big = sem("all_big")
    dve = sem("dve")
    w_split, w_turned, w_kept = sem("w_split"), sem("w_turned"), sem("w_kept")
    g_done, g_kept, u_done = sem("g_done"), sem("g_kept"), sem("u_done")
    x_split, x_summed = sem("x_split"), sem("x_summed")
    t_mm, t_kept = sem("t_mm"), sem("t_kept")
    l0_done, gelu_done, hi_done, lo_done, halo_done = sem("l0_done"), sem("gelu_done"), sem("hi_done"), sem("lo_done"), sem("halo_done")
    conv_done, evac_done = sem("conv_done"), {by: sem(f"evac_done_{by}") for by in ("act", "dve")}
    gn_stat, gn_group, gn_var, gn_pow, gn_coef = sem("gn_stat"), sem("gn_group"), sem("gn_var"), sem("gn_pow"), sem("gn_coef")
    emb_done = sem("emb_done")

    block = ctx.enter_context(nc.Block())

    def buf(t, parts, ap, off=0):
        row = 1
        for d in t.shape[1:]:
            row *= d
        return bass.AP(t, off, [[row, parts]] + ap)

    def ring_rows(u, plane, row, ap):
        return buf(ring[u.stream], C, ap, off=(u.par * 2 + plane) * PL + row * P)

    def first_row(u):
        return [[P, CH], [CH * P, 2], [1, P]] if u.stream == "A" else [[1, u.rows * P]]

    def split_ap(t, u):
        return buf(t, C, [[2 * P, CH], [P, 2], [1, P]] if u.stream == "A" else [[1, u.rows * P]], off=u.slot_g * UC)

    def y_out(u):
        return y[u.layer][:, bass.ds(u.j * OC, u.size)]

    @block.sync
    def _(sp):
        sp.wait_ge(halo0, 1)
        for b in range(0, B, 2):
            for p0, p1, n in ((0, 112, XW), (112, P - 1, XW), (P - 1, P, SP)):
                sp.dma_start(xs[p0:p1, b:b + 2, 0:n], bass.AP(x.tensor, b * L + p0 * SP, [[SP, p1 - p0], [L, 2], [1, n]])).then_inc(loaded_x[b // 2], 16)
        sp.dma_start(xlast[:, :, :], bass.AP(x.tensor, L - S0, [[0, C], [L, B], [1, S0]])).then_inc(loaded_xl, 16)

    @block.gpsimd
    def _(pool):
        pool.memset(ident[:, :], 0.0).then_inc(zeroed, 1)
        pool.memset(ident16[:, :], 0.0).then_inc(zeroed, 1)
        pool.memset(quad[:, :], 0.25).then_inc(zeroed, 1)
        pool.memset(mhalf[:, :], -0.5).then_inc(zeroed, 1)
        for s in "AB":
            pool.memset(ring[s][:, :, :, :], 0.0).then_inc(zeroed, 1)
        pool.wait_ge(zeroed, 6)
        for m in (ident, ident16):
            pool.affine_select(out=m[:, :], in_=m[:, :], compare_op=ALU.not_equal, fill=1.0, base=0,
                               pattern=[[-1, C]], channel_multiplier=1).then_inc(made_ident, 1)
        q = quad[:, :].rearrange("p (g c) -> p g c", c=4)
        pool.affine_select(out=q, in_=q, compare_op=ALU.is_ge, fill=0.0, base=0,
                           pattern=[[-4, 32], [0, 4]], channel_multiplier=1).then_inc(made_quad, 1)
        pool.wait_ge(made_quad, 1)
        pool.affine_select(out=q, in_=q, compare_op=ALU.is_ge, fill=0.0, base=3,
                           pattern=[[4, 32], [0, 4]], channel_multiplier=-1).then_inc(made_quad, 1)
        pool.wait_ge(made_big, 1)
        pool.partition_all_reduce(bigall[:, 6:6 + B], big[:, 6:6 + B], C, bass.bass_isa.ReduceOp.max).then_inc(all_big, 1)

        def power(n, v):
            pool.wait_ge(gn_var, n)
            pool.tensor_tensor(v, v, mhalf[:, 0:v.shape[1]], ALU.pow).then_inc(gn_pow, 1)

        power(1, gs[:, 0:B])

        for t in slots:
            if t.gn is not None:
                power(t.gn + 2, gs[:, 0:1])

    @block.scalar
    def _(act):
        for n in range(6):
            act.dma_start(wn[n][:, :], w[n]).then_inc(loaded_w[n], 16)
        for n in range(6):
            for k in range(3):
                act.dma_start(pars[:, n, k:k + 1], par[n][k].rearrange("(c o) -> c o", o=1)).then_inc(loaded_p, 16)
        act.wait_ge(w_turned, 1)
        nc.scalar.copy(w0T16[:, :, :], p_w16[0][0:TK, 0:CH * C].rearrange("p (i c) -> p i c", i=CH)).then_inc(w_kept, 1)
        act.wait_ge(w_turned, 2)
        nc.scalar.copy(w0T[:, :, :], p_l0[0:CW, 2, 0:CH * C].rearrange("p (i c) -> p i c", i=CH)).then_inc(w_kept, 1)

        def keep_first(k0, k1):
            with act.Fori(k0, k1) as k:
                for half in range(2):
                    act.wait_ge(t_mm, k * 2 + (half + 1))
                    nc.scalar.copy(buf(x0T, TK, [[1, 2 * P]], off=k * 4 * P + half * 2 * P), p_l0[0:TK, half, 0:2 * P]).then_inc(t_kept, 1)

        keep_first(0, NCH // 6)
        for n in range(1, 6):
            if n == 3:
                keep_first(NCH // 6, NCH // 4)
            act.wait_ge(w_turned, n + 2)
            nc.scalar.copy(wT[n][:, :, :, :], p_w16[(n + 1) % 2][:, 0:2 * TAPS[n] * C]
                     .rearrange("p (s k c) -> p s k c", s=2, k=TAPS[n])).then_inc(w_kept, 1)

        def gelu(u):
            if u.head:
                act.wait_ge(gn_coef, u.coef_need)
            if u.stream == "A":
                act.wait_ge(l0_done, u.l0 + 1)
                src = p_l0[:, 2 * u.par:2 * u.par + 2, 0:2 * CH * P // 2]
                cf = coef0[:, u.batch, :]
                dst = buf(geluf, C, [[UC // 2, 2], [1, UC // 2]], off=u.slot_g * UC)
            else:
                src = y[u.layer - 1][:, bass.ds(u.j * UC + P, u.rows * P)]
                cf = coef[:, u.layer - 1, :]
                dst = geluf[:, u.slot_g, 0:u.rows * P]
            if not is_low(u.g, 2):
                act.wait_ge(hi_done, u.g - 1)
                act.wait_ge(lo_done, u.g - 1)
            nc.scalar.activation(dst, src, GELU, bias=cf[:, 1:2], scale=cf[:, 0:1]).then_inc(gelu_done, 1)
            if not is_zero(u.buf_free):
                act.wait_ge(conv_done, u.buf_free)
            if not is_zero(u.halo_read):
                act.wait_ge(halo_done, u.halo_read)
            act.wait_ge(gelu_done, u.g + 1)
            nc.scalar.copy(ring_rows(u, 0, 2, first_row(u)), split_ap(geluf, u)).then_inc(hi_done, 1)

        def result(t):
            act.wait_ge(gn_coef, t.gn + 2)
            nc.scalar.activation(h5[:, t.batch, :], y[5][:, :], GELU, bias=coef[:, 5, 1:2], scale=coef[:, 5, 0:1]).then_inc(emb_done, 1)

        for u in lead:
            gelu(u)

        def work(t, before, after):
            for u in before:
                gelu(u)
            if t.by == "act":
                act.wait_ge(conv_done, t.c + 1)
                act.wait_ge(gelu_done, t.read)
                if t.layer == 5 and t.head and t.batch:
                    act.wait_ge(emb_done, t.batch)
                nc.scalar.copy(y_out(t), p_y[:, t.bank, 0:t.size]).then_inc(evac_done["act"], 1)
            if t.ends is not None:
                result(t.ends)
            for u in after:
                gelu(u)

        take(act, slots, loops, work)

    @block.vector
    def _(v):
        chain = [0]

        def link(ins):
            chain[0] += 1
            ins.then_inc(dve, 1)
            v.wait_ge(dve, chain[0])

        v.memset(xs[:, :, SP:XW], 0.0).then_inc(halo0, 1)
        v.memset(ones[:, :], 1.0).then_inc(made_ident, 1)
        v.memset(big[:, :], 0.0)
        v.memset(w0pad[:, :, :], 0.0)
        link(v.memset(w0pad16[:, :, :], 0.0))
        for n in range(6):
            v.wait_ge(loaded_w[n], 16)
            v.tensor_reduce(big[:, n:n + 1], wn[n][:, :], AX_X, ALU.max, apply_absolute_value=True)
        v.wait_ge(loaded_x[0], 16 * 3)
        v.tensor_reduce(big[0:P, 6:8], xs[:, 0:2, :], AX_X, ALU.max, apply_absolute_value=True)
        v.wait_ge(loaded_x[1], 16 * 3)
        link(v.tensor_reduce(big[0:P, 8:6 + B], xs[:, 2:B, :], AX_X, ALU.max, apply_absolute_value=True))
        v.tensor_copy(bigall[:, 0:6], big[:, 0:6]).then_inc(made_big, 1)
        v.wait_ge(made_big, 1)
        v.wait_ge(all_big, 1)
        link(v.tensor_scalar(bigall[:, :], bigall[:, :], 1e-30, None, ALU.max))
        link(v.tensor_scalar(pow2[:, :].bitcast(I32), bigall[:, :].bitcast(I32), 0x7F800000, None, ALU.bitwise_and))
        link(v.reciprocal(inv2[:, :], pow2[:, :]))
        v.tensor_scalar(up[:, 0:6], inv2[:, 0:6], 16.0, None, ALU.mult)
        v.tensor_scalar(up[:, 6:6 + B], inv2[:, 6:6 + B], 64.0, None, ALU.mult)
        v.tensor_scalar(unscale[:, 6:6 + B], pow2[:, 6:6 + B], 1.0 / 64, None, ALU.mult)
        link(v.tensor_scalar(unscale[:, 0:6], pow2[:, 0:6], 1.0 / 16, None, ALU.mult))
        v.tensor_tensor(unscale2[:, :], unscale[:, 0:6], unscale[:, 0:6], ALU.mult)
        link(v.tensor_scalar(unscale[:, 6:6 + B], unscale[:, 6:6 + B], unscale[:, 0:1], None, ALU.mult))
        link(v.tensor_scalar(w0h[:, :], wn[0][:, :], up[:, 0:1], None, ALU.mult))
        link(v.scalar_tensor_tensor(out=w0l[:, :], in0=wn[0][:, :], scalar=up[:, 0:1], in1=w0h[:, :], op0=ALU.mult, op1=ALU.subtract))
        for part, t in ((0, w0h), (1, w0l)):
            for s in range(2):
                v.tensor_copy(buf(w0pad16, C, [[TK + 4 * S0, CH], [4, K0]], off=2 * part + s),
                              buf(t, C, [[0, CH], [1, K0]]))
        v.tensor_copy(buf(w0pad, C, [[CW + S0, CH], [1, K0]]), buf(y[1], C, [[0, CH], [1, K0]])).then_inc(w_split, 1)

        def split_x(b):
            link(v.tensor_scalar(x16[:, b, :, 0], xs[:, b, :], up[0:P, 6 + b:7 + b], None, ALU.mult))
            link(v.scalar_tensor_tensor(out=x16[:, b, :, 1], in0=xs[:, b, :], scalar=up[0:P, 6 + b:7 + b], in1=x16[:, b, :, 0],
                                        op0=ALU.mult, op1=ALU.subtract))
            v.tensor_copy(x16[:, b, :, 2:4].bitcast(I32), x16[:, b, :, 0:2].bitcast(I32)).then_inc(x_split, 1)

        def split_w(n):
            w_n = C * TAPS[n]
            h, l = wh[n % 2], wl[n % 2]
            if n > 2:
                v.wait_ge(w_turned, n)
            link(v.tensor_scalar(h[:, 0:w_n], wn[n][:, :], up[:, n:n + 1], None, ALU.mult))
            v.scalar_tensor_tensor(out=l[:, 0:w_n], in0=wn[n][:, :], scalar=up[:, n:n + 1], in1=h[:, 0:w_n],
                                   op0=ALU.mult, op1=ALU.subtract).then_inc(w_split, 1)

        split_x(0)
        for b in range(B):
            v.tensor_reduce(xsum[:, b, :], buf(y[2], P, [[1, CW], [CS, NCH]], off=b * XW), AX_X, ALU.add).then_inc(x_summed, 1)
        v.wait_ge(g_done, 1)
        v.tensor_copy(gram[:, :, :], p_t[0:CW, 0:B * CW].rearrange("p (b s) -> p b s", b=B)).then_inc(g_kept, 1)
        split_w(1)
        split_w(2)
        for b in range(1, B):
            split_x(b)
        v.wait_ge(u_done, 1)
        for b in range(B):
            last = v.tensor_tensor_reduce(out=energy[:, b, :], in0=w0pad[:, :, :].rearrange("p i s -> p (i s)"), in1=p_y[:, 0, b * CH * CW:(b + 1) * CH * CW],
                                   scale=1.0, scalar=0.0, op0=ALU.mult, op1=ALU.add, accum_out=acc[:, 0, b:b + 1])
        link(last)
        v.wait_ge(u_done, 2)
        v.wait_ge(loaded_xl, 16)
        for b in range(B):
            v.tensor_tensor_reduce(out=energy[:, b, :].rearrange("p (i s) -> p i s", i=CH), in0=w0pad[:, :, :],
                                   in1=bass.AP(p_y, 512 + b * CW, [[1024, C], [0, CH], [1, CW]]),
                                   scale=1.0, scalar=0.0, op0=ALU.mult, op1=ALU.add, accum_out=acc[:, 1, b:b + 1])
            last = v.tensor_tensor_reduce(out=xlast[:, b, :], in0=wn[0][:, 0:S0], in1=xlast[:, b, :],
                                          scale=1.0, scalar=0.0, op0=ALU.mult, op1=ALU.add, accum_out=acc[:, 2, b:b + 1])
        link(last)
        link(v.tensor_tensor(acc[:, 3, :], acc[:, 2, :], acc[:, 2, :], ALU.mult))
        v.tensor_tensor(acc[:, 0, :], acc[:, 0, :], acc[:, 3, :], ALU.subtract)
        link(v.tensor_tensor(acc[:, 1, :], acc[:, 1, :], acc[:, 2, :], ALU.subtract))
        v.wait_ge(loaded_p, 16 * 18)
        link(v.tensor_scalar(acc[:, 2, :], acc[:, 1, :], 1.0 / VALID[0], None, ALU.mult))
        link(v.tensor_tensor(acc[:, 3, :], acc[:, 2, :], acc[:, 2, :], ALU.mult))
        link(v.scalar_tensor_tensor(out=acc[:, 3, :], in0=acc[:, 0, :], scalar=1.0 / VALID[0], in1=acc[:, 3, :], op0=ALU.mult, op1=ALU.subtract))
        v.tensor_scalar(stat0[:, :, 0], acc[:, 2, :], pars[:, 0, 0:1], None, ALU.add)
        link(v.tensor_scalar(acc[:, 2, :], acc[:, 2, :], pars[:, 0, 0:1], None, ALU.add))
        link(v.tensor_tensor(acc[:, 2, :], acc[:, 2, :], acc[:, 2, :], ALU.mult))
        v.tensor_tensor(stat0[:, :, 1], acc[:, 2, :], acc[:, 3, :], ALU.add).then_inc(gn_stat, 1)

        def coefs(n, cnt, layer, group, out_scale, out_bias, un):
            a, t, m = gs[:, 0:cnt], gs[:, 4:4 + cnt], gs[:, 8:8 + 2 * cnt]
            mean, square = m[:, 0:2 * cnt:2], m[:, 1:2 * cnt:2]
            v.wait_ge(gn_group, n)
            link(v.tensor_copy(m, group))
            link(v.tensor_tensor(t, mean, mean, ALU.mult))
            link(v.tensor_tensor(t, square, t, ALU.subtract))
            v.tensor_scalar(a, t, 0.0, EPS, ALU.max, ALU.add).then_inc(gn_var, 1)
            v.wait_ge(gn_pow, n)
            link(v.tensor_scalar(a, a, pars[:, layer, 1:2], None, ALU.mult))
            link(v.tensor_tensor(t, mean, a, ALU.mult))
            link(v.tensor_scalar(t, t, -1.0, pars[:, layer, 2:3], ALU.mult, ALU.add))
            v.tensor_tensor(out_scale, a, un, ALU.mult)
            v.scalar_tensor_tensor(out=out_bias, in0=a, scalar=pars[:, layer, 0:1], in1=t, op0=ALU.mult, op1=ALU.add).then_inc(gn_coef, 1)
            v.wait_ge(gn_coef, n)

        for n in range(3, 6):
            split_w(n)
        coefs(1, B, 0, p_y[:, 1, 0:2 * B], coef0[:, :, 0], coef0[:, :, 1], unscale[:, 6:6 + B])

        def keep_chunks(k, b):
            v.wait_ge(t_mm, b * NCH // 2 + k + 1)
            v.tensor_copy(buf(x0T, TK, [[1, 2 * P]], off=(b % 2) * NCH * P + k * 2 * P), p_t[0:TK, 0:2 * P]).then_inc(t_kept, 1)

        def low(u):
            v.wait_ge(hi_done, u.g + 1)
            v.wait_ge(gelu_done, u.g + 1)
            nc.vector.tensor_tensor(ring_rows(u, 1, 2, first_row(u)), split_ap(geluf, u),
                                    ring_rows(u, 0, 2, first_row(u)), ALU.subtract).then_inc(lo_done, 1)
            if u.head and u.layer != 5:
                v.wait_ge(lo_done, u.g + 1)
                if u.all_before:
                    v.wait_ge(conv_done, u.all_before)
                src = ring[u.stream]
                nc.vector.tensor_copy(wrap[u.stream][:, :, :], buf(src, C, [[PL, 2], [1, P]], off=u.par * 2 * PL + 2 * P))
                nc.vector.tensor_copy(buf(src, C, [[PL, 2], [1, 2 * P]], off=(1 - u.par) * 2 * PL),
                                      buf(src, C, [[PL, 2], [1, 2 * P]], off=u.par * 2 * PL + UR * P)).then_inc(halo_done, 1)

        for u in lead:
            low(u)

        def work(t, before, after):
            if t.stream == "A" and not t.final and t.batch + 1 < B:
                keep_chunks(t.j, t.batch + 1)
            for u in before:
                low(u)
            for m in t.tails:
                v.wait_ge(conv_done, m.c + 1)
                v.wait_ge(lo_done, m.nxt_g)
                src = ring[m.stream]
                nc.vector.tensor_copy(buf(src, C, [[PL, 2], [1, 2 * P]], off=m.par * 2 * PL),
                                      buf(src, C, [[PL, 2], [1, 2 * P]], off=(1 - m.par) * 2 * PL + UR * P)).then_inc(halo_done, 1)
            if t.by == "dve":
                v.wait_ge(conv_done, t.c + 1)
                v.wait_ge(gelu_done, t.read)
                nc.vector.tensor_copy(y_out(t), p_y[:, t.bank, 0:t.size]).then_inc(evac_done["dve"], 1)
            v.wait_ge(evac_done[t.by], t.taken + 1)
            skip = P if (t.head and t.layer != 5) else 0
            size = t.size - (1 if t.last_of_layer else 0)
            stats = nc.vector.bn_stats(bst[t.stream][:, bass.ds(t.j * 6, 6)], y[t.layer][:, bass.ds(t.j * OC + skip, size - skip)])
            if t.gn is not None:
                n = t.layer
                link(stats)
                link(v.bn_aggr(mv[:, :], bst[t.stream][:, 0:6 * (t.n_stats)]))
                link(v.tensor_scalar(gs[:, 0:1], mv[:, 0:1], unscale[:, n:n + 1], pars[:, n, 0:1], ALU.mult, ALU.add))
                link(v.tensor_tensor(gs[:, 4:5], gs[:, 0:1], gs[:, 0:1], ALU.mult))
                v.scalar_tensor_tensor(out=gs[:, 1:2], in0=mv[:, 1:2], scalar=unscale2[:, n:n + 1], in1=gs[:, 4:5],
                                       op0=ALU.mult, op1=ALU.add).then_inc(gn_stat, 1)
                coefs(t.gn + 2, 1, n, p_m[:, 0:2], coef[:, n, 0:1], coef[:, n, 1:2], unscale[:, n:n + 1])
            for u in after:
                low(u)

        take(v, slots, loops, work)

    @block.tensor
    def _(pe):
        pe.wait_ge(made_ident, 3)
        for b in range(B):
            pe.wait_ge(loaded_x[b // 2], 16 * 3)
            for c in range(NCH):
                xc = xs[:, b, c * CS:c * CS + CW]
                last = pe.matmul(p_t[0:CW, b * CW:(b + 1) * CW], xc, xc, start=(c == 0), stop=(c == NCH - 1))
        last.then_inc(g_done, 1)
        pe.wait_ge(w_split, 1)
        for i in range(CH):
            last = pe.transpose(p_w16[0][0:TK, i * C:(i + 1) * C], w0pad16[:, i, :], ident16[:, :])
        last.then_inc(w_turned, 1)
        for i in range(CH):
            last = pe.transpose(p_l0[0:CW, 2, i * C:(i + 1) * C], w0pad[:, i, :], ident[:, :])
        last.then_inc(w_turned, 1)

        def turn_chunks(k, b, into):
            for c in range(2):
                last = pe.matmul(into[0:TK, c * P:(c + 1) * P],
                                 buf(x16, P, [[1, TK]], off=b * 4 * XW + k * (8 * CS) + c * 4 * CS),
                                 ident16[0:P, 0:P], start=True, stop=True)
            last.then_inc(t_mm, 1)

        pe.wait_ge(x_split, 1)
        turn_chunks(0, 0, p_l0[:, 0, :])
        turn_chunks(1, 0, p_l0[:, 1, :])

        def turn_first(k0, k1):
            with pe.Fori(k0, k1) as k:
                for half in range(2):
                    pe.wait_ge(t_kept, k * 2 + (half - 1))
                    turn_chunks(k * 2 + half, 0, p_l0[:, half, :])

        turn_first(1, NCH // 6)
        pe.wait_ge(g_kept, 1)
        pe.wait_ge(w_kept, 2)
        for b in range(B):
            for i in range(CH):
                at = (b * CH + i) * CW
                last = pe.matmul(p_y[:, 0, at:at + CW], w0T[:, i, :], gram[:, b, :], start=True, stop=True)
        last.then_inc(u_done, 1)
        pe.wait_ge(x_summed, B)
        pe.matmul(p_y[:, 1, 0:B * CW], ones[0:P, :], xsum[:, :, :].rearrange("p b s -> p (b s)"), start=True, stop=True).then_inc(u_done, 1)

        def turn_weights(n):
            pe.wait_ge(w_split, n + 1)
            pe.wait_ge(w_kept, n)
            for s, t in enumerate((wh[n % 2], wl[n % 2])):
                for k in range(TAPS[n]):
                    at = (s * TAPS[n] + k) * C
                    last = pe.transpose(p_w16[(n + 1) % 2][:, at:at + C], t[:, k:TAPS[n] * C:TAPS[n]], ident16[:, :])
            last.then_inc(w_turned, 1)

        turn_weights(1)
        turn_weights(2)
        turn_first(NCH // 6, NCH // 4)
        pe.wait_ge(gn_stat, 1)
        pe.wait_ge(made_quad, 2)
        pe.matmul(p_y[:, 1, 0:2 * B], quad[:, :], stat0[:, :, :].rearrange("p b s -> p (b s)"), start=True, stop=True).then_inc(gn_group, 1)
        for n in range(3, 6):
            turn_weights(n)
        pe.wait_ge(w_kept, 7)
        pe.wait_ge(x_split, B)

        def first(u):
            pe.wait_ge(t_kept, NCH // 2 if u in lead else u.batch * NCH // 2 + u.j + 1)
            if not is_zero(u.l0_wait):
                pe.wait_ge(gelu_done, u.l0_wait)
            for i in range(CH):
                last = pe.matmul(p_l0[:, 2 * u.par + i // 2, (i % 2) * 2 * P:(i % 2 + 1) * 2 * P], w0T16[:, i, :],
                                 buf(x0T, TK, [[1, 2 * P]], off=(u.batch % 2) * NCH * P + u.j * 2 * P), start=True, stop=True)
            last.then_inc(l0_done, 1)

        for u in lead:
            first(u)

        def conv(t):
            n = t.layer
            if not t.final:
                pe.wait_ge(lo_done, t.g + 1)
            if not is_zero(t.need_halo):
                pe.wait_ge(halo_done, t.need_halo)
            if not is_low(t.c, 2):
                pe.wait_ge(evac_done[t.free_by], t.free)
            out = p_y[:, t.bank, 0:t.size]
            if t.final:
                src, q = ring[t.stream], (t.j - 1) % 2
                ops = []
                for k in range(3):
                    for wp, xp in ((0, 0), (0, 1), (1, 0)):
                        if k < 2:
                            rhs, o = buf(src, C, [[1, P]], off=(q * 2 + xp) * PL + (UR + k) * P), p_y[:, t.bank, 0:P]
                        else:
                            rhs, o = wrap[t.stream][:, xp, 1:P], p_y[:, t.bank, 0:P - 1]
                        ops.append((o, wT[n][:, wp, k, :], rhs))
            else:
                half = t.rows // 2
                base = 2 if n == 5 else 0
                ops = [(out, wT[n][:, wp, k, :], ring_rows(t, xp, base + k, [[2 * P, half], [1, P]]))
                       for k in range(TAPS[n]) for wp, xp in ((0, 0), (0, 1), (1, 0))]
            for m, (o, lhs, rhs) in enumerate(ops):
                last = pe.matmul(o, lhs, rhs, start=(m == 0), stop=(m == len(ops) - 1))
            last.then_inc(conv_done, 1)

        def group(t):
            pe.wait_ge(gn_stat, t.gn + 2)
            pe.matmul(p_m[:, 0:2], quad[:, :], gs[:, 0:2], start=True, stop=True).then_inc(gn_group, 1)

        pending = []

        def work(t, before, after):
            for u in before:
                if u.stream == "A":
                    first(u)
            if pending and needs(t, pending[0]):
                group(pending.pop())
            if t.stream == "A" and not t.final and t.batch + 1 < B:
                pe.wait_ge(t_kept, (t.batch + 1) * (NCH // 2) + t.j)
                turn_chunks(t.j, t.batch + 1, p_t)
            conv(t)
            if pending:
                group(pending.pop())
            if t.gn is not None:
                pending.append(t)
            for u in after:
                if u.stream == "A":
                    first(u)

        take(pe, slots, loops, work)
        if pending:
            group(pending.pop())

    ctx.close()
    with ExitStack() as ctx:
        transformer(nc, ctx, h5, kept, t_in, out)
    outer.close()

class Tick:

    def __init__(self, sem, per, base=0):
        self.sem, self.per, self.base, self.at = sem, per, base, 0

    def wait(self, eng, b, n):
        eng.wait_ge(self.sem, b * self.per + (self.base + n))


def transformer(nc, ctx, h5, kept, w, out):
    sb = lambda name, shape, dt=F32: ctx.enter_context(nc.sbuf_tensor(name, shape, dt))
    sem = lambda name: ctx.enter_context(nc.semaphore(name))
    bank = ctx.enter_context(nc.psum_tensor("bank", [C, 8, 512], F32))

    pwn = [sb("pwn0", [C, C]), sb("pwn1", [E1, C])]
    pwT = sb("pwT", [C, E])
    wqkv = [sb("wqkv0", [C, 3 * E]), sb("wqkv1", [E1, 3 * E])]
    wq16 = [sb("wq16a", [C, 2, 3 * E], F16), sb("wq16b", [E1, 2, 3 * E], F16)]
    most = sb("most", [C, 2])
    scales = sb("scales", [C, 2 + HT])
    pow2 = sb("pow2w", [C, 2 + HT])
    up = sb("upw", [C, 2 + HT])
    unscale = sb("unscalew", [C, 2 + HT])
    wpr = [sb("wpr0", [C, E]), sb("wpr1", [E1, E])]
    fcn = sb("fcn", [C, HT, E])
    w0T = [sb("w0Ta", [C, 2, HID], F16), sb("w0Tb", [E1, 2, HID], F16)]
    w1all = sb("w1all", [C, 2 * HID])
    w1n = [w1all[:, 0:HID], w1all[0:E1, HID:2 * HID]]
    w1T = sb("w1T", [C, HT, E])
    rows = sb("rows", [P, 3, E])
    bfc = sb("bfc", [C, HT])
    alpha = sb("alpha", [C, 6])
    hnum = sb("hnum", [C, HT])
    hnum_i = sb("hnum_i", [C, HT], I32)
    mix = sb("mix", [C, 3, HT])
    tmp = sb("tmp", [C, 3, HT])
    sums = sb("sums", [C, 4])
    pmn = sb("pmn", [M, HD])
    pmT = sb("pmT", [HD, M])
    spread = sb("spread", [HD, 8, HD])
    own = sb("own", [C, 8])
    feat = [sb("feat0", [C, 8, M]), sb("feat1", [E1, 4, M])]
    diag = [sb("diag0", [C, HEADS]), sb("diag1", [E1, HEADS])]
    kvmask = sb("kvmask", [2 * M, GR, 2 * VW])
    ident = sb("identt", [C, C])
    mhalf = sb("mhalft", [P, R])
    feps = sb("feps", [C, 1])
    hcur = sb("hcur", [C, R * P])
    res = sb("res", [P, B, R, E])
    xn = sb("xn", [P, R, E])
    xc = [sb("xc0", [C, 2, R * P], F16), sb("xc1", [E1, 2, R * P], F16)]
    xt = [sb("xt0", [C, B, 2, R * P], F16), sb("xt1", [E1, B, 2, R * P], F16)]
    ft = [sb("ft0", [C, R * P]), sb("ft1", [E1, R * P])]
    sq = [sb("sq0", [C, R * P]), sb("sq1", [E1, R * P])]
    dk = sb("dk", [P, B, R, FE])
    vals = sb("vals", [P, B * R * HEADS, VW])
    kmax = sb("kmax", [C, B, 2 * R])
    kmin = sb("kmin", [C, 2])
    dg = sb("dg", [P, 2, HEADS])
    mq = sb("mq", [P, 2, HEADS])
    st = sb("st", [P, R, 6])
    mv = sb("mvt", [P, R, 2])
    rs = sb("rs", [P, R])
    hid = sb("hid", [C, HT, HALF])
    ek = kept[0:P, :].rearrange("p (r f) -> p r f", f=FE)
    dq = sb("dq", [P, 2, FE])
    q1T = w1all[0:2 * M, 0:2 * GR * P].rearrange("p (a g t) -> p a g t", a=2, g=GR)
    kvm = sb("kvm", [2 * M, GR, 2 * VW])
    zr = sb("zr", [P, 2, HEADS])
    at = sb("at", [P, 2, E])
    prb = sb("prb", [P, 2, E])
    atT = [sb("atT0", [C, 2, P]), sb("atT1", [E1, 2, P])]
    osb = fcn[0:P, :, :]

    loads = [sem(f"load{n}") for n in range(12)]
    made = sem("made")
    tw, twk = sem("tw"), sem("twk")
    ch = sem("ch")
    wq_max, wq_all, wq_high, w0_high, scaled = sem("wq_max"), sem("wq_all"), sem("wq_high"), sem("w0_high"), sem("scaled")
    ready = sem("ready")
    passed = sem("passed")
    gmax, gmax_all, gmax_neg = sem("gmax"), sem("gmax_all"), sem("gmax_neg")
    out_done = sem("out_done")
    T = lambda name, per: Tick(sem(name), per)
    hc, h_mm, var_t, pow_t, xn_t, xt_mm, xt_k = T("hc", 1), T("h_mm", 3), T("var_t", 1), T("pow_t", 1), T("xn_t", 6), T("xt_mm", 2), T("xt_k", 4)
    k_mm, k_k, v_mm, v_k, dk_mm, dk_k = T("k_mm", 4), T("k_k", 8), T("v_mm", 3), T("v_k", 3), T("dk_mm", 6), T("dk_k", 6)
    dg_t = T("dg_t", 6)
    q_mm, q_k, ek_t, k1_t, kv_mm, kv_k = T("q_mm", 4), T("q_k", 8), T("ek_t", 6), T("k1_t", 6), T("kv_mm", 1), T("kv_k", 1)
    dq_mm, dq_t, eq_t, qt_mm, qt_k = T("dq_mm", 6), T("dq_t", 6), T("eq_t", 6), T("qt_mm", 6), T("qt_k", 12)
    o_mm, at_t, at_mm, at_k, pr_mm, pr_k = T("o_mm", 6), T("at_t", 6), T("at_mm", 6), T("at_k", 12), T("pr_mm", 6), T("pr_k", 6)
    var2, pow2_t, x2_t, x2_mm, x2_k = T("var2", 1), T("pow2_t", 1), T("x2_t", 6), T("x2_mm", 2), T("x2_k", 4)
    xt_kept = T("xt_kept", 1)
    xt_l, x2_l = T("xt_l", 4), T("x2_l", 4)
    f_mm, f_k, y_mm, y_k, stored = T("f_mm", 12), T("f_k", 12), T("y_mm", 6), T("y_k", 6), T("stored", 32)

    block = ctx.enter_context(nc.Block())

    KEY_BANKS, QUERY_BANKS, FORWARD_BANKS = ((2, 4), (3, 5)), ((0, 1), (4, 5)), (2, 3)
    W1_BANKS = (2, 3, 6)
    TURN_BANKS, VALUE_BANKS, EMBED_BANKS = (2, 3), (0, 1, 0), (0, 1, 6)
    FEATURE_BANKS = ((6, 7), (4, 5))
    part = lambda what, half, *n: [(what, half, t) for t in n]
    BEFORE = part("turn", 0, 0)
    FILL = [part("hidden", 0, 0, 1), part("hidden", 0, 2, 3), part("hidden", 0, 4, 5), part("out", 0, 0, 1, 2), part("turn", 1, 0), part("hidden", 1, 0, 1), part("hidden", 1, 2, 3), part("hidden", 1, 4, 5), part("out", 1, 0, 1, 2), []]

    def tile_(t, r):
        return t[:, r * P:(r + 1) * P]

    ops = {"pw": (0, 2), "rows": (1, 3), "qkv": (2, 2), "pr": (3, 2), "fc": (4, 1), "w1": (5, 2), "bfc": (6, 1), "alpha": (7, 2), "pm": (8, 1)}

    def loaded(eng, what):
        n, times = ops[what]
        eng.wait_ge(loads[n], 16 * times)

    @block.sync
    def _(sp):
        def load(what, dst, src, slow=False):
            sp.dma_start(dst, src, allow_slow_non_contiguous=slow).then_inc(loads[ops[what][0]], 16)

        load("pw", pwn[0][:, :], w["tok_pw"][0:C, :])
        load("pw", pwn[1][:, :], w["tok_pw"][C:E, :])
        load("pm", pmn[:, :], w["attn_proj_mat"])
        for n, name in enumerate(("tok_pb", "attn_b_proj", "ffn_b_proj")):
            load("rows", rows[:, n, :], bass.AP(w[name].tensor, 0, [[0, P], [1, E]]))
        for n in range(2):
            load("qkv", wqkv[n][:, :], w["attn_W_qkv"][n * C:n * C + (C, E1)[n], :])
            load("pr", wpr[n][:, :], w["attn_W_proj"][n * C:n * C + (C, E1)[n], :])
            load("w1", w1n[n][:, :], w["ffn_w_proj"][n * C:n * C + (C, E1)[n], :])
        load("fc", fcn[:, :, :], w["ffn_w_fc"].rearrange("(t p) e -> p t e", p=C))
        load("bfc", bfc[:, :], w["ffn_b_fc"].rearrange("(t p) -> p t", p=C), slow=True)
        for n, name in enumerate(("ffn_alpha_e", "ffn_alpha_r")):
            load("alpha", alpha[:, 3 * n:3 * n + 3], bass.AP(w[name].tensor, 0, [[0, C], [1, 3]]))
        sp.sem_inc(stored.sem, 32)
        with sp.Fori(0, B) as b:
            y_k.wait(sp, b, R)
            row = b * (E * (R * P - 1))
            sp.dma_start(bass.AP(out.tensor, row, [[R * E, P - 1], [1, R * E]]), osb[0:P - 1, :, :].rearrange("p r e -> p (r e)")).then_inc(stored.sem, 16)
            sp.dma_start(bass.AP(out.tensor, row + (P - 1) * R * E, [[R * E, 1], [1, (R - 1) * E]]),
                         osb[P - 1:P, 0:R - 1, :].rearrange("p r e -> p (r e)")).then_inc(stored.sem, 16)
        sp.wait_ge(stored.sem, 32 * B + 32)

    @block.gpsimd
    def _(pool):
        def step(ins, n):
            ins.then_inc(made, 1)
            pool.wait_ge(made, n)

        pool.memset(ident[:, :], 0.0).then_inc(made, 1)
        pool.memset(spread[:, :, :], 0.0).then_inc(made, 1)
        pool.memset(own[:, :], 1.0).then_inc(made, 1)
        step(pool.memset(kvmask[:, :, :], 1.0), 4)
        pool.iota(hnum_i[:, :], pattern=[[C, HT]], base=0, channel_multiplier=1).then_inc(made, 1)
        pool.affine_select(out=ident[:, :], in_=ident[:, :], compare_op=ALU.not_equal, fill=1.0, base=0,
                           pattern=[[-1, C]], channel_multiplier=1).then_inc(made, 1)
        pool.affine_select(out=spread[:, :, :], in_=spread[:, :, :], compare_op=ALU.not_equal, fill=1.0, base=0,
                           pattern=[[0, 8], [-1, HD]], channel_multiplier=1).then_inc(made, 1)
        pool.affine_select(out=own[:, :], in_=own[:, :], compare_op=ALU.is_ge, fill=0.0, base=0,
                           pattern=[[-HD, 8]], channel_multiplier=1).then_inc(made, 1)
        m = kvmask[:, :, :].rearrange("p g (a v) -> p g a v", a=2)
        step(pool.affine_select(out=m, in_=m, compare_op=ALU.is_ge, fill=0.0, base=0,
                                pattern=[[0, GR], [-M, 2], [0, VW]], channel_multiplier=1), 9)
        pool.affine_select(out=own[:, :], in_=own[:, :], compare_op=ALU.is_ge, fill=0.0, base=HD - 1,
                           pattern=[[HD, 8]], channel_multiplier=-1).then_inc(made, 1)
        pool.affine_select(out=m, in_=m, compare_op=ALU.is_ge, fill=0.0, base=M - 1,
                           pattern=[[0, GR], [M, 2], [0, VW]], channel_multiplier=-1).then_inc(made, 1)
        pool.memset(mhalf[:, :], -0.5).then_inc(made, 1)
        pool.memset(vals[:, :, :], 1.0).then_inc(made, 1)
        pool.memset(kmax[:, :, :], -3e38).then_inc(made, 1)
        pool.memset(feps[:, :], FEPS * RATIO).then_inc(made, 1)
        pool.wait_ge(wq_max, 1)
        pool.partition_all_reduce(scales[:, 0:2], most[:, :], C, bass.bass_isa.ReduceOp.max).then_inc(wq_all, 1)
        with pool.Fori(0, B) as b:
            var_t.wait(pool, b, 1)
            pool.tensor_tensor(rs[:, :], rs[:, :], mhalf[:, :], ALU.pow).then_inc(pow_t.sem, 1)
        pool.wait_ge(gmax, 1)
        pool.partition_all_reduce(kmin[:, 1:2], kmin[:, 0:1], C, bass.bass_isa.ReduceOp.max).then_inc(gmax_all, 1)
        with pool.Fori(0, B) as b:
            var2.wait(pool, b, 1)
            pool.tensor_tensor(rs[:, :], rs[:, :], mhalf[:, :], ALU.pow).then_inc(pow2_t.sem, 1)

    @block.scalar
    def _(act):
        S = nc.scalar

        def turned(b, mm, kept, half, banks):
            mm.wait(act, b, half + 1)
            for n, rowsn in enumerate((C, E1)):
                S.copy(xc[n][:, 0, half * HALF:(half + 1) * HALF], bank[0:rowsn, banks[n], 0:HALF]).then_inc(kept.sem, 1)

        def project(b, mm, kept, banks):
            for half in range(2):
                for n, rowsn in enumerate((C, E1)):
                    mm.wait(act, b, 2 * half + n + 1)
                    src = bank[0:rowsn, banks[half][n], 0:HALF]
                    S.activation(ft[n][:, half * HALF:(half + 1) * HALF], src, ACT.Identity, scale=unscale[0:rowsn, 0:1]).then_inc(kept.sem, 1)
                    S.activation(sq[n][:, half * HALF:(half + 1) * HALF], src, ACT.Square, scale=unscale[0:rowsn, 0:1]).then_inc(kept.sem, 1)

        def keys(b, after):
            xt_kept.wait(act, b, 1)
            for half in range(2):
                turned(b, xt_mm, xt_k, half, TURN_BANKS)
            project(b, k_mm, k_k, KEY_BANKS)
            for q in range(R // 2):
                v_mm.wait(act, b, q + 1)
                S.activation(bass.AP(vals, b * (R * HEADS * VW) + q * 2 * HEADS * VW, [[B * R * HEADS * VW, P], [VW, 2 * HEADS], [1, HD]]),
                             bank[0:P, VALUE_BANKS[q], 0:2 * E].rearrange("p (h d) -> p h d", d=HD), ACT.Identity, scale=unscale[0:P, 0:1]).then_inc(v_k.sem, 1)
            xt_l.wait(act, b, 4)
            for n in range(2):
                last = S.copy(xt[n][:, b, :, :].rearrange("p s t -> p (s t)"), xc[n][:, :, :].rearrange("p s t -> p (s t)"))
            last.then_inc(xt_kept.sem, 1)
            if after is not None:
                h_mm.wait(act, after - 1, 3)
                S.copy(hcur[:, :], h5[:, after, :]).then_inc(hc.sem, 1)

        act.sem_inc(xt_kept.sem, 1)
        S.copy(hcur[:, :], h5[:, 0, :]).then_inc(hc.sem, 1)
        act.wait_ge(scaled, 1)
        for n, rowsn in enumerate((C, E1)):
            S.activation(wq16[n][:, 0, :], wqkv[n][:, :], ACT.Identity, scale=up[0:rowsn, 0:1]).then_inc(wq_high, 1)
        h_mm.wait(act, 0, 3)
        S.copy(hcur[:, :], h5[:, 1, :]).then_inc(hc.sem, 1)
        with act.Fori(0, B - 2) as b:
            keys(b, b + 2)
        keys(B - 2, None)
        keys(B - 1, None)
        act.wait_ge(gmax_neg, 1)

        def attend(b, first, f):
            project(b, q_mm, q_k, QUERY_BANKS)
            forward(f, BEFORE)
            for r in range(R):
                S.activation(ek[:, r, :], dk[:, b, r, :], ACT.Exp, bias=kmin[0:P, 0:1]).then_inc(ek_t.sem, 1)
            if f is None:
                act.wait_ge(tw, 3)
                for n, rowsn in enumerate((C, E1)):
                    S.copy(w0T[n][:, 0, 0:512], bank[0:rowsn, (2, 6)[n], :]).then_inc(w0_high, 1)
                    S.copy(w0T[n][:, 0, 512:768], bank[0:rowsn, (3, 7)[n], 0:256]).then_inc(w0_high, 1)
            for s in range(R + 4):
                if s < R:
                    r = s
                    dq_t.wait(act, b, r + 1)
                    S.activation(dq[:, r % 2, :], dq[:, r % 2, :], ACT.Exp).then_inc(eq_t.sem, 1)
                if 0 <= s - 1 < R:
                    r = s - 1
                    qt_mm.wait(act, b, r + 1)
                    if r >= 2:
                        o_mm.wait(act, b, r - 1)
                    S.activation(q1T[:, r % 2, 0:4, :], bank[0:2 * M, 4, 0:4 * P].rearrange("p (g t) -> p g t", g=4), ACT.Identity,
                                 bias=feps[0:2 * M, :], scale=RATIO).then_inc(qt_k.sem, 1)
                    S.activation(q1T[:, r % 2, 4:6, :], bank[0:2 * M, 5, 0:2 * P].rearrange("p (g t) -> p g t", g=2), ACT.Identity,
                                 bias=feps[0:2 * M, :], scale=RATIO).then_inc(qt_k.sem, 1)
                if 0 <= s - 3 < R:
                    r = s - 3
                    at_mm.wait(act, b, r + 1)
                    if r >= 2 or not first:
                        pr_mm.wait(act, b, r - 1)
                    S.copy(atT[0][:, r % 2, :], bank[0:C, 6, 0:P]).then_inc(at_k.sem, 1)
                    S.copy(atT[1][:, r % 2, :], bank[0:E1, 6, 128:128 + P]).then_inc(at_k.sem, 1)
                forward(f, FILL[s])

        def forward(f, work):
            if f is None:
                return
            for what, half, t in work:
                if what == "turn":
                    turned(f, x2_mm, x2_k, half, FORWARD_BANKS)
                if what == "hidden":
                    if half == 1 and t == 0:
                        y_mm.wait(act, f, 3)
                    if half == 0 and t == 0 and not is_zero(f):
                        y_mm.wait(act, f, 0)
                    f_mm.wait(act, f, HT * half + t + 1)
                    S.activation(hid[:, t, :], bank[:, FORWARD_BANKS[t % 2], 0:HALF], GELU, bias=bfc[:, t:t + 1], scale=unscale[:, 2 + t:3 + t]).then_inc(f_k.sem, 1)

        attend(0, True, None)
        with act.Fori(0, B - 1) as f:
            attend(f + 1, False, f)
        for work in [BEFORE] + FILL:
            forward(B - 1, work)

    @block.vector
    def _(v):
        chain = [0]
        body = [None, 0, 0]

        def link(ins):
            ins.then_inc(ch, 1)
            if body[0] is None:
                chain[0] += 1
                v.wait_ge(ch, chain[0])
            else:
                body[1] += 1
                v.wait_ge(ch, body[0] * body[2] + (chain[0] + body[1]))

        link(v.memset(most[:, :], 0.0))
        loaded(v, "qkv")
        v.tensor_reduce(most[:, 0:1], wqkv[0][:, :], AX_X, ALU.max, apply_absolute_value=True)
        v.tensor_reduce(most[0:E1, 1:2], wqkv[1][:, :], AX_X, ALU.max, apply_absolute_value=True).then_inc(wq_max, 1)
        v.wait_ge(made, 15)
        v.wait_ge(tw, 1)
        v.tensor_copy(pmT[:, :], bank[0:HD, 0, 0:M]).then_inc(twk, 1)
        v.tensor_copy(pwT[:, :], bank[:, 1, 0:E]).then_inc(twk, 1)
        v.wait_ge(tw, 2)
        for n, (rn, hn) in enumerate(((C, 8), (E1, 4))):
            v.scalar_tensor_tensor(out=feat[n][:, :, :], in0=bass.AP(bank, 2 * 512, [[8 * 512, rn], [0, hn], [1, M]]), scalar=NORM,
                                   in1=bass.AP(own, 0, [[8, rn], [1, hn], [0, M]]), op0=ALU.mult, op1=ALU.mult)
        v.memset(diag[0][:, 8:12], 0.0)
        v.memset(diag[1][:, 0:8], 0.0)
        v.tensor_scalar(diag[0][:, 0:8], own[:, :], 0.5 * NORM * NORM, None, ALU.mult)
        v.tensor_scalar(diag[1][:, 8:12], own[0:E1, 0:4], 0.5 * NORM * NORM, None, ALU.mult)
        def factors(c0, c1):
            link(v.tensor_scalar(scales[:, c0:c1], scales[:, c0:c1], 1e-30, None, ALU.max))
            link(v.tensor_scalar(pow2[:, c0:c1].bitcast(I32), scales[:, c0:c1].bitcast(I32), 0x7F800000, None, ALU.bitwise_and))
            link(v.reciprocal(up[:, c0:c1], pow2[:, c0:c1]))
            link(v.tensor_scalar(up[:, c0:c1], up[:, c0:c1], 16.0, None, ALU.mult))
            v.tensor_scalar(unscale[:, c0:c1], pow2[:, c0:c1], 1.0 / 16, None, ALU.mult).then_inc(scaled, 1)

        def prepare_mix():
            loaded(v, "alpha")
            link(v.tensor_copy(hnum[:, :], hnum_i[:, :]))
            for i in range(3):
                for j in range(3):
                    link(v.tensor_scalar(tmp[:, j, :], hnum[:, :], float(RATIOS[j] * EMBEDS[i]), alpha[:, 3 + j:4 + j], ALU.is_lt, ALU.mult))
                link(v.tensor_tensor(tmp[:, 0, :], tmp[:, 0, :], tmp[:, 1, :], ALU.add))
                link(v.tensor_tensor(tmp[:, 0, :], tmp[:, 0, :], tmp[:, 2, :], ALU.add))
                link(v.tensor_scalar(mix[:, i, :], tmp[:, 0, :], alpha[:, i:i + 1], None, ALU.mult))
            link(v.tensor_tensor(mix[:, 1, :], mix[:, 1, :], mix[:, 2, :], ALU.add))
            link(v.tensor_tensor(mix[:, 0, :], mix[:, 0, :], mix[:, 1, :], ALU.add))
            link(v.tensor_tensor(sums[:, 3:4], alpha[:, 3:4], alpha[:, 4:5], ALU.add))
            link(v.tensor_tensor(sums[:, 3:4], sums[:, 3:4], alpha[:, 5:6], ALU.add))
            link(v.tensor_tensor(sums[:, 1:2], alpha[:, 1:2], alpha[:, 2:3], ALU.add))
            link(v.tensor_tensor(sums[:, 0:1], alpha[:, 0:1], sums[:, 1:2], ALU.add))
            v.tensor_scalar(sums[:, 0:2], sums[:, 0:2], sums[:, 3:4], None, ALU.mult)
            link(v.tensor_scalar(sums[:, 2:3], alpha[:, 2:3], sums[:, 3:4], None, ALU.mult))

        def prepare_forward():
            loaded(v, "bfc")
            loaded(v, "fc")
            for s, (e0, e1) in enumerate(SEG):
                v.tensor_scalar(rows[:, 2, e0:e1], rows[:, 2, e0:e1], sums[0:P, s:s + 1], None, ALU.mult)
                last = v.tensor_tensor(fcn[:, :, e0:e1], fcn[:, :, e0:e1], bass.AP(mix, s * HT, [[3 * HT, C], [1, HT], [0, e1 - e0]]), ALU.mult)
            link(last)
            link(v.tensor_reduce(scales[:, 2:2 + HT], fcn[:, :, :], AX_X, ALU.max, apply_absolute_value=True))
            factors(2, 2 + HT)
            v.tensor_tensor(fcn[:, :, :], fcn[:, :, :], bass.AP(up, 2, [[2 + HT, C], [1, HT], [0, E]]), ALU.mult).then_inc(twk, 1)
            v.tensor_tensor(bfc[:, :], bfc[:, :], mix[:, 0, :], ALU.mult)
            v.wait_ge(tw, 3)
            for n, rn in enumerate((C, E1)):
                v.wait_ge(w0_high, 2 * n + 2)
                v.tensor_tensor(w0T[n][:, 1, 0:512], bank[0:rn, (2, 6)[n], :], w0T[n][:, 0, 0:512], ALU.subtract)
                last = v.tensor_tensor(w0T[n][:, 1, 512:768], bank[0:rn, (3, 7)[n], 0:256], w0T[n][:, 0, 512:768], ALU.subtract)
            last.then_inc(twk, 1)
            v.wait_ge(tw, 4)
            for p in range(3):
                for s, (e0, e1) in enumerate(SEG):
                    last = v.tensor_tensor(w1T[:, 2 * p:2 * p + 2, e0:e1], bass.AP(bank, W1_BANKS[p] * 512 + e0, [[8 * 512, C], [E, 2], [1, e1 - e0]]),
                                           bass.AP(mix, s * HT + 2 * p, [[3 * HT, C], [1, 2], [0, e1 - e0]]), ALU.mult)
            last.then_inc(twk, 1)


        def measured(src, var):
            v.sem_inc(passed, 1)
            for r in range(R):
                last = v.bn_stats(st[:, r, :], src(r))
            link(last)
            v.sem_inc(passed, 1)
            for r in range(R):
                last = v.bn_aggr(mv[:, r, :], st[:, r, :])
            link(last)
            v.tensor_scalar(rs[:, :], mv[:, :, 1], EPS, None, ALU.add).then_inc(var.sem, 1)

        def normed(b, src, powed, done):
            powed.wait(v, b, 1)
            for r in range(R):
                v.tensor_scalar(xn[:, r, :], src(r), mv[:, r, 0:1], rs[:, r:r + 1], ALU.subtract, ALU.mult).then_inc(done.sem, 1)

        def wide(k, n0, n):
            return bass.AP(k[0], k[1] + n0, [[2 * HEADS, P], [1, n], [0, M]])

        def lowered(b, high, low, half, banks):
            for n, rn in enumerate((C, E1)):
                high.wait(v, b, 2 * half + n + 1)
                at_ = slice(half * HALF, (half + 1) * HALF)
                v.tensor_tensor(xc[n][:, 1, at_], bank[0:rn, banks[n], 0:HALF], xc[n][:, 0, at_], ALU.subtract).then_inc(low.sem, 1)

        def embed(b):
            for q in range(R // 2):
                h_mm.wait(v, b, q + 1)
                last = v.tensor_tensor(res[:, b, 2 * q:2 * q + 2, :], bank[0:P, EMBED_BANKS[q], 0:2 * E].rearrange("p (r e) -> p r e", r=2),
                                       bass.AP(rows, 0, [[3 * E, P], [0, 2], [1, E]]), ALU.add)
            link(last)
            measured(lambda r: res[:, b, r, :], var_t)

        def features(b, r):
            a, c = FEATURE_BANKS[r % 2]
            dk_mm.wait(v, b, r + 1)
            pn = P - 1 if r == R - 1 else P
            v.tensor_reduce(kmax[0:pn, b, 2 * r:2 * r + 1], bank[0:pn, a, 0:FA], AX_X, ALU.max)
            v.tensor_reduce(kmax[0:pn, b, 2 * r + 1:2 * r + 2], bank[0:pn, c, 0:FE - FA], AX_X, ALU.max)
            if r >= 2:
                dk_k.wait(v, b, r - 1)
            elif not is_zero(b):
                dk_k.wait(v, b, 0)
            v.tensor_copy(dg[:, r % 2, :], bank[0:P, a, FA:FA + HEADS]).then_inc(dg_t.sem, 1)
            dg_t.wait(v, b, r + 1)
            k = (dg, r % 2 * HEADS)
            v.tensor_tensor(dk[:, b, r, 0:FA].rearrange("p (h m) -> p h m", m=M), bank[0:P, a, 0:FA].rearrange("p (h m) -> p h m", m=M), wide(k, 0, 8), ALU.subtract)
            v.tensor_tensor(dk[:, b, r, FA:FE].rearrange("p (h m) -> p h m", m=M), bank[0:P, c, 0:FE - FA].rearrange("p (h m) -> p h m", m=M), wide(k, 8, 4), ALU.subtract).then_inc(dk_k.sem, 1)

        def keys(b, following):
            if following is not None:
                embed(following)
            for r in range(R):
                features(b, r)
                if following is not None:
                    if r == 0:
                        normed(following, lambda r: res[:, following, r, :], pow_t, xn_t)
                    if r >= R - 2:
                        lowered(following, xt_k, xt_l, r - (R - 2), TURN_BANKS)

        def looped(times, links, work):
            with v.Fori(0, times) as i:
                body[0], body[1], body[2] = i, 0, links
                work(i)
            assert body[1] == links, body[1]
            chain[0] += links * times
            body[0] = None

        loaded(v, "rows")
        embed(0)
        v.wait_ge(wq_all, 1)
        link(v.tensor_tensor(scales[:, 0:1], scales[:, 0:1], scales[:, 1:2], ALU.max))
        factors(0, 2)
        normed(0, lambda r: res[:, 0, r, :], pow_t, xn_t)
        for n, rn in enumerate((C, E1)):
            v.wait_ge(wq_high, n + 1)
            v.scalar_tensor_tensor(out=wq16[n][:, 1, :], in0=wqkv[n][:, :], scalar=up[0:rn, 0:1], in1=wq16[n][:, 0, :],
                                   op0=ALU.mult, op1=ALU.subtract).then_inc(ready, 1)
        for half in range(2):
            lowered(0, xt_k, xt_l, half, TURN_BANKS)
        looped(B - 1, 3, lambda b: keys(b, b + 1))
        keys(B - 1, None)
        dk_k.wait(v, B - 1, R)
        v.tensor_reduce(kmin[:, 0:1], kmax[:, :, :].rearrange("p b r -> p (b r)"), AX_X, ALU.max).then_inc(gmax, 1)
        prepare_mix()
        v.wait_ge(gmax_all, 1)
        v.tensor_scalar(kmin[:, 0:1], kmin[:, 1:2], -1.0, None, ALU.mult).then_inc(gmax_neg, 1)

        def attend(b, f):
            if f is not None:
                measured(lambda r: res[:, f, r, :], var2)
                normed(f, lambda r: res[:, f, r, :], pow2_t, x2_t)
                forward(f, BEFORE)
            for s in range(R + 4):
                if s == 1:
                    for r in range(R):
                        ek_t.wait(v, b, r + 1)
                        v.tensor_scalar(ek[:, r, :], ek[:, r, :], FEPS, RATIO, ALU.add, ALU.mult).then_inc(k1_t.sem, 1)
                if s == 2:
                    kv_mm.wait(v, b, 1)
                    v.tensor_tensor(kvm[:, :, :], bank[0:2 * M, 6, 0:GR * 2 * VW].rearrange("p (g c) -> p g c", g=GR), kvmask[:, :, :], ALU.mult).then_inc(kv_k.sem, 1)
                if s < R:
                    r = s
                    a, c = 0, 1
                    dq_mm.wait(v, b, r + 1)
                    if r >= 2:
                        qt_mm.wait(v, b, r - 1)
                    v.tensor_reduce(mq[:, r % 2, 0:8], bank[0:P, a, 0:FA].rearrange("p (h m) -> p h m", m=M), AX_X, ALU.max)
                    link(v.tensor_reduce(mq[:, r % 2, 8:12], bank[0:P, c, 0:FE - FA].rearrange("p (h m) -> p h m", m=M), AX_X, ALU.max))
                    link(v.tensor_tensor(mq[:, r % 2, :], bank[0:P, a, FA:FA + HEADS], mq[:, r % 2, :], ALU.add))
                    k = (mq, r % 2 * HEADS)
                    v.tensor_tensor(dq[:, r % 2, 0:FA].rearrange("p (h m) -> p h m", m=M), bank[0:P, a, 0:FA].rearrange("p (h m) -> p h m", m=M), wide(k, 0, 8), ALU.subtract)
                    v.tensor_tensor(dq[:, r % 2, FA:FE].rearrange("p (h m) -> p h m", m=M), bank[0:P, c, 0:FE - FA].rearrange("p (h m) -> p h m", m=M), wide(k, 8, 4), ALU.subtract).then_inc(dq_t.sem, 1)
                if 0 <= s - 2 < R:
                    r = s - 2
                    o_mm.wait(v, b, r + 1)
                    if r >= 2:
                        at_mm.wait(v, b, r - 1)
                    o = bank[0:P, 7, 0:HEADS * VW].rearrange("p (h c) -> p h c", c=VW)
                    link(v.reciprocal(zr[:, r % 2, :], o[:, :, HD]))
                    v.tensor_tensor(at[:, r % 2, :].rearrange("p (h d) -> p h d", d=HD), o[:, :, 0:HD],
                                    bass.AP(zr, r % 2 * HEADS, [[2 * HEADS, P], [1, HEADS], [0, HD]]), ALU.mult).then_inc(at_t.sem, 1)
                if 0 <= s - 4 < R:
                    r = s - 4
                    pr_mm.wait(v, b, r + 1)
                    v.tensor_tensor(prb[:, r % 2, :], bank[0:P, 7, 256:256 + E], rows[:, 1, :], ALU.add).then_inc(pr_k.sem, 1)
                    pr_k.wait(v, b, r + 1)
                    last = v.tensor_tensor(res[:, b, r, :], res[:, b, r, :], prb[:, r % 2, :], ALU.add)
                    if r == R - 1:
                        link(last)
                forward(f, FILL[s])

        def forward(f, work):
            if f is None:
                return
            for what, half, r in work:
                if what == "turn":
                    lowered(f, x2_k, x2_l, half, FORWARD_BANKS)
                if what == "out":
                    if half == 0 and r == 0:
                        v.wait_ge(stored.sem, f * 32 + 32)
                    r += 3 * half
                    y_mm.wait(v, f, r + 1)
                    link(v.tensor_tensor(osb[:, r, :], bank[0:P, FORWARD_BANKS[r % 3 % 2], 0:E], rows[:, 2, :], ALU.add))
                    v.tensor_tensor(osb[:, r, :], osb[:, r, :], res[:, f, r, :], ALU.add).then_inc(y_k.sem, 1)

        prepare_forward()
        attend(0, None)
        looped(B - 1, 27, lambda f: attend(f + 1, f))
        measured(lambda r: res[:, B - 1, r, :], var2)
        normed(B - 1, lambda r: res[:, B - 1, r, :], pow2_t, x2_t)
        for work in [BEFORE] + FILL:
            forward(B - 1, work)

    @block.tensor
    def _(pe):
        pe.wait_ge(made, 15)
        loaded(pe, "pm")
        loaded(pe, "pw")
        pe.transpose(bank[0:HD, 0, 0:M], pmn[:, :], ident[0:M, 0:M])
        pe.transpose(bank[:, 1, 0:C], pwn[0][:, :], ident[:, :])
        pe.transpose(bank[:, 1, C:E], pwn[1][:, :], ident[0:E1, 0:E1]).then_inc(tw, 1)
        pe.wait_ge(twk, 2)
        pe.matmul(bank[:, 2, 0:M], spread[:, :, :].rearrange("p h d -> p (h d)"), pmT[:, :], start=True, stop=True).then_inc(tw, 1)
        def mm(out, pairs, inc=None):
            for n, (lhs, rhs) in enumerate(pairs):
                last = pe.matmul(out, lhs, rhs, start=(n == 0), stop=(n == len(pairs) - 1))
            if inc:
                last.then_inc(inc.sem, 1)

        def turn(b, need, done, half, banks):
            for k in range(3):
                r = 3 * half + k
                need.wait(pe, b, r + 1)
                pe.transpose(bank[0:C, banks[0], k * P:(k + 1) * P], xn[:, r, 0:C], ident[0:P, 0:P])
                last = pe.transpose(bank[0:E1, banks[1], k * P:(k + 1) * P], xn[:, r, C:E], ident[0:P, 0:P])
            last.then_inc(done.sem, 1)

        def parts(a, b):
            return [(a(0), b(0)), (a(0), b(1)), (a(1), b(0))]

        def project(src, col, done, banks):
            for half in range(2):
                for n, rn in enumerate((C, E1)):
                    c0 = col + n * C
                    mm(bank[:, banks[half][n], 0:HALF],
                       [op for k in range(2) for op in parts(lambda s: wq16[k][:, s, c0:c0 + C], lambda s: src(k, s, half))], done)

        def features(r, a, c, done):
            mm(bank[0:P, a, 0:FA], [(tile_(ft[0], r), feat[0][:, :, :].rearrange("p h m -> p (h m)"))])
            mm(bank[0:P, a, FA:FA + HEADS], [(tile_(sq[n], r), diag[n][:, :]) for n in range(2)])
            mm(bank[0:P, c, 0:FE - FA], [(tile_(ft[1], r), feat[1][:, :, :].rearrange("p h m -> p (h m)"))], done)

        def embed(b, q):
            mm(bank[0:P, EMBED_BANKS[q], 0:E], [(tile_(hcur, 2 * q), pwT[:, :])])
            mm(bank[0:P, EMBED_BANKS[q], E:2 * E], [(tile_(hcur, 2 * q + 1), pwT[:, :])], h_mm)

        def values(b, q):
            for i in range(2):
                mm(bank[0:P, VALUE_BANKS[q], i * E:(i + 1) * E],
                   [op for k in range(2) for op in parts(lambda s: tile_(xc[k][:, s, :], 2 * q + i), lambda s: wq16[k][:, s, 2 * E:3 * E])], (None, v_mm)[i])

        def keys(b, following):
            xt_l.wait(pe, b, 4)
            if following is not None:
                hc.wait(pe, following, 1)
                for q in range(R // 2):
                    embed(following, q)
            project(lambda k, s, half: xc[k][:, s, half * HALF:(half + 1) * HALF], E, k_mm, KEY_BANKS)
            for r in range(R):
                if r == 0:
                    k_k.wait(pe, b, 4)
                    if following is not None:
                        var_t.wait(pe, following, 1)
                if r == 1:
                    k_k.wait(pe, b, 8)
                if r >= 2:
                    dk_k.wait(pe, b, r - 1)
                features(r, *FEATURE_BANKS[r % 2], dk_mm)
                if r == 0:
                    values(b, 0)
                if r == 1:
                    values(b, 1)
                if r == 2:
                    v_k.wait(pe, b, 1)
                    values(b, 2)
                if following is not None and r >= R - 2:
                    if r == R - 1:
                        xt_l.wait(pe, following, 2)
                    turn(following, xn_t, xt_mm, r - (R - 2), TURN_BANKS)

        hc.wait(pe, 0, 1)
        for q in range(R // 2):
            embed(0, q)
        turn(0, xn_t, xt_mm, 0, TURN_BANKS)
        xt_l.wait(pe, 0, 2)
        turn(0, xn_t, xt_mm, 1, TURN_BANKS)
        pe.wait_ge(ready, 2)
        with pe.Fori(0, B - 1) as b:
            keys(b, b + 1)
        keys(B - 1, None)
        v_k.wait(pe, B - 1, 3)
        dk_k.wait(pe, B - 1, R)

        def turn_forward():
            pe.wait_ge(twk, 3)
            for t in range(HT):
                pe.transpose(bank[:, 2 + t // 4, t % 4 * C:t % 4 * C + C], fcn[:, t, 0:C], ident[:, :])
                last = pe.transpose(bank[0:E1, 6 + t // 4, t % 4 * C:t % 4 * C + C], fcn[:, t, C:E], ident[:, :])
            last.then_inc(tw, 1)
            loaded(pe, "w1")
            pe.wait_ge(twk, 4)
            for t in range(HT):
                a = t % 2 * E
                pe.transpose(bank[:, W1_BANKS[t // 2], a:a + C], w1n[0][:, t * C:t * C + C], ident[:, :])
                last = pe.transpose(bank[:, W1_BANKS[t // 2], a + C:a + E], w1n[1][:, t * C:t * C + C], ident[0:E1, 0:E1])
            last.then_inc(tw, 1)

            loaded(pe, "pr")

        def attend(b, f):
            if f is not None:
                dq_t.wait(pe, b, 0)
                qt_k.wait(pe, b, 0)
            project(lambda k, s, half: xt[k][:, b, s, half * HALF:(half + 1) * HALF], 0, q_mm, QUERY_BANKS)
            q_k.wait(pe, b, 8)
            if f is None:
                turn_forward()
            forward(f, BEFORE)
            for s in range(R + 4):
                if s == 2:
                    k1_t.wait(pe, b, R)
                    if f is not None:
                        at_k.wait(pe, b, 0)
                    for g in range(GR):
                        for r in range(R):
                            pn = P - 1 if r == R - 1 else P
                            last = pe.matmul(bank[0:2 * M, 6, g * 2 * VW:(g + 1) * 2 * VW], ek[0:pn, r, g * 2 * M:(g + 1) * 2 * M],
                                             bass.AP(vals, b * (R * HEADS * VW) + (r * HEADS + 2 * g) * VW, [[B * R * HEADS * VW, pn], [1, 2 * VW]]),
                                             start=(r == 0), stop=(r == R - 1))
                    last.then_inc(kv_mm.sem, 1)
                if s < R:
                    if s >= 1:
                        dq_t.wait(pe, b, s)
                    features(s, 0, 1, dq_mm)
                if 0 <= s - 1 < R:
                    r = s - 1
                    eq_t.wait(pe, b, r + 1)
                    if r >= 1:
                        qt_k.wait(pe, b, 2 * r)
                    for g in range(GR):
                        last = pe.transpose(bank[0:2 * M, 4 + g // 4, g % 4 * P:g % 4 * P + P], dq[:, r % 2, g * 2 * M:(g + 1) * 2 * M], ident[0:P, 0:P])
                    last.then_inc(qt_mm.sem, 1)
                if 0 <= s - 2 < R:
                    r = s - 2
                    qt_k.wait(pe, b, 2 * r + 2)
                    kv_k.wait(pe, b, 1)
                    if r >= 3:
                        pr_k.wait(pe, b, r - 2)
                    elif r == 0 and f is not None:
                        pr_k.wait(pe, b, 0)
                    if r >= 1:
                        at_t.wait(pe, b, r)
                    for g in range(GR):
                        last = pe.matmul(bank[0:P, 7, g * 2 * VW:(g + 1) * 2 * VW], q1T[:, r % 2, g, :], kvm[:, g, :], start=True, stop=True)
                    last.then_inc(o_mm.sem, 1)
                if 0 <= s - 3 < R:
                    r = s - 3
                    at_t.wait(pe, b, r + 1)
                    if r >= 1:
                        at_k.wait(pe, b, 2 * r)
                    pe.transpose(bank[0:C, 6, 0:P], at[:, r % 2, 0:C], ident[0:P, 0:P])
                    pe.transpose(bank[0:E1, 6, 128:128 + P], at[:, r % 2, C:E], ident[0:P, 0:P]).then_inc(at_mm.sem, 1)
                if 0 <= s - 4 < R:
                    r = s - 4
                    at_k.wait(pe, b, 2 * r + 2)
                    at_t.wait(pe, b, min(R, r + 3))
                    if r >= 1:
                        pr_k.wait(pe, b, r)
                    mm(bank[0:P, 7, 256:256 + E], [(atT[k][:, r % 2, :], wpr[k][:, :]) for k in range(2)], pr_mm)
                forward(f, FILL[s])

        def forward(f, work):
            if f is None:
                return
            for what, half, n in work:
                if what == "turn":
                    if half == 1 or not is_zero(f):
                        y_k.wait(pe, f, 3 * half)
                    turn(f, x2_t, x2_mm, half, FORWARD_BANKS)
                if what == "hidden":
                    if n == 0:
                        x2_l.wait(pe, f, 2 * half + 2)
                    if n >= 2:
                        f_k.wait(pe, f, HT * half + n - 1)
                    mm(bank[:, FORWARD_BANKS[n % 2], 0:HALF], 
                       [op for k in range(2) for op in parts(lambda s: w0T[k][:, s, n * C:(n + 1) * C], lambda s: xc[k][:, s, half * HALF:(half + 1) * HALF])], f_mm)
                if what == "out":
                    if n == 0:
                        f_k.wait(pe, f, HT * (half + 1))
                    if n == 2:
                        y_k.wait(pe, f, 3 * half + 1)
                    mm(bank[0:P, FORWARD_BANKS[n % 2], 0:E], [(hid[:, t, n * P:(n + 1) * P], w1T[:, t, :]) for t in range(HT)], y_mm)

        attend(0, None)
        with pe.Fori(0, B - 1) as f:
            attend(f + 1, f)
        for work in [BEFORE] + FILL:
            forward(B - 1, work)


_CONV = [f"L0_tok_{k}{n}" for n in range(6) for k in ("cw", "cb", "gw", "gb")]
_REST = ["tok_pw", "tok_pb", "attn_W_qkv", "attn_W_proj", "attn_b_proj", "attn_proj_mat", "ffn_w_fc", "ffn_b_fc",
         "ffn_w_proj", "ffn_b_proj", "ffn_alpha_e", "ffn_alpha_r"]


def kernel(**inputs):
    import numpy as _np
    import concourse.bacc as _bacc
    from concourse import mybir as _mybir
    from concourse.bass_utils import run_bass_kernel_spmd as _run

    nc = _bacc.Bacc("TRN2", target_bir_lowering=False, num_devices=1)
    arrays, args = {}, {}
    for name in ["x"] + _CONV + ["L0_" + n for n in _REST]:
        a = _np.ascontiguousarray(inputs[name])
        if name.startswith("L0_tok_cw"):
            a = a.reshape(a.shape[0], -1)
        arrays[f"in_{name}"] = a
        args[name] = nc.dram_tensor(f"in_{name}", a.shape, _mybir.dt.from_np(a.dtype), kind="ExternalInput").ap()
    out = nc.dram_tensor("out", (B, R * P - 1, E), _mybir.dt.float32, kind="ExternalOutput").ap()
    audio_tower(nc, args["x"], [args[f"L0_tok_cw{n}"] for n in range(6)],
                [[args[f"L0_tok_{k}{n}"] for k in ("cb", "gw", "gb")] for n in range(6)],
                {n: args["L0_" + n] for n in _REST}, out)
    r = _run(nc, [arrays], core_ids=[0])
    return r.results[0]["out"]
```

```python
import math
from contextlib import ExitStack

import numpy as np
import concourse.bass as bass
from concourse import mybir

ALU = mybir.AluOpType
ACT = mybir.ActivationFunctionType
AX_X = mybir.AxisListType.X
F32 = mybir.dt.float32
F16 = mybir.dt.float16
I32 = mybir.dt.int32
GELU = ACT.Gelu_apprx_tanh

B = 4
L = 120000
C = 128
P = 125
SP = L // P
K0, S0 = 10, 5
ROWS = [SP // S0 >> n for n in range(6)]
VALID = [P * r - 1 for r in ROWS]
XW = SP + S0
CH = 4
CS = CH * S0
CW = CS + S0
NCH = SP // CS
TK = 4 * CW
UR = 8
UC = UR * P
OC = UC // 2
TAPS = [K0, 3, 3, 3, 3, 2]
EPS = 1e-5
BUFR = UR + 2
PL = BUFR * P


R = ROWS[5]
E = 192
E1 = E - C
HEADS, HD, M = 12, 16, 44
FE = HEADS * M
FA = 8 * M
GR = HEADS // 2
VW = HD + 1
HID = 768
HT = HID // C
HALF = R * P // 2
NORM = 1.0 / math.sqrt(math.sqrt(HD))
RATIO = 1.0 / math.sqrt(M)
FEPS = 1e-4
EMBEDS, RATIOS = (96, 144, 192), (2, 3, 4)
SEG = ((0, 96), (96, 144), (144, 192))


class Slot:

    def __init__(self, stream, layer, batch, j, rows=UR, final=False):
        self.stream, self.layer, self.batch, self.j, self.rows, self.final = stream, layer, batch, j, rows, final
        self.par = j % 2


def plan():
    slots, loops = [], []

    def a(b, j):
        return Slot("A", 1, b, j)

    def layer_b(n, b):
        return [Slot("B", n, b, j) for j in range(ROWS[n - 1] // UR)] + [Slot("B", n, b, ROWS[n - 1] // UR, final=True)]

    def a_end(b):
        return Slot("A", 1, b, ROWS[0] // UR, final=True)

    def loop(body, times):
        first = len(slots)
        for i in range(times):
            slots.extend(body(i))
        size = (len(slots) - first) // times
        if times > 3:
            loops.append((first + size, size, times - 2))

    na = ROWS[0] // UR
    loop(lambda i: [a(0, 2 * i), a(0, 2 * i + 1)], na // 2)
    slots.append(a_end(0))
    for b in range(1, B):
        l2, l3, l4 = (layer_b(n, b - 1) for n in (2, 3, 4))
        loop(lambda i: [l2[2 * i], a(b, 2 * i), l2[2 * i + 1], a(b, 2 * i + 1)], 5)
        slots.extend([l2[10], l2[11], a(b, 10), l2[12], a(b, 11), a(b, 12), a(b, 13)])
        slots.extend([l3[0], l3[1], l3[2], a(b, 14), l3[3], l3[4], a(b, 15), l3[5], l3[6], a(b, 16), a(b, 17), a(b, 18)])
        slots.extend([l4[0], a(b, 19), l4[1], a(b, 20), l4[2], l4[3], a(b, 21), a(b, 22), a(b, 23), a_end(b)])
        slots.extend([Slot("B", 5, b - 1, 0), Slot("B", 5, b - 1, 1, rows=4)])
    l2, l3, l4 = (layer_b(n, B - 1) for n in (2, 3, 4))
    loop(lambda i: l2[2 * i:2 * i + 2], 6)
    slots.append(l2[12])
    loop(lambda i: l3[2 * i:2 * i + 2], 3)
    slots.append(l3[6])
    slots.extend(l4)
    slots.extend([Slot("B", 5, B - 1, 0), Slot("B", 5, B - 1, 1, rows=4)])
    return slots, loops


def number(slots):
    for s, u in enumerate(slots):
        u.c = s
        u.g, u.l0, u.nxt, u.bank = 0, 0, None, s % 2
        u.head = not u.final and u.j == 0
        u.last_of_layer = u.final or (u.layer == 5 and u.j == 1)
        u.size = P if u.final else u.rows * P // 2
        u.before, u.after, u.gn, u.tail, u.tails, u.ends, u.need_halo = [], [], None, 0, [], None, 0
        u.n_stats = u.j + 1
    taken = {"act": 0, "dve": 0}
    for u in slots:
        shared = u.batch > 0 if u.stream == "A" else u.batch == B - 1 and u.layer < 5
        u.by = "dve" if shared and u.j % 2 == 0 and not u.final else "act"
        u.taken = taken[u.by]
        taken[u.by] += 1
    for u in slots:
        before = slots[u.c - 2] if u.c >= 2 else None
        u.free_by, u.free = (before.by, before.taken + 1) if before is not None else ("act", 0)
    gn = 0
    for u in slots:
        if u.last_of_layer:
            u.gn = gn
            gn += 1
    ends = {(u.layer, u.batch): u for u in slots if u.last_of_layer}
    lead = slots[:2]
    for u in slots:
        u.coef_need = 1 if u.layer == 1 else ends[(u.layer - 1, u.batch)].gn + 2
        if u.final or u in lead:
            continue
        at = u.c - 2
        dep = ends.get((u.layer - 1, u.batch)) if u.layer > 1 else None
        if dep is not None and dep.c >= at:
            slots[dep.c].after.append(u)
        else:
            slots[at].before.append(u)
    g = l0 = 0
    for u in lead + [v for t in slots for v in t.before + t.after]:
        u.g, u.slot_g = g, g % 2
        g += 1
        if u.stream == "A":
            u.l0 = l0
            l0 += 1
    by = {"A": [u for u in slots if u.stream == "A"], "B": [u for u in slots if u.stream == "B"]}
    for st in by.values():
        units = [u for u in st if not u.final]
        for n, u in enumerate(units):
            u.nxt = units[n + 1] if n + 1 < len(units) and units[n + 1].j == u.j + 1 and u.layer != 5 else None
            prev = [v for v in st if v.c < u.c]
            same = [v for v in prev if (not v.final and v.par == u.par)]
            u.buf_free = same[-1].c + 1 if same else 0
            if same:
                for v in prev:
                    if v.final and v.c > same[-1].c and (v.j - 1) % 2 == u.par:
                        u.buf_free = max(u.buf_free, v.c + 1)
            u.all_before = prev[-1].c + 1 if prev else 0
            u.nxt_g = u.nxt.g + 1 if u.nxt is not None else 0
            u.l0_wait = units[n - 2].g + 1 if u.stream == "A" and n >= 2 else 0
    issued = len(lead)
    for u in slots:
        issued += len(u.before)
        u.read = issued - 1
        issued += len(u.after)
    for u in slots:
        if not u.final and u.nxt is not None:
            slots[max(u.c, u.nxt.c - 2)].tails.append(u)
    for u in slots:
        if u.layer == 5 and u.last_of_layer:
            slots[min(u.c + 2, len(slots) - 1)].ends = u
    order = []
    for u in lead:
        order.append(("head", u)) if u.head else None
    for u in slots:
        for v in u.before:
            if v.head and v.layer != 5:
                order.append(("head", v))
        for v in u.tails:
            order.append(("tail", v))
        for v in u.after:
            if v.head and v.layer != 5:
                order.append(("head", v))
    for n, (kind, u) in enumerate(order):
        if kind == "head":
            u.head_copy = n + 1
        else:
            u.tail = n + 1
    for st in by.values():
        units = [u for u in st if not u.final]
        for n, u in enumerate(units):
            u.need_halo = 0
            if u.layer != 5 and u.j == 1:
                u.need_halo = units[n - 1].head_copy
            elif u.layer != 5 and u.j >= 2:
                u.need_halo = units[n - 2].tail
            u.halo_read = 0
            same = [v for v in units[:n] if v.par == u.par]
            if same:
                v = same[-1]
                m = units.index(v)
                reads = []
                if v.head and v.layer != 5:
                    reads.append(v.head_copy)
                if m >= 1 and units[m - 1].nxt is v:
                    reads.append(units[m - 1].tail)
                u.halo_read = max(reads, default=0)
    return lead, gn


def moved(u, i, later):
    v = Slot(u.stream, u.layer, u.batch, u.j + i * (later.j - u.j), u.rows, u.final)
    v.par, v.size, v.head, v.nxt, v.last_of_layer = u.par, u.size, u.head, u.nxt, u.last_of_layer
    v.bank, v.slot_g = u.c % 2, u.g % 2
    v.by, v.free_by = u.by, u.free_by
    v.taken = u.taken + i * (later.taken - u.taken)
    v.free = u.free + i * (later.free - u.free)
    v.c = u.c + i * (later.c - u.c)
    v.g = u.g + i * (later.g - u.g)
    v.buf_free = u.buf_free + i * (later.buf_free - u.buf_free)
    v.need_halo = u.need_halo + i * (later.need_halo - u.need_halo)
    v.halo_read = u.halo_read + i * (later.halo_read - u.halo_read)
    v.nxt_g = u.nxt_g + i * (later.nxt_g - u.nxt_g)
    v.l0 = u.l0 + i * (later.l0 - u.l0)
    v.l0_wait = u.l0_wait + i * (later.l0_wait - u.l0_wait)
    v.read = u.read + i * (later.read - u.read)
    v.gn, v.tails, v.ends = None, [v], None
    return v


def take(eng, slots, loops, work):
    s = 0
    spans = {first: (size, times) for first, size, times in loops}
    while s < len(slots):
        if s in spans:
            size, times = spans[s]
            with eng.Fori(0, times) as i:
                for k in range(size):
                    t, later = slots[s + k], slots[s + size + k]
                    work(moved(t, i, later), [moved(x, i, y) for x, y in zip(t.before, later.before)], [])
            s += size * times
        else:
            t = slots[s]
            work(t, t.before, t.after)
            s += 1


def is_zero(n):
    return isinstance(n, int) and n == 0


def is_low(n, least):
    return isinstance(n, int) and n < least


def needs(t, p):
    return not t.final and t.layer == p.layer + 1 and t.batch == p.batch and t.head


def audio_tower(nc, x, w, par, t_in, out):
    slots, loops = plan()
    lead, n_gn = number(slots)
    outer, ctx = ExitStack(), ExitStack()
    kept = outer.enter_context(nc.sbuf_tensor("kept", [C, R * FE], F32))
    h5 = kept[:, 0:B * R * P].rearrange("c (b t) -> c b t", b=B)
    sb = lambda name, shape, dt=F32: ctx.enter_context(nc.sbuf_tensor(name, shape, dt))
    psum = lambda name, shape, dt=F32: ctx.enter_context(nc.psum_tensor(name, shape, dt))
    sem = lambda name: ctx.enter_context(nc.semaphore(name))

    y = [None] + [sb(f"y{n}", [C, (ROWS[n] + (n < 5)) * P]) for n in range(1, 6)]
    place = [0]

    def early(words):
        place[0] += words
        return y[1][:, place[0] - words:place[0]]

    wn = [early(C * TAPS[n] if n else K0 + 2) for n in range(6)]
    wn[0] = wn[0][:, 0:K0]
    wh = [early(C * 3 // 2).bitcast(F16) for _ in range(2)]
    wl = [early(C * 3 // 2).bitcast(F16) for _ in range(2)]
    w0h = sb("w0h", [C, K0], F16)
    w0l = sb("w0l", [C, K0], F16)
    w0pad = sb("w0pad", [C, CH, CW])
    w0pad16 = sb("w0pad16", [C, CH, TK], F16)
    w0T = sb("w0T", [CW, CH, C])
    w0T16 = sb("w0T16", [TK, CH, C], F16)
    wT = [None] + [sb(f"wT{n}", [C, 2, TAPS[n], C], F16) for n in range(1, 6)]
    pars = sb("pars", [C, 6, 3])
    big = sb("big", [C, 6 + B])
    bigall = sb("bigall", [C, 6 + B])
    pow2 = sb("pow2", [C, 6 + B])
    inv2 = sb("inv2", [C, 6 + B])
    up = sb("up", [C, 6 + B])
    unscale = sb("unscale", [C, 6 + B])
    unscale2 = sb("unscale2", [C, 6])
    ident = sb("ident", [C, C])
    ident16 = sb("ident16", [C, C], F16)
    quad = sb("quad", [C, C])
    ones = sb("ones", [C, C])
    mhalf = sb("mhalf", [C, B])
    x16 = sb("x16", [P, B, XW, 4], F16)
    xlast = sb("xlast", [C, B, S0])
    gram = sb("gram", [CW, B, CW])
    xsum = early(B * CW)[0:P, :].rearrange("p (b s) -> p b s", b=B)
    energy = early(B * CH * CW).rearrange("p (b s) -> p b s", b=B)
    acc = sb("acc", [C, 4, B])
    stat0 = sb("stat0", [C, B, 2])
    x0T = sb("x0T", [TK, 2, NCH, P], F16)
    xs = y[2][0:P, 0:B * XW].rearrange("p (b s) -> p b s", b=B)
    geluf = sb("geluf", [C, 2, UC])
    ring = {s: sb(f"ring{s}", [C, 2, 2, PL], F16) for s in "AB"}
    wrap = {s: sb(f"wrap{s}", [C, 2, P], F16) for s in "AB"}
    bst = {s: sb(f"bst{s}", [C, 25 * 6]) for s in "AB"}
    mv = sb("mv", [C, 2])
    gs = sb("gs", [C, 16])
    coef0 = sb("coef0", [C, B, 2])
    coef = sb("coef", [C, 6, 2])

    p_l0 = psum("p_l0", [C, 4, 512])
    p_y = psum("p_y", [C, 2, 512])
    p_t = psum("p_t", [C, 512])
    p_m = psum("p_m", [C, 512])
    p_w16 = [p_m[:, :].bitcast(F16), p_l0[:, 3, :].bitcast(F16)]

    loaded_x, loaded_w, loaded_p, loaded_xl = [sem(f"loaded_x{n}") for n in range(2)], [sem(f"loaded_w{n}") for n in range(6)], sem("loaded_p"), sem("loaded_xl")
    zeroed, halo0 = sem("zeroed"), sem("halo0")
    made_ident, made_quad, made_big = sem("made_ident"), sem("made_quad"), sem("made_big")
    all_big = sem("all_big")
    dve = sem("dve")
    w_split, w_turned, w_kept = sem("w_split"), sem("w_turned"), sem("w_kept")
    g_done, g_kept, u_done = sem("g_done"), sem("g_kept"), sem("u_done")
    x_split, x_summed = sem("x_split"), sem("x_summed")
    t_mm, t_kept = sem("t_mm"), sem("t_kept")
    l0_done, gelu_done, hi_done, lo_done, halo_done = sem("l0_done"), sem("gelu_done"), sem("hi_done"), sem("lo_done"), sem("halo_done")
    conv_done, evac_done = sem("conv_done"), {by: sem(f"evac_done_{by}") for by in ("act", "dve")}
    gn_stat, gn_group, gn_var, gn_pow, gn_coef = sem("gn_stat"), sem("gn_group"), sem("gn_var"), sem("gn_pow"), sem("gn_coef")
    emb_done = sem("emb_done")

    block = ctx.enter_context(nc.Block())

    def buf(t, parts, ap, off=0):
        row = 1
        for d in t.shape[1:]:
            row *= d
        return bass.AP(t, off, [[row, parts]] + ap)

    def ring_rows(u, plane, row, ap):
        return buf(ring[u.stream], C, ap, off=(u.par * 2 + plane) * PL + row * P)

    def first_row(u):
        return [[P, CH], [CH * P, 2], [1, P]] if u.stream == "A" else [[1, u.rows * P]]

    def split_ap(t, u):
        return buf(t, C, [[2 * P, CH], [P, 2], [1, P]] if u.stream == "A" else [[1, u.rows * P]], off=u.slot_g * UC)

    def y_out(u):
        return y[u.layer][:, bass.ds(u.j * OC, u.size)]

    @block.sync
    def _(sp):
        sp.wait_ge(halo0, 1)
        for b in range(0, B, 2):
            for p0, p1, n in ((0, 112, XW), (112, P - 1, XW), (P - 1, P, SP)):
                sp.dma_start(xs[p0:p1, b:b + 2, 0:n], bass.AP(x.tensor, b * L + p0 * SP, [[SP, p1 - p0], [L, 2], [1, n]])).then_inc(loaded_x[b // 2], 16)
        sp.dma_start(xlast[:, :, :], bass.AP(x.tensor, L - S0, [[0, C], [L, B], [1, S0]])).then_inc(loaded_xl, 16)

    @block.gpsimd
    def _(pool):
        pool.memset(ident[:, :], 0.0).then_inc(zeroed, 1)
        pool.memset(ident16[:, :], 0.0).then_inc(zeroed, 1)
        pool.memset(quad[:, :], 0.25).then_inc(zeroed, 1)
        pool.memset(mhalf[:, :], -0.5).then_inc(zeroed, 1)
        for s in "AB":
            pool.memset(ring[s][:, :, :, :], 0.0).then_inc(zeroed, 1)
        pool.wait_ge(zeroed, 6)
        for m in (ident, ident16):
            pool.affine_select(out=m[:, :], in_=m[:, :], compare_op=ALU.not_equal, fill=1.0, base=0,
                               pattern=[[-1, C]], channel_multiplier=1).then_inc(made_ident, 1)
        q = quad[:, :].rearrange("p (g c) -> p g c", c=4)
        pool.affine_select(out=q, in_=q, compare_op=ALU.is_ge, fill=0.0, base=0,
                           pattern=[[-4, 32], [0, 4]], channel_multiplier=1).then_inc(made_quad, 1)
        pool.wait_ge(made_quad, 1)
        pool.affine_select(out=q, in_=q, compare_op=ALU.is_ge, fill=0.0, base=3,
                           pattern=[[4, 32], [0, 4]], channel_multiplier=-1).then_inc(made_quad, 1)
        pool.wait_ge(made_big, 1)
        pool.partition_all_reduce(bigall[:, 6:6 + B], big[:, 6:6 + B], C, bass.bass_isa.ReduceOp.max).then_inc(all_big, 1)

        def power(n, v):
            pool.wait_ge(gn_var, n)
            pool.tensor_tensor(v, v, mhalf[:, 0:v.shape[1]], ALU.pow).then_inc(gn_pow, 1)

        power(1, gs[:, 0:B])

        for t in slots:
            if t.gn is not None:
                power(t.gn + 2, gs[:, 0:1])

    @block.scalar
    def _(act):
        for n in range(6):
            act.dma_start(wn[n][:, :], w[n]).then_inc(loaded_w[n], 16)
        for n in range(6):
            for k in range(3):
                act.dma_start(pars[:, n, k:k + 1], par[n][k].rearrange("(c o) -> c o", o=1)).then_inc(loaded_p, 16)
        act.wait_ge(w_turned, 1)
        nc.scalar.copy(w0T16[:, :, :], p_w16[0][0:TK, 0:CH * C].rearrange("p (i c) -> p i c", i=CH)).then_inc(w_kept, 1)
        act.wait_ge(w_turned, 2)
        nc.scalar.copy(w0T[:, :, :], p_l0[0:CW, 2, 0:CH * C].rearrange("p (i c) -> p i c", i=CH)).then_inc(w_kept, 1)

        def keep_first(k0, k1):
            with act.Fori(k0, k1) as k:
                for half in range(2):
                    act.wait_ge(t_mm, k * 2 + (half + 1))
                    nc.scalar.copy(buf(x0T, TK, [[1, 2 * P]], off=k * 4 * P + half * 2 * P), p_l0[0:TK, half, 0:2 * P]).then_inc(t_kept, 1)

        keep_first(0, NCH // 6)
        for n in range(1, 6):
            if n == 3:
                keep_first(NCH // 6, NCH // 4)
            act.wait_ge(w_turned, n + 2)
            nc.scalar.copy(wT[n][:, :, :, :], p_w16[(n + 1) % 2][:, 0:2 * TAPS[n] * C]
                     .rearrange("p (s k c) -> p s k c", s=2, k=TAPS[n])).then_inc(w_kept, 1)

        def gelu(u):
            if u.head:
                act.wait_ge(gn_coef, u.coef_need)
            if u.stream == "A":
                act.wait_ge(l0_done, u.l0 + 1)
                src = p_l0[:, 2 * u.par:2 * u.par + 2, 0:2 * CH * P // 2]
                cf = coef0[:, u.batch, :]
                dst = buf(geluf, C, [[UC // 2, 2], [1, UC // 2]], off=u.slot_g * UC)
            else:
                src = y[u.layer - 1][:, bass.ds(u.j * UC + P, u.rows * P)]
                cf = coef[:, u.layer - 1, :]
                dst = geluf[:, u.slot_g, 0:u.rows * P]
            if not is_low(u.g, 2):
                act.wait_ge(hi_done, u.g - 1)
                act.wait_ge(lo_done, u.g - 1)
            nc.scalar.activation(dst, src, GELU, bias=cf[:, 1:2], scale=cf[:, 0:1]).then_inc(gelu_done, 1)
            if not is_zero(u.buf_free):
                act.wait_ge(conv_done, u.buf_free)
            if not is_zero(u.halo_read):
                act.wait_ge(halo_done, u.halo_read)
            act.wait_ge(gelu_done, u.g + 1)
            nc.scalar.copy(ring_rows(u, 0, 2, first_row(u)), split_ap(geluf, u)).then_inc(hi_done, 1)

        def result(t):
            act.wait_ge(gn_coef, t.gn + 2)
            nc.scalar.activation(h5[:, t.batch, :], y[5][:, :], GELU, bias=coef[:, 5, 1:2], scale=coef[:, 5, 0:1]).then_inc(emb_done, 1)

        for u in lead:
            gelu(u)

        def work(t, before, after):
            for u in before:
                gelu(u)
            if t.by == "act":
                act.wait_ge(conv_done, t.c + 1)
                act.wait_ge(gelu_done, t.read)
                if t.layer == 5 and t.head and t.batch:
                    act.wait_ge(emb_done, t.batch)
                nc.scalar.copy(y_out(t), p_y[:, t.bank, 0:t.size]).then_inc(evac_done["act"], 1)
            if t.ends is not None:
                result(t.ends)
            for u in after:
                gelu(u)

        take(act, slots, loops, work)

    @block.vector
    def _(v):
        chain = [0]

        def link(ins):
            chain[0] += 1
            ins.then_inc(dve, 1)
            v.wait_ge(dve, chain[0])

        v.memset(xs[:, :, SP:XW], 0.0).then_inc(halo0, 1)
        v.memset(ones[:, :], 1.0).then_inc(made_ident, 1)
        v.memset(big[:, :], 0.0)
        v.memset(w0pad[:, :, :], 0.0)
        link(v.memset(w0pad16[:, :, :], 0.0))
        for n in range(6):
            v.wait_ge(loaded_w[n], 16)
            v.tensor_reduce(big[:, n:n + 1], wn[n][:, :], AX_X, ALU.max, apply_absolute_value=True)
        v.wait_ge(loaded_x[0], 16 * 3)
        v.tensor_reduce(big[0:P, 6:8], xs[:, 0:2, :], AX_X, ALU.max, apply_absolute_value=True)
        v.wait_ge(loaded_x[1], 16 * 3)
        link(v.tensor_reduce(big[0:P, 8:6 + B], xs[:, 2:B, :], AX_X, ALU.max, apply_absolute_value=True))
        v.tensor_copy(bigall[:, 0:6], big[:, 0:6]).then_inc(made_big, 1)
        v.wait_ge(made_big, 1)
        v.wait_ge(all_big, 1)
        link(v.tensor_scalar(bigall[:, :], bigall[:, :], 1e-30, None, ALU.max))
        link(v.tensor_scalar(pow2[:, :].bitcast(I32), bigall[:, :].bitcast(I32), 0x7F800000, None, ALU.bitwise_and))
        link(v.reciprocal(inv2[:, :], pow2[:, :]))
        v.tensor_scalar(up[:, 0:6], inv2[:, 0:6], 16.0, None, ALU.mult)
        v.tensor_scalar(up[:, 6:6 + B], inv2[:, 6:6 + B], 64.0, None, ALU.mult)
        v.tensor_scalar(unscale[:, 6:6 + B], pow2[:, 6:6 + B], 1.0 / 64, None, ALU.mult)
        link(v.tensor_scalar(unscale[:, 0:6], pow2[:, 0:6], 1.0 / 16, None, ALU.mult))
        v.tensor_tensor(unscale2[:, :], unscale[:, 0:6], unscale[:, 0:6], ALU.mult)
        link(v.tensor_scalar(unscale[:, 6:6 + B], unscale[:, 6:6 + B], unscale[:, 0:1], None, ALU.mult))
        link(v.tensor_scalar(w0h[:, :], wn[0][:, :], up[:, 0:1], None, ALU.mult))
        link(v.scalar_tensor_tensor(out=w0l[:, :], in0=wn[0][:, :], scalar=up[:, 0:1], in1=w0h[:, :], op0=ALU.mult, op1=ALU.subtract))
        for part, t in ((0, w0h), (1, w0l)):
            for s in range(2):
                v.tensor_copy(buf(w0pad16, C, [[TK + 4 * S0, CH], [4, K0]], off=2 * part + s),
                              buf(t, C, [[0, CH], [1, K0]]))
        v.tensor_copy(buf(w0pad, C, [[CW + S0, CH], [1, K0]]), buf(y[1], C, [[0, CH], [1, K0]])).then_inc(w_split, 1)

        def split_x(b):
            link(v.tensor_scalar(x16[:, b, :, 0], xs[:, b, :], up[0:P, 6 + b:7 + b], None, ALU.mult))
            link(v.scalar_tensor_tensor(out=x16[:, b, :, 1], in0=xs[:, b, :], scalar=up[0:P, 6 + b:7 + b], in1=x16[:, b, :, 0],
                                        op0=ALU.mult, op1=ALU.subtract))
            v.tensor_copy(x16[:, b, :, 2:4].bitcast(I32), x16[:, b, :, 0:2].bitcast(I32)).then_inc(x_split, 1)

        def split_w(n):
            w_n = C * TAPS[n]
            h, l = wh[n % 2], wl[n % 2]
            if n > 2:
                v.wait_ge(w_turned, n)
            link(v.tensor_scalar(h[:, 0:w_n], wn[n][:, :], up[:, n:n + 1], None, ALU.mult))
            v.scalar_tensor_tensor(out=l[:, 0:w_n], in0=wn[n][:, :], scalar=up[:, n:n + 1], in1=h[:, 0:w_n],
                                   op0=ALU.mult, op1=ALU.subtract).then_inc(w_split, 1)

        split_x(0)
        for b in range(B):
            v.tensor_reduce(xsum[:, b, :], buf(y[2], P, [[1, CW], [CS, NCH]], off=b * XW), AX_X, ALU.add).then_inc(x_summed, 1)
        v.wait_ge(g_done, 1)
        v.tensor_copy(gram[:, :, :], p_t[0:CW, 0:B * CW].rearrange("p (b s) -> p b s", b=B)).then_inc(g_kept, 1)
        split_w(1)
        split_w(2)
        for b in range(1, B):
            split_x(b)
        v.wait_ge(u_done, 1)
        for b in range(B):
            last = v.tensor_tensor_reduce(out=energy[:, b, :], in0=w0pad[:, :, :].rearrange("p i s -> p (i s)"), in1=p_y[:, 0, b * CH * CW:(b + 1) * CH * CW],
                                   scale=1.0, scalar=0.0, op0=ALU.mult, op1=ALU.add, accum_out=acc[:, 0, b:b + 1])
        link(last)
        v.wait_ge(u_done, 2)
        v.wait_ge(loaded_xl, 16)
        for b in range(B):
            v.tensor_tensor_reduce(out=energy[:, b, :].rearrange("p (i s) -> p i s", i=CH), in0=w0pad[:, :, :],
                                   in1=bass.AP(p_y, 512 + b * CW, [[1024, C], [0, CH], [1, CW]]),
                                   scale=1.0, scalar=0.0, op0=ALU.mult, op1=ALU.add, accum_out=acc[:, 1, b:b + 1])
            last = v.tensor_tensor_reduce(out=xlast[:, b, :], in0=wn[0][:, 0:S0], in1=xlast[:, b, :],
                                          scale=1.0, scalar=0.0, op0=ALU.mult, op1=ALU.add, accum_out=acc[:, 2, b:b + 1])
        link(last)
        link(v.tensor_tensor(acc[:, 3, :], acc[:, 2, :], acc[:, 2, :], ALU.mult))
        v.tensor_tensor(acc[:, 0, :], acc[:, 0, :], acc[:, 3, :], ALU.subtract)
        link(v.tensor_tensor(acc[:, 1, :], acc[:, 1, :], acc[:, 2, :], ALU.subtract))
        v.wait_ge(loaded_p, 16 * 18)
        link(v.tensor_scalar(acc[:, 2, :], acc[:, 1, :], 1.0 / VALID[0], None, ALU.mult))
        link(v.tensor_tensor(acc[:, 3, :], acc[:, 2, :], acc[:, 2, :], ALU.mult))
        link(v.scalar_tensor_tensor(out=acc[:, 3, :], in0=acc[:, 0, :], scalar=1.0 / VALID[0], in1=acc[:, 3, :], op0=ALU.mult, op1=ALU.subtract))
        v.tensor_scalar(stat0[:, :, 0], acc[:, 2, :], pars[:, 0, 0:1], None, ALU.add)
        link(v.tensor_scalar(acc[:, 2, :], acc[:, 2, :], pars[:, 0, 0:1], None, ALU.add))
        link(v.tensor_tensor(acc[:, 2, :], acc[:, 2, :], acc[:, 2, :], ALU.mult))
        v.tensor_tensor(stat0[:, :, 1], acc[:, 2, :], acc[:, 3, :], ALU.add).then_inc(gn_stat, 1)

        def coefs(n, cnt, layer, group, out_scale, out_bias, un):
            a, t, m = gs[:, 0:cnt], gs[:, 4:4 + cnt], gs[:, 8:8 + 2 * cnt]
            mean, square = m[:, 0:2 * cnt:2], m[:, 1:2 * cnt:2]
            v.wait_ge(gn_group, n)
            link(v.tensor_copy(m, group))
            link(v.tensor_tensor(t, mean, mean, ALU.mult))
            link(v.tensor_tensor(t, square, t, ALU.subtract))
            v.tensor_scalar(a, t, 0.0, EPS, ALU.max, ALU.add).then_inc(gn_var, 1)
            v.wait_ge(gn_pow, n)
            link(v.tensor_scalar(a, a, pars[:, layer, 1:2], None, ALU.mult))
            link(v.tensor_tensor(t, mean, a, ALU.mult))
            link(v.tensor_scalar(t, t, -1.0, pars[:, layer, 2:3], ALU.mult, ALU.add))
            v.tensor_tensor(out_scale, a, un, ALU.mult)
            v.scalar_tensor_tensor(out=out_bias, in0=a, scalar=pars[:, layer, 0:1], in1=t, op0=ALU.mult, op1=ALU.add).then_inc(gn_coef, 1)
            v.wait_ge(gn_coef, n)

        for n in range(3, 6):
            split_w(n)
        coefs(1, B, 0, p_y[:, 1, 0:2 * B], coef0[:, :, 0], coef0[:, :, 1], unscale[:, 6:6 + B])

        def keep_chunks(k, b):
            v.wait_ge(t_mm, b * NCH // 2 + k + 1)
            v.tensor_copy(buf(x0T, TK, [[1, 2 * P]], off=(b % 2) * NCH * P + k * 2 * P), p_t[0:TK, 0:2 * P]).then_inc(t_kept, 1)

        def low(u):
            v.wait_ge(hi_done, u.g + 1)
            v.wait_ge(gelu_done, u.g + 1)
            nc.vector.tensor_tensor(ring_rows(u, 1, 2, first_row(u)), split_ap(geluf, u),
                                    ring_rows(u, 0, 2, first_row(u)), ALU.subtract).then_inc(lo_done, 1)
            if u.head and u.layer != 5:
                v.wait_ge(lo_done, u.g + 1)
                if u.all_before:
                    v.wait_ge(conv_done, u.all_before)
                src = ring[u.stream]
                nc.vector.tensor_copy(wrap[u.stream][:, :, :], buf(src, C, [[PL, 2], [1, P]], off=u.par * 2 * PL + 2 * P))
                nc.vector.tensor_copy(buf(src, C, [[PL, 2], [1, 2 * P]], off=(1 - u.par) * 2 * PL),
                                      buf(src, C, [[PL, 2], [1, 2 * P]], off=u.par * 2 * PL + UR * P)).then_inc(halo_done, 1)

        for u in lead:
            low(u)

        def work(t, before, after):
            if t.stream == "A" and not t.final and t.batch + 1 < B:
                keep_chunks(t.j, t.batch + 1)
            for u in before:
                low(u)
            for m in t.tails:
                v.wait_ge(conv_done, m.c + 1)
                v.wait_ge(lo_done, m.nxt_g)
                src = ring[m.stream]
                nc.vector.tensor_copy(buf(src, C, [[PL, 2], [1, 2 * P]], off=m.par * 2 * PL),
                                      buf(src, C, [[PL, 2], [1, 2 * P]], off=(1 - m.par) * 2 * PL + UR * P)).then_inc(halo_done, 1)
            if t.by == "dve":
                v.wait_ge(conv_done, t.c + 1)
                v.wait_ge(gelu_done, t.read)
                nc.vector.tensor_copy(y_out(t), p_y[:, t.bank, 0:t.size]).then_inc(evac_done["dve"], 1)
            v.wait_ge(evac_done[t.by], t.taken + 1)
            skip = P if (t.head and t.layer != 5) else 0
            size = t.size - (1 if t.last_of_layer else 0)
            stats = nc.vector.bn_stats(bst[t.stream][:, bass.ds(t.j * 6, 6)], y[t.layer][:, bass.ds(t.j * OC + skip, size - skip)])
            if t.gn is not None:
                n = t.layer
                link(stats)
                link(v.bn_aggr(mv[:, :], bst[t.stream][:, 0:6 * (t.n_stats)]))
                link(v.tensor_scalar(gs[:, 0:1], mv[:, 0:1], unscale[:, n:n + 1], pars[:, n, 0:1], ALU.mult, ALU.add))
                link(v.tensor_tensor(gs[:, 4:5], gs[:, 0:1], gs[:, 0:1], ALU.mult))
                v.scalar_tensor_tensor(out=gs[:, 1:2], in0=mv[:, 1:2], scalar=unscale2[:, n:n + 1], in1=gs[:, 4:5],
                                       op0=ALU.mult, op1=ALU.add).then_inc(gn_stat, 1)
                coefs(t.gn + 2, 1, n, p_m[:, 0:2], coef[:, n, 0:1], coef[:, n, 1:2], unscale[:, n:n + 1])
            for u in after:
                low(u)

        take(v, slots, loops, work)

    @block.tensor
    def _(pe):
        pe.wait_ge(made_ident, 3)
        for b in range(B):
            pe.wait_ge(loaded_x[b // 2], 16 * 3)
            for c in range(NCH):
                xc = xs[:, b, c * CS:c * CS + CW]
                last = pe.matmul(p_t[0:CW, b * CW:(b + 1) * CW], xc, xc, start=(c == 0), stop=(c == NCH - 1))
        last.then_inc(g_done, 1)
        pe.wait_ge(w_split, 1)
        for i in range(CH):
            last = pe.transpose(p_w16[0][0:TK, i * C:(i + 1) * C], w0pad16[:, i, :], ident16[:, :])
        last.then_inc(w_turned, 1)
        for i in range(CH):
            last = pe.transpose(p_l0[0:CW, 2, i * C:(i + 1) * C], w0pad[:, i, :], ident[:, :])
        last.then_inc(w_turned, 1)

        def turn_chunks(k, b, into):
            for c in range(2):
                last = pe.matmul(into[0:TK, c * P:(c + 1) * P],
                                 buf(x16, P, [[1, TK]], off=b * 4 * XW + k * (8 * CS) + c * 4 * CS),
                                 ident16[0:P, 0:P], start=True, stop=True)
            last.then_inc(t_mm, 1)

        pe.wait_ge(x_split, 1)
        turn_chunks(0, 0, p_l0[:, 0, :])
        turn_chunks(1, 0, p_l0[:, 1, :])

        def turn_first(k0, k1):
            with pe.Fori(k0, k1) as k:
                for half in range(2):
                    pe.wait_ge(t_kept, k * 2 + (half - 1))
                    turn_chunks(k * 2 + half, 0, p_l0[:, half, :])

        turn_first(1, NCH // 6)
        pe.wait_ge(g_kept, 1)
        pe.wait_ge(w_kept, 2)
        for b in range(B):
            for i in range(CH):
                at = (b * CH + i) * CW
                last = pe.matmul(p_y[:, 0, at:at + CW], w0T[:, i, :], gram[:, b, :], start=True, stop=True)
        last.then_inc(u_done, 1)
        pe.wait_ge(x_summed, B)
        pe.matmul(p_y[:, 1, 0:B * CW], ones[0:P, :], xsum[:, :, :].rearrange("p b s -> p (b s)"), start=True, stop=True).then_inc(u_done, 1)

        def turn_weights(n):
            pe.wait_ge(w_split, n + 1)
            pe.wait_ge(w_kept, n)
            for s, t in enumerate((wh[n % 2], wl[n % 2])):
                for k in range(TAPS[n]):
                    at = (s * TAPS[n] + k) * C
                    last = pe.transpose(p_w16[(n + 1) % 2][:, at:at + C], t[:, k:TAPS[n] * C:TAPS[n]], ident16[:, :])
            last.then_inc(w_turned, 1)

        turn_weights(1)
        turn_weights(2)
        turn_first(NCH // 6, NCH // 4)
        pe.wait_ge(gn_stat, 1)
        pe.wait_ge(made_quad, 2)
        pe.matmul(p_y[:, 1, 0:2 * B], quad[:, :], stat0[:, :, :].rearrange("p b s -> p (b s)"), start=True, stop=True).then_inc(gn_group, 1)
        for n in range(3, 6):
            turn_weights(n)
        pe.wait_ge(w_kept, 7)
        pe.wait_ge(x_split, B)

        def first(u):
            pe.wait_ge(t_kept, NCH // 2 if u in lead else u.batch * NCH // 2 + u.j + 1)
            if not is_zero(u.l0_wait):
                pe.wait_ge(gelu_done, u.l0_wait)
            for i in range(CH):
                last = pe.matmul(p_l0[:, 2 * u.par + i // 2, (i % 2) * 2 * P:(i % 2 + 1) * 2 * P], w0T16[:, i, :],
                                 buf(x0T, TK, [[1, 2 * P]], off=(u.batch % 2) * NCH * P + u.j * 2 * P), start=True, stop=True)
            last.then_inc(l0_done, 1)

        for u in lead:
            first(u)

        def conv(t):
            n = t.layer
            if not t.final:
                pe.wait_ge(lo_done, t.g + 1)
            if not is_zero(t.need_halo):
                pe.wait_ge(halo_done, t.need_halo)
            if not is_low(t.c, 2):
                pe.wait_ge(evac_done[t.free_by], t.free)
            out = p_y[:, t.bank, 0:t.size]
            if t.final:
                src, q = ring[t.stream], (t.j - 1) % 2
                ops = []
                for k in range(3):
                    for wp, xp in ((0, 0), (0, 1), (1, 0)):
                        if k < 2:
                            rhs, o = buf(src, C, [[1, P]], off=(q * 2 + xp) * PL + (UR + k) * P), p_y[:, t.bank, 0:P]
                        else:
                            rhs, o = wrap[t.stream][:, xp, 1:P], p_y[:, t.bank, 0:P - 1]
                        ops.append((o, wT[n][:, wp, k, :], rhs))
            else:
                half = t.rows // 2
                base = 2 if n == 5 else 0
                ops = [(out, wT[n][:, wp, k, :], ring_rows(t, xp, base + k, [[2 * P, half], [1, P]]))
                       for k in range(TAPS[n]) for wp, xp in ((0, 0), (0, 1), (1, 0))]
            for m, (o, lhs, rhs) in enumerate(ops):
                last = pe.matmul(o, lhs, rhs, start=(m == 0), stop=(m == len(ops) - 1))
            last.then_inc(conv_done, 1)

        def group(t):
            pe.wait_ge(gn_stat, t.gn + 2)
            pe.matmul(p_m[:, 0:2], quad[:, :], gs[:, 0:2], start=True, stop=True).then_inc(gn_group, 1)

        pending = []

        def work(t, before, after):
            for u in before:
                if u.stream == "A":
                    first(u)
            if pending and needs(t, pending[0]):
                group(pending.pop())
            if t.stream == "A" and not t.final and t.batch + 1 < B:
                pe.wait_ge(t_kept, (t.batch + 1) * (NCH // 2) + t.j)
                turn_chunks(t.j, t.batch + 1, p_t)
            conv(t)
            if pending:
                group(pending.pop())
            if t.gn is not None:
                pending.append(t)
            for u in after:
                if u.stream == "A":
                    first(u)

        take(pe, slots, loops, work)
        if pending:
            group(pending.pop())

    ctx.close()
    with ExitStack() as ctx:
        transformer(nc, ctx, h5, kept, t_in, out)
    outer.close()

class Tick:

    def __init__(self, sem, per):
        self.sem, self.per = sem, per

    def wait(self, eng, b, n):
        eng.wait_ge(self.sem, b * self.per + n)


def transformer(nc, ctx, h5, kept, w, out):
    sb = lambda name, shape, dt=F32: ctx.enter_context(nc.sbuf_tensor(name, shape, dt))
    sem = lambda name: ctx.enter_context(nc.semaphore(name))
    bank = ctx.enter_context(nc.psum_tensor("bank", [C, 8, 512], F32))

    pwn = [sb("pwn0", [C, C]), sb("pwn1", [E1, C])]
    pwT = sb("pwT", [C, E])
    wqkv = [sb("wqkv0", [C, 3 * E]), sb("wqkv1", [E1, 3 * E])]
    wq16 = [sb("wq16a", [C, 2, 3 * E], F16), sb("wq16b", [E1, 2, 3 * E], F16)]
    most = sb("most", [C, 2])
    scales = sb("scales", [C, 2 + HT])
    pow2 = sb("pow2w", [C, 2 + HT])
    up = sb("upw", [C, 2 + HT])
    unscale = sb("unscalew", [C, 2 + HT])
    wpr = [sb("wpr0", [C, E]), sb("wpr1", [E1, E])]
    fcn = sb("fcn", [C, HT, E])
    w0T = [sb("w0Ta", [C, 2, HID], F16), sb("w0Tb", [E1, 2, HID], F16)]
    w1all = sb("w1all", [C, 2 * HID])
    w1n = [w1all[:, 0:HID], w1all[0:E1, HID:2 * HID]]
    w1T = sb("w1T", [C, HT, E])
    rows = sb("rows", [P, 3, E])
    bfc = sb("bfc", [C, HT])
    alpha = sb("alpha", [C, 6])
    hnum = sb("hnum", [C, HT])
    hnum_i = sb("hnum_i", [C, HT], I32)
    mix = sb("mix", [C, 3, HT])
    tmp = sb("tmp", [C, 3, HT])
    sums = sb("sums", [C, 4])
    pmn = sb("pmn", [M, HD])
    pmT = sb("pmT", [HD, M])
    spread = sb("spread", [HD, 8, HD])
    own = sb("own", [C, 8])
    feat = [sb("feat0", [C, 8, M]), sb("feat1", [E1, 4, M])]
    diag = [sb("diag0", [C, HEADS]), sb("diag1", [E1, HEADS])]
    kvmask = sb("kvmask", [2 * M, GR, 2 * VW])
    ident = sb("identt", [C, C])
    mhalf = sb("mhalft", [P, R])
    feps = sb("feps", [C, 1])
    hcur = sb("hcur", [C, R * P])
    res = sb("res", [P, B, R, E])
    xn = sb("xn", [P, R, E])
    xc = [sb("xc0", [C, 2, R * P], F16), sb("xc1", [E1, 2, R * P], F16)]
    xt = [sb("xt0", [C, B, 2, R * P], F16), sb("xt1", [E1, B, 2, R * P], F16)]
    ft = [sb("ft0", [C, R * P]), sb("ft1", [E1, R * P])]
    sq = [sb("sq0", [C, R * P]), sb("sq1", [E1, R * P])]
    dk = sb("dk", [P, B, R, FE])
    vals = sb("vals", [P, B * R * HEADS, VW])
    kmax = sb("kmax", [C, B, 2 * R])
    kmin = sb("kmin", [C, 2])
    dg = sb("dg", [P, 2, HEADS])
    mq = sb("mq", [P, 2, HEADS])
    st = sb("st", [P, R, 6])
    mv = sb("mvt", [P, R, 2])
    rs = sb("rs", [P, R])
    hid = sb("hid", [C, HT, HALF])
    ek = kept[0:P, :].rearrange("p (r f) -> p r f", f=FE)
    dq = sb("dq", [P, 2, FE])
    q1T = w1all[0:2 * M, 0:2 * GR * P].rearrange("p (a g t) -> p a g t", a=2, g=GR)
    kvm = sb("kvm", [2 * M, GR, 2 * VW])
    zr = sb("zr", [P, 2, HEADS])
    at = sb("at", [P, 2, E])
    prb = sb("prb", [P, 2, E])
    atT = [sb("atT0", [C, 2, P]), sb("atT1", [E1, 2, P])]
    osb = fcn[0:P, :, :]

    loads = [sem(f"load{n}") for n in range(12)]
    made = sem("made")
    weights_turned, weights_kept = sem("weights_turned"), sem("weights_kept")
    dve_steps = sem("dve_steps")
    wq_max, wq_all, wq_high, w0_high, scaled = sem("wq_max"), sem("wq_all"), sem("wq_high"), sem("w0_high"), sem("scaled")
    ready = sem("ready")
    passed = sem("passed")
    gmax, gmax_all, gmax_neg = sem("gmax"), sem("gmax_all"), sem("gmax_neg")
    T = lambda name, per: Tick(sem(name), per)
    result_copied, embed_mm, norm1_var, norm1_pow = T("result_copied", 1), T("embed_mm", 3), T("norm1_var", 1), T("norm1_pow", 1)
    normed1 = T("normed1", 6)
    turned1_mm, turned1_high, turned1_low, turned1_saved = T("turned1_mm", 2), T("turned1_high", 4), T("turned1_low", 4), T("turned1_saved", 1)
    key_mm, key_kept, value_mm, value_kept = T("key_mm", 4), T("key_kept", 8), T("value_mm", 3), T("value_kept", 3)
    key_feature_mm, key_feature_kept, key_diag_kept = T("key_feature_mm", 6), T("key_feature_kept", 6), T("key_diag_kept", 6)
    key_exp, key_feature_done, kv_mm, kv_kept = T("key_exp", 6), T("key_feature_done", 6), T("kv_mm", 1), T("kv_kept", 1)
    query_mm, query_kept, query_feature_mm, query_feature_kept = T("query_mm", 4), T("query_kept", 8), T("query_feature_mm", 6), T("query_feature_kept", 6)
    query_exp, query_turned_mm, query_turned_kept = T("query_exp", 6), T("query_turned_mm", 6), T("query_turned_kept", 12)
    mixed_mm, mixed_kept, mixed_turned_mm, mixed_turned_kept = T("mixed_mm", 6), T("mixed_kept", 6), T("mixed_turned_mm", 6), T("mixed_turned_kept", 12)
    attn_out_mm, attn_out_kept = T("attn_out_mm", 6), T("attn_out_kept", 6)
    norm2_var, norm2_pow, normed2, turned2_mm = T("norm2_var", 1), T("norm2_pow", 1), T("normed2", 6), T("turned2_mm", 2)
    turned2_high, turned2_low = T("turned2_high", 4), T("turned2_low", 4)
    hidden_mm, hidden_kept, ffn_out_mm, ffn_out_done = T("hidden_mm", 12), T("hidden_kept", 12), T("ffn_out_mm", 6), T("ffn_out_done", 6)
    stored = T("stored", 32)

    block = ctx.enter_context(nc.Block())

    KEY_BANKS, QUERY_BANKS, FORWARD_BANKS = ((2, 4), (3, 5)), ((0, 1), (4, 5)), (2, 3)
    W1_BANKS = (2, 3, 6)
    TURN_BANKS, VALUE_BANKS, EMBED_BANKS = (2, 3), (0, 1, 0), (0, 1, 6)
    FEATURE_BANKS = ((6, 7), (4, 5))
    part = lambda what, half, *n: [(what, half, t) for t in n]
    BEFORE = part("turn", 0, 0)
    FILL = [part("hidden", 0, 0, 1), part("hidden", 0, 2, 3), part("hidden", 0, 4, 5), part("out", 0, 0, 1, 2), part("turn", 1, 0), part("hidden", 1, 0, 1), part("hidden", 1, 2, 3), part("hidden", 1, 4, 5), part("out", 1, 0, 1, 2), []]

    def tile_(t, r):
        return t[:, r * P:(r + 1) * P]

    ops = {"pw": (0, 2), "rows": (1, 3), "qkv": (2, 2), "pr": (3, 2), "fc": (4, 1), "w1": (5, 2), "bfc": (6, 1), "alpha": (7, 2), "pm": (8, 1)}

    def loaded(eng, what):
        n, times = ops[what]
        eng.wait_ge(loads[n], 16 * times)

    @block.sync
    def _(sp):
        def load(what, dst, src, slow=False):
            sp.dma_start(dst, src, allow_slow_non_contiguous=slow).then_inc(loads[ops[what][0]], 16)

        load("pw", pwn[0][:, :], w["tok_pw"][0:C, :])
        load("pw", pwn[1][:, :], w["tok_pw"][C:E, :])
        load("pm", pmn[:, :], w["attn_proj_mat"])
        for n, name in enumerate(("tok_pb", "attn_b_proj", "ffn_b_proj")):
            load("rows", rows[:, n, :], bass.AP(w[name].tensor, 0, [[0, P], [1, E]]))
        for n in range(2):
            load("qkv", wqkv[n][:, :], w["attn_W_qkv"][n * C:n * C + (C, E1)[n], :])
            load("pr", wpr[n][:, :], w["attn_W_proj"][n * C:n * C + (C, E1)[n], :])
            load("w1", w1n[n][:, :], w["ffn_w_proj"][n * C:n * C + (C, E1)[n], :])
        load("fc", fcn[:, :, :], w["ffn_w_fc"].rearrange("(t p) e -> p t e", p=C))
        load("bfc", bfc[:, :], w["ffn_b_fc"].rearrange("(t p) -> p t", p=C), slow=True)
        for n, name in enumerate(("ffn_alpha_e", "ffn_alpha_r")):
            load("alpha", alpha[:, 3 * n:3 * n + 3], bass.AP(w[name].tensor, 0, [[0, C], [1, 3]]))
        sp.sem_inc(stored.sem, 32)
        with sp.Fori(0, B) as b:
            ffn_out_done.wait(sp, b, R)
            row = b * (E * (R * P - 1))
            sp.dma_start(bass.AP(out.tensor, row, [[R * E, P - 1], [1, R * E]]), osb[0:P - 1, :, :].rearrange("p r e -> p (r e)")).then_inc(stored.sem, 16)
            sp.dma_start(bass.AP(out.tensor, row + (P - 1) * R * E, [[R * E, 1], [1, (R - 1) * E]]),
                         osb[P - 1:P, 0:R - 1, :].rearrange("p r e -> p (r e)")).then_inc(stored.sem, 16)
        sp.wait_ge(stored.sem, 32 * B + 32)

    @block.gpsimd
    def _(pool):
        def step(ins, n):
            ins.then_inc(made, 1)
            pool.wait_ge(made, n)

        pool.memset(ident[:, :], 0.0).then_inc(made, 1)
        pool.memset(spread[:, :, :], 0.0).then_inc(made, 1)
        pool.memset(own[:, :], 1.0).then_inc(made, 1)
        step(pool.memset(kvmask[:, :, :], 1.0), 4)
        pool.iota(hnum_i[:, :], pattern=[[C, HT]], base=0, channel_multiplier=1).then_inc(made, 1)
        pool.affine_select(out=ident[:, :], in_=ident[:, :], compare_op=ALU.not_equal, fill=1.0, base=0,
                           pattern=[[-1, C]], channel_multiplier=1).then_inc(made, 1)
        pool.affine_select(out=spread[:, :, :], in_=spread[:, :, :], compare_op=ALU.not_equal, fill=1.0, base=0,
                           pattern=[[0, 8], [-1, HD]], channel_multiplier=1).then_inc(made, 1)
        pool.affine_select(out=own[:, :], in_=own[:, :], compare_op=ALU.is_ge, fill=0.0, base=0,
                           pattern=[[-HD, 8]], channel_multiplier=1).then_inc(made, 1)
        m = kvmask[:, :, :].rearrange("p g (a v) -> p g a v", a=2)
        step(pool.affine_select(out=m, in_=m, compare_op=ALU.is_ge, fill=0.0, base=0,
                                pattern=[[0, GR], [-M, 2], [0, VW]], channel_multiplier=1), 9)
        pool.affine_select(out=own[:, :], in_=own[:, :], compare_op=ALU.is_ge, fill=0.0, base=HD - 1,
                           pattern=[[HD, 8]], channel_multiplier=-1).then_inc(made, 1)
        pool.affine_select(out=m, in_=m, compare_op=ALU.is_ge, fill=0.0, base=M - 1,
                           pattern=[[0, GR], [M, 2], [0, VW]], channel_multiplier=-1).then_inc(made, 1)
        pool.memset(mhalf[:, :], -0.5).then_inc(made, 1)
        pool.memset(vals[:, :, :], 1.0).then_inc(made, 1)
        pool.memset(kmax[:, :, :], -3e38).then_inc(made, 1)
        pool.memset(feps[:, :], FEPS * RATIO).then_inc(made, 1)
        pool.wait_ge(wq_max, 1)
        pool.partition_all_reduce(scales[:, 0:2], most[:, :], C, bass.bass_isa.ReduceOp.max).then_inc(wq_all, 1)
        with pool.Fori(0, B) as b:
            norm1_var.wait(pool, b, 1)
            pool.tensor_tensor(rs[:, :], rs[:, :], mhalf[:, :], ALU.pow).then_inc(norm1_pow.sem, 1)
        pool.wait_ge(gmax, 1)
        pool.partition_all_reduce(kmin[:, 1:2], kmin[:, 0:1], C, bass.bass_isa.ReduceOp.max).then_inc(gmax_all, 1)
        with pool.Fori(0, B) as b:
            norm2_var.wait(pool, b, 1)
            pool.tensor_tensor(rs[:, :], rs[:, :], mhalf[:, :], ALU.pow).then_inc(norm2_pow.sem, 1)

    @block.scalar
    def _(act):
        S = nc.scalar

        def turned(b, mm, kept, half, banks):
            mm.wait(act, b, half + 1)
            for n, rowsn in enumerate((C, E1)):
                S.copy(xc[n][:, 0, half * HALF:(half + 1) * HALF], bank[0:rowsn, banks[n], 0:HALF]).then_inc(kept.sem, 1)

        def project(b, mm, kept, banks):
            for half in range(2):
                for n, rowsn in enumerate((C, E1)):
                    mm.wait(act, b, 2 * half + n + 1)
                    src = bank[0:rowsn, banks[half][n], 0:HALF]
                    S.activation(ft[n][:, half * HALF:(half + 1) * HALF], src, ACT.Identity, scale=unscale[0:rowsn, 0:1]).then_inc(kept.sem, 1)
                    S.activation(sq[n][:, half * HALF:(half + 1) * HALF], src, ACT.Square, scale=unscale[0:rowsn, 0:1]).then_inc(kept.sem, 1)

        def keys(b, after):
            turned1_saved.wait(act, b, 1)
            for half in range(2):
                turned(b, turned1_mm, turned1_high, half, TURN_BANKS)
            project(b, key_mm, key_kept, KEY_BANKS)
            for q in range(R // 2):
                value_mm.wait(act, b, q + 1)
                S.activation(bass.AP(vals, b * (R * HEADS * VW) + q * 2 * HEADS * VW, [[B * R * HEADS * VW, P], [VW, 2 * HEADS], [1, HD]]),
                             bank[0:P, VALUE_BANKS[q], 0:2 * E].rearrange("p (h d) -> p h d", d=HD), ACT.Identity, scale=unscale[0:P, 0:1]).then_inc(value_kept.sem, 1)
            turned1_low.wait(act, b, 4)
            for n in range(2):
                last = S.copy(xt[n][:, b, :, :].rearrange("p s t -> p (s t)"), xc[n][:, :, :].rearrange("p s t -> p (s t)"))
            last.then_inc(turned1_saved.sem, 1)
            if after is not None:
                embed_mm.wait(act, after - 1, 3)
                S.copy(hcur[:, :], h5[:, after, :]).then_inc(result_copied.sem, 1)

        act.sem_inc(turned1_saved.sem, 1)
        S.copy(hcur[:, :], h5[:, 0, :]).then_inc(result_copied.sem, 1)
        act.wait_ge(scaled, 1)
        for n, rowsn in enumerate((C, E1)):
            S.activation(wq16[n][:, 0, :], wqkv[n][:, :], ACT.Identity, scale=up[0:rowsn, 0:1]).then_inc(wq_high, 1)
        embed_mm.wait(act, 0, 3)
        S.copy(hcur[:, :], h5[:, 1, :]).then_inc(result_copied.sem, 1)
        with act.Fori(0, B - 2) as b:
            keys(b, b + 2)
        keys(B - 2, None)
        keys(B - 1, None)
        act.wait_ge(gmax_neg, 1)

        def attend(b, first, f):
            project(b, query_mm, query_kept, QUERY_BANKS)
            forward(f, BEFORE)
            for r in range(R):
                S.activation(ek[:, r, :], dk[:, b, r, :], ACT.Exp, bias=kmin[0:P, 0:1]).then_inc(key_exp.sem, 1)
            if f is None:
                act.wait_ge(weights_turned, 3)
                for n, rowsn in enumerate((C, E1)):
                    S.copy(w0T[n][:, 0, 0:512], bank[0:rowsn, (2, 6)[n], :]).then_inc(w0_high, 1)
                    S.copy(w0T[n][:, 0, 512:768], bank[0:rowsn, (3, 7)[n], 0:256]).then_inc(w0_high, 1)
            for s in range(R + 4):
                if s < R:
                    r = s
                    query_feature_kept.wait(act, b, r + 1)
                    S.activation(dq[:, r % 2, :], dq[:, r % 2, :], ACT.Exp).then_inc(query_exp.sem, 1)
                if 0 <= s - 1 < R:
                    r = s - 1
                    query_turned_mm.wait(act, b, r + 1)
                    if r >= 2:
                        mixed_mm.wait(act, b, r - 1)
                    S.activation(q1T[:, r % 2, 0:4, :], bank[0:2 * M, 4, 0:4 * P].rearrange("p (g t) -> p g t", g=4), ACT.Identity,
                                 bias=feps[0:2 * M, :], scale=RATIO).then_inc(query_turned_kept.sem, 1)
                    S.activation(q1T[:, r % 2, 4:6, :], bank[0:2 * M, 5, 0:2 * P].rearrange("p (g t) -> p g t", g=2), ACT.Identity,
                                 bias=feps[0:2 * M, :], scale=RATIO).then_inc(query_turned_kept.sem, 1)
                if 0 <= s - 3 < R:
                    r = s - 3
                    mixed_turned_mm.wait(act, b, r + 1)
                    if r >= 2 or not first:
                        attn_out_mm.wait(act, b, r - 1)
                    S.copy(atT[0][:, r % 2, :], bank[0:C, 6, 0:P]).then_inc(mixed_turned_kept.sem, 1)
                    S.copy(atT[1][:, r % 2, :], bank[0:E1, 6, 128:128 + P]).then_inc(mixed_turned_kept.sem, 1)
                forward(f, FILL[s])

        def forward(f, work):
            if f is None:
                return
            for what, half, t in work:
                if what == "turn":
                    turned(f, turned2_mm, turned2_high, half, FORWARD_BANKS)
                if what == "hidden":
                    if half == 1 and t == 0:
                        ffn_out_mm.wait(act, f, 3)
                    if half == 0 and t == 0 and not is_zero(f):
                        ffn_out_mm.wait(act, f, 0)
                    hidden_mm.wait(act, f, HT * half + t + 1)
                    S.activation(hid[:, t, :], bank[:, FORWARD_BANKS[t % 2], 0:HALF], GELU, bias=bfc[:, t:t + 1], scale=unscale[:, 2 + t:3 + t]).then_inc(hidden_kept.sem, 1)

        attend(0, True, None)
        with act.Fori(0, B - 1) as f:
            attend(f + 1, False, f)
        for work in [BEFORE] + FILL:
            forward(B - 1, work)

    @block.vector
    def _(v):
        chain = [0]
        body = [None, 0, 0]

        def link(ins):
            ins.then_inc(dve_steps, 1)
            if body[0] is None:
                chain[0] += 1
                v.wait_ge(dve_steps, chain[0])
            else:
                body[1] += 1
                v.wait_ge(dve_steps, body[0] * body[2] + (chain[0] + body[1]))

        link(v.memset(most[:, :], 0.0))
        loaded(v, "qkv")
        v.tensor_reduce(most[:, 0:1], wqkv[0][:, :], AX_X, ALU.max, apply_absolute_value=True)
        v.tensor_reduce(most[0:E1, 1:2], wqkv[1][:, :], AX_X, ALU.max, apply_absolute_value=True).then_inc(wq_max, 1)
        v.wait_ge(made, 15)
        v.wait_ge(weights_turned, 1)
        v.tensor_copy(pmT[:, :], bank[0:HD, 0, 0:M]).then_inc(weights_kept, 1)
        v.tensor_copy(pwT[:, :], bank[:, 1, 0:E]).then_inc(weights_kept, 1)
        v.wait_ge(weights_turned, 2)
        for n, (rn, hn) in enumerate(((C, 8), (E1, 4))):
            v.scalar_tensor_tensor(out=feat[n][:, :, :], in0=bass.AP(bank, 2 * 512, [[8 * 512, rn], [0, hn], [1, M]]), scalar=NORM,
                                   in1=bass.AP(own, 0, [[8, rn], [1, hn], [0, M]]), op0=ALU.mult, op1=ALU.mult)
        v.memset(diag[0][:, 8:12], 0.0)
        v.memset(diag[1][:, 0:8], 0.0)
        v.tensor_scalar(diag[0][:, 0:8], own[:, :], 0.5 * NORM * NORM, None, ALU.mult)
        v.tensor_scalar(diag[1][:, 8:12], own[0:E1, 0:4], 0.5 * NORM * NORM, None, ALU.mult)
        def factors(c0, c1):
            link(v.tensor_scalar(scales[:, c0:c1], scales[:, c0:c1], 1e-30, None, ALU.max))
            link(v.tensor_scalar(pow2[:, c0:c1].bitcast(I32), scales[:, c0:c1].bitcast(I32), 0x7F800000, None, ALU.bitwise_and))
            link(v.reciprocal(up[:, c0:c1], pow2[:, c0:c1]))
            link(v.tensor_scalar(up[:, c0:c1], up[:, c0:c1], 16.0, None, ALU.mult))
            v.tensor_scalar(unscale[:, c0:c1], pow2[:, c0:c1], 1.0 / 16, None, ALU.mult).then_inc(scaled, 1)

        def prepare_mix():
            loaded(v, "alpha")
            link(v.tensor_copy(hnum[:, :], hnum_i[:, :]))
            for i in range(3):
                for j in range(3):
                    link(v.tensor_scalar(tmp[:, j, :], hnum[:, :], float(RATIOS[j] * EMBEDS[i]), alpha[:, 3 + j:4 + j], ALU.is_lt, ALU.mult))
                link(v.tensor_tensor(tmp[:, 0, :], tmp[:, 0, :], tmp[:, 1, :], ALU.add))
                link(v.tensor_tensor(tmp[:, 0, :], tmp[:, 0, :], tmp[:, 2, :], ALU.add))
                link(v.tensor_scalar(mix[:, i, :], tmp[:, 0, :], alpha[:, i:i + 1], None, ALU.mult))
            link(v.tensor_tensor(mix[:, 1, :], mix[:, 1, :], mix[:, 2, :], ALU.add))
            link(v.tensor_tensor(mix[:, 0, :], mix[:, 0, :], mix[:, 1, :], ALU.add))
            link(v.tensor_tensor(sums[:, 3:4], alpha[:, 3:4], alpha[:, 4:5], ALU.add))
            link(v.tensor_tensor(sums[:, 3:4], sums[:, 3:4], alpha[:, 5:6], ALU.add))
            link(v.tensor_tensor(sums[:, 1:2], alpha[:, 1:2], alpha[:, 2:3], ALU.add))
            link(v.tensor_tensor(sums[:, 0:1], alpha[:, 0:1], sums[:, 1:2], ALU.add))
            v.tensor_scalar(sums[:, 0:2], sums[:, 0:2], sums[:, 3:4], None, ALU.mult)
            link(v.tensor_scalar(sums[:, 2:3], alpha[:, 2:3], sums[:, 3:4], None, ALU.mult))

        def prepare_forward():
            loaded(v, "bfc")
            loaded(v, "fc")
            for s, (e0, e1) in enumerate(SEG):
                v.tensor_scalar(rows[:, 2, e0:e1], rows[:, 2, e0:e1], sums[0:P, s:s + 1], None, ALU.mult)
                last = v.tensor_tensor(fcn[:, :, e0:e1], fcn[:, :, e0:e1], bass.AP(mix, s * HT, [[3 * HT, C], [1, HT], [0, e1 - e0]]), ALU.mult)
            link(last)
            link(v.tensor_reduce(scales[:, 2:2 + HT], fcn[:, :, :], AX_X, ALU.max, apply_absolute_value=True))
            factors(2, 2 + HT)
            v.tensor_tensor(fcn[:, :, :], fcn[:, :, :], bass.AP(up, 2, [[2 + HT, C], [1, HT], [0, E]]), ALU.mult).then_inc(weights_kept, 1)
            v.tensor_tensor(bfc[:, :], bfc[:, :], mix[:, 0, :], ALU.mult)
            v.wait_ge(weights_turned, 3)
            for n, rn in enumerate((C, E1)):
                v.wait_ge(w0_high, 2 * n + 2)
                v.tensor_tensor(w0T[n][:, 1, 0:512], bank[0:rn, (2, 6)[n], :], w0T[n][:, 0, 0:512], ALU.subtract)
                last = v.tensor_tensor(w0T[n][:, 1, 512:768], bank[0:rn, (3, 7)[n], 0:256], w0T[n][:, 0, 512:768], ALU.subtract)
            last.then_inc(weights_kept, 1)
            v.wait_ge(weights_turned, 4)
            for p in range(3):
                for s, (e0, e1) in enumerate(SEG):
                    last = v.tensor_tensor(w1T[:, 2 * p:2 * p + 2, e0:e1], bass.AP(bank, W1_BANKS[p] * 512 + e0, [[8 * 512, C], [E, 2], [1, e1 - e0]]),
                                           bass.AP(mix, s * HT + 2 * p, [[3 * HT, C], [1, 2], [0, e1 - e0]]), ALU.mult)
            last.then_inc(weights_kept, 1)


        def measured(src, var):
            v.sem_inc(passed, 1)
            for r in range(R):
                last = v.bn_stats(st[:, r, :], src(r))
            link(last)
            v.sem_inc(passed, 1)
            for r in range(R):
                last = v.bn_aggr(mv[:, r, :], st[:, r, :])
            link(last)
            v.tensor_scalar(rs[:, :], mv[:, :, 1], EPS, None, ALU.add).then_inc(var.sem, 1)

        def normed(b, src, powed, done):
            powed.wait(v, b, 1)
            for r in range(R):
                v.tensor_scalar(xn[:, r, :], src(r), mv[:, r, 0:1], rs[:, r:r + 1], ALU.subtract, ALU.mult).then_inc(done.sem, 1)

        def wide(k, n0, n):
            return bass.AP(k[0], k[1] + n0, [[2 * HEADS, P], [1, n], [0, M]])

        def lowered(b, high, low, half, banks):
            for n, rn in enumerate((C, E1)):
                high.wait(v, b, 2 * half + n + 1)
                at_ = slice(half * HALF, (half + 1) * HALF)
                v.tensor_tensor(xc[n][:, 1, at_], bank[0:rn, banks[n], 0:HALF], xc[n][:, 0, at_], ALU.subtract).then_inc(low.sem, 1)

        def embed(b):
            for q in range(R // 2):
                embed_mm.wait(v, b, q + 1)
                last = v.tensor_tensor(res[:, b, 2 * q:2 * q + 2, :], bank[0:P, EMBED_BANKS[q], 0:2 * E].rearrange("p (r e) -> p r e", r=2),
                                       bass.AP(rows, 0, [[3 * E, P], [0, 2], [1, E]]), ALU.add)
            link(last)
            measured(lambda r: res[:, b, r, :], norm1_var)

        def features(b, r):
            a, c = FEATURE_BANKS[r % 2]
            key_feature_mm.wait(v, b, r + 1)
            pn = P - 1 if r == R - 1 else P
            v.tensor_reduce(kmax[0:pn, b, 2 * r:2 * r + 1], bank[0:pn, a, 0:FA], AX_X, ALU.max)
            v.tensor_reduce(kmax[0:pn, b, 2 * r + 1:2 * r + 2], bank[0:pn, c, 0:FE - FA], AX_X, ALU.max)
            if r >= 2:
                key_feature_kept.wait(v, b, r - 1)
            elif not is_zero(b):
                key_feature_kept.wait(v, b, 0)
            v.tensor_copy(dg[:, r % 2, :], bank[0:P, a, FA:FA + HEADS]).then_inc(key_diag_kept.sem, 1)
            key_diag_kept.wait(v, b, r + 1)
            k = (dg, r % 2 * HEADS)
            v.tensor_tensor(dk[:, b, r, 0:FA].rearrange("p (h m) -> p h m", m=M), bank[0:P, a, 0:FA].rearrange("p (h m) -> p h m", m=M), wide(k, 0, 8), ALU.subtract)
            v.tensor_tensor(dk[:, b, r, FA:FE].rearrange("p (h m) -> p h m", m=M), bank[0:P, c, 0:FE - FA].rearrange("p (h m) -> p h m", m=M), wide(k, 8, 4), ALU.subtract).then_inc(key_feature_kept.sem, 1)

        def keys(b, following):
            if following is not None:
                embed(following)
            for r in range(R):
                features(b, r)
                if following is not None:
                    if r == 0:
                        normed(following, lambda r: res[:, following, r, :], norm1_pow, normed1)
                    if r >= R - 2:
                        lowered(following, turned1_high, turned1_low, r - (R - 2), TURN_BANKS)

        def looped(times, links, work):
            with v.Fori(0, times) as i:
                body[0], body[1], body[2] = i, 0, links
                work(i)
            assert body[1] == links, body[1]
            chain[0] += links * times
            body[0] = None

        loaded(v, "rows")
        embed(0)
        v.wait_ge(wq_all, 1)
        link(v.tensor_tensor(scales[:, 0:1], scales[:, 0:1], scales[:, 1:2], ALU.max))
        factors(0, 2)
        normed(0, lambda r: res[:, 0, r, :], norm1_pow, normed1)
        for n, rn in enumerate((C, E1)):
            v.wait_ge(wq_high, n + 1)
            v.scalar_tensor_tensor(out=wq16[n][:, 1, :], in0=wqkv[n][:, :], scalar=up[0:rn, 0:1], in1=wq16[n][:, 0, :],
                                   op0=ALU.mult, op1=ALU.subtract).then_inc(ready, 1)
        for half in range(2):
            lowered(0, turned1_high, turned1_low, half, TURN_BANKS)
        looped(B - 1, 3, lambda b: keys(b, b + 1))
        keys(B - 1, None)
        key_feature_kept.wait(v, B - 1, R)
        v.tensor_reduce(kmin[:, 0:1], kmax[:, :, :].rearrange("p b r -> p (b r)"), AX_X, ALU.max).then_inc(gmax, 1)
        prepare_mix()
        v.wait_ge(gmax_all, 1)
        v.tensor_scalar(kmin[:, 0:1], kmin[:, 1:2], -1.0, None, ALU.mult).then_inc(gmax_neg, 1)

        def attend(b, f):
            if f is not None:
                measured(lambda r: res[:, f, r, :], norm2_var)
                normed(f, lambda r: res[:, f, r, :], norm2_pow, normed2)
                forward(f, BEFORE)
            for s in range(R + 4):
                if s == 1:
                    for r in range(R):
                        key_exp.wait(v, b, r + 1)
                        v.tensor_scalar(ek[:, r, :], ek[:, r, :], FEPS, RATIO, ALU.add, ALU.mult).then_inc(key_feature_done.sem, 1)
                if s == 2:
                    kv_mm.wait(v, b, 1)
                    v.tensor_tensor(kvm[:, :, :], bank[0:2 * M, 6, 0:GR * 2 * VW].rearrange("p (g c) -> p g c", g=GR), kvmask[:, :, :], ALU.mult).then_inc(kv_kept.sem, 1)
                if s < R:
                    r = s
                    a, c = 0, 1
                    query_feature_mm.wait(v, b, r + 1)
                    if r >= 2:
                        query_turned_mm.wait(v, b, r - 1)
                    v.tensor_reduce(mq[:, r % 2, 0:8], bank[0:P, a, 0:FA].rearrange("p (h m) -> p h m", m=M), AX_X, ALU.max)
                    link(v.tensor_reduce(mq[:, r % 2, 8:12], bank[0:P, c, 0:FE - FA].rearrange("p (h m) -> p h m", m=M), AX_X, ALU.max))
                    link(v.tensor_tensor(mq[:, r % 2, :], bank[0:P, a, FA:FA + HEADS], mq[:, r % 2, :], ALU.add))
                    k = (mq, r % 2 * HEADS)
                    v.tensor_tensor(dq[:, r % 2, 0:FA].rearrange("p (h m) -> p h m", m=M), bank[0:P, a, 0:FA].rearrange("p (h m) -> p h m", m=M), wide(k, 0, 8), ALU.subtract)
                    v.tensor_tensor(dq[:, r % 2, FA:FE].rearrange("p (h m) -> p h m", m=M), bank[0:P, c, 0:FE - FA].rearrange("p (h m) -> p h m", m=M), wide(k, 8, 4), ALU.subtract).then_inc(query_feature_kept.sem, 1)
                if 0 <= s - 2 < R:
                    r = s - 2
                    mixed_mm.wait(v, b, r + 1)
                    if r >= 2:
                        mixed_turned_mm.wait(v, b, r - 1)
                    o = bank[0:P, 7, 0:HEADS * VW].rearrange("p (h c) -> p h c", c=VW)
                    link(v.reciprocal(zr[:, r % 2, :], o[:, :, HD]))
                    v.tensor_tensor(at[:, r % 2, :].rearrange("p (h d) -> p h d", d=HD), o[:, :, 0:HD],
                                    bass.AP(zr, r % 2 * HEADS, [[2 * HEADS, P], [1, HEADS], [0, HD]]), ALU.mult).then_inc(mixed_kept.sem, 1)
                if 0 <= s - 4 < R:
                    r = s - 4
                    attn_out_mm.wait(v, b, r + 1)
                    v.tensor_tensor(prb[:, r % 2, :], bank[0:P, 7, 256:256 + E], rows[:, 1, :], ALU.add).then_inc(attn_out_kept.sem, 1)
                    attn_out_kept.wait(v, b, r + 1)
                    last = v.tensor_tensor(res[:, b, r, :], res[:, b, r, :], prb[:, r % 2, :], ALU.add)
                    if r == R - 1:
                        link(last)
                forward(f, FILL[s])

        def forward(f, work):
            if f is None:
                return
            for what, half, r in work:
                if what == "turn":
                    lowered(f, turned2_high, turned2_low, half, FORWARD_BANKS)
                if what == "out":
                    if half == 0 and r == 0:
                        v.wait_ge(stored.sem, f * 32 + 32)
                    r += 3 * half
                    ffn_out_mm.wait(v, f, r + 1)
                    link(v.tensor_tensor(osb[:, r, :], bank[0:P, FORWARD_BANKS[r % 3 % 2], 0:E], rows[:, 2, :], ALU.add))
                    v.tensor_tensor(osb[:, r, :], osb[:, r, :], res[:, f, r, :], ALU.add).then_inc(ffn_out_done.sem, 1)

        prepare_forward()
        attend(0, None)
        looped(B - 1, 27, lambda f: attend(f + 1, f))
        measured(lambda r: res[:, B - 1, r, :], norm2_var)
        normed(B - 1, lambda r: res[:, B - 1, r, :], norm2_pow, normed2)
        for work in [BEFORE] + FILL:
            forward(B - 1, work)

    @block.tensor
    def _(pe):
        pe.wait_ge(made, 15)
        loaded(pe, "pm")
        loaded(pe, "pw")
        pe.transpose(bank[0:HD, 0, 0:M], pmn[:, :], ident[0:M, 0:M])
        pe.transpose(bank[:, 1, 0:C], pwn[0][:, :], ident[:, :])
        pe.transpose(bank[:, 1, C:E], pwn[1][:, :], ident[0:E1, 0:E1]).then_inc(weights_turned, 1)
        pe.wait_ge(weights_kept, 2)
        pe.matmul(bank[:, 2, 0:M], spread[:, :, :].rearrange("p h d -> p (h d)"), pmT[:, :], start=True, stop=True).then_inc(weights_turned, 1)
        def mm(out, pairs, inc=None):
            for n, (lhs, rhs) in enumerate(pairs):
                last = pe.matmul(out, lhs, rhs, start=(n == 0), stop=(n == len(pairs) - 1))
            if inc:
                last.then_inc(inc.sem, 1)

        def turn(b, need, done, half, banks):
            for k in range(3):
                r = 3 * half + k
                need.wait(pe, b, r + 1)
                pe.transpose(bank[0:C, banks[0], k * P:(k + 1) * P], xn[:, r, 0:C], ident[0:P, 0:P])
                last = pe.transpose(bank[0:E1, banks[1], k * P:(k + 1) * P], xn[:, r, C:E], ident[0:P, 0:P])
            last.then_inc(done.sem, 1)

        def parts(a, b):
            return [(a(0), b(0)), (a(0), b(1)), (a(1), b(0))]

        def project(src, col, done, banks):
            for half in range(2):
                for n, rn in enumerate((C, E1)):
                    c0 = col + n * C
                    mm(bank[:, banks[half][n], 0:HALF],
                       [op for k in range(2) for op in parts(lambda s: wq16[k][:, s, c0:c0 + C], lambda s: src(k, s, half))], done)

        def features(r, a, c, done):
            mm(bank[0:P, a, 0:FA], [(tile_(ft[0], r), feat[0][:, :, :].rearrange("p h m -> p (h m)"))])
            mm(bank[0:P, a, FA:FA + HEADS], [(tile_(sq[n], r), diag[n][:, :]) for n in range(2)])
            mm(bank[0:P, c, 0:FE - FA], [(tile_(ft[1], r), feat[1][:, :, :].rearrange("p h m -> p (h m)"))], done)

        def embed(b, q):
            mm(bank[0:P, EMBED_BANKS[q], 0:E], [(tile_(hcur, 2 * q), pwT[:, :])])
            mm(bank[0:P, EMBED_BANKS[q], E:2 * E], [(tile_(hcur, 2 * q + 1), pwT[:, :])], embed_mm)

        def values(b, q):
            for i in range(2):
                mm(bank[0:P, VALUE_BANKS[q], i * E:(i + 1) * E],
                   [op for k in range(2) for op in parts(lambda s: tile_(xc[k][:, s, :], 2 * q + i), lambda s: wq16[k][:, s, 2 * E:3 * E])], (None, value_mm)[i])

        def keys(b, following):
            turned1_low.wait(pe, b, 4)
            if following is not None:
                result_copied.wait(pe, following, 1)
                for q in range(R // 2):
                    embed(following, q)
            project(lambda k, s, half: xc[k][:, s, half * HALF:(half + 1) * HALF], E, key_mm, KEY_BANKS)
            for r in range(R):
                if r == 0:
                    key_kept.wait(pe, b, 4)
                    if following is not None:
                        norm1_var.wait(pe, following, 1)
                if r == 1:
                    key_kept.wait(pe, b, 8)
                if r >= 2:
                    key_feature_kept.wait(pe, b, r - 1)
                features(r, *FEATURE_BANKS[r % 2], key_feature_mm)
                if r == 0:
                    values(b, 0)
                if r == 1:
                    values(b, 1)
                if r == 2:
                    value_kept.wait(pe, b, 1)
                    values(b, 2)
                if following is not None and r >= R - 2:
                    if r == R - 1:
                        turned1_low.wait(pe, following, 2)
                    turn(following, normed1, turned1_mm, r - (R - 2), TURN_BANKS)

        result_copied.wait(pe, 0, 1)
        for q in range(R // 2):
            embed(0, q)
        turn(0, normed1, turned1_mm, 0, TURN_BANKS)
        turned1_low.wait(pe, 0, 2)
        turn(0, normed1, turned1_mm, 1, TURN_BANKS)
        pe.wait_ge(ready, 2)
        with pe.Fori(0, B - 1) as b:
            keys(b, b + 1)
        keys(B - 1, None)
        value_kept.wait(pe, B - 1, 3)
        key_feature_kept.wait(pe, B - 1, R)

        def turn_forward():
            pe.wait_ge(weights_kept, 3)
            for t in range(HT):
                pe.transpose(bank[:, 2 + t // 4, t % 4 * C:t % 4 * C + C], fcn[:, t, 0:C], ident[:, :])
                last = pe.transpose(bank[0:E1, 6 + t // 4, t % 4 * C:t % 4 * C + C], fcn[:, t, C:E], ident[:, :])
            last.then_inc(weights_turned, 1)
            loaded(pe, "w1")
            pe.wait_ge(weights_kept, 4)
            for t in range(HT):
                a = t % 2 * E
                pe.transpose(bank[:, W1_BANKS[t // 2], a:a + C], w1n[0][:, t * C:t * C + C], ident[:, :])
                last = pe.transpose(bank[:, W1_BANKS[t // 2], a + C:a + E], w1n[1][:, t * C:t * C + C], ident[0:E1, 0:E1])
            last.then_inc(weights_turned, 1)

            loaded(pe, "pr")

        def attend(b, f):
            if f is not None:
                query_feature_kept.wait(pe, b, 0)
                query_turned_kept.wait(pe, b, 0)
            project(lambda k, s, half: xt[k][:, b, s, half * HALF:(half + 1) * HALF], 0, query_mm, QUERY_BANKS)
            query_kept.wait(pe, b, 8)
            if f is None:
                turn_forward()
            forward(f, BEFORE)
            for s in range(R + 4):
                if s == 2:
                    key_feature_done.wait(pe, b, R)
                    if f is not None:
                        mixed_turned_kept.wait(pe, b, 0)
                    for g in range(GR):
                        for r in range(R):
                            pn = P - 1 if r == R - 1 else P
                            last = pe.matmul(bank[0:2 * M, 6, g * 2 * VW:(g + 1) * 2 * VW], ek[0:pn, r, g * 2 * M:(g + 1) * 2 * M],
                                             bass.AP(vals, b * (R * HEADS * VW) + (r * HEADS + 2 * g) * VW, [[B * R * HEADS * VW, pn], [1, 2 * VW]]),
                                             start=(r == 0), stop=(r == R - 1))
                    last.then_inc(kv_mm.sem, 1)
                if s < R:
                    if s >= 1:
                        query_feature_kept.wait(pe, b, s)
                    features(s, 0, 1, query_feature_mm)
                if 0 <= s - 1 < R:
                    r = s - 1
                    query_exp.wait(pe, b, r + 1)
                    if r >= 1:
                        query_turned_kept.wait(pe, b, 2 * r)
                    for g in range(GR):
                        last = pe.transpose(bank[0:2 * M, 4 + g // 4, g % 4 * P:g % 4 * P + P], dq[:, r % 2, g * 2 * M:(g + 1) * 2 * M], ident[0:P, 0:P])
                    last.then_inc(query_turned_mm.sem, 1)
                if 0 <= s - 2 < R:
                    r = s - 2
                    query_turned_kept.wait(pe, b, 2 * r + 2)
                    kv_kept.wait(pe, b, 1)
                    if r >= 3:
                        attn_out_kept.wait(pe, b, r - 2)
                    elif r == 0 and f is not None:
                        attn_out_kept.wait(pe, b, 0)
                    if r >= 1:
                        mixed_kept.wait(pe, b, r)
                    for g in range(GR):
                        last = pe.matmul(bank[0:P, 7, g * 2 * VW:(g + 1) * 2 * VW], q1T[:, r % 2, g, :], kvm[:, g, :], start=True, stop=True)
                    last.then_inc(mixed_mm.sem, 1)
                if 0 <= s - 3 < R:
                    r = s - 3
                    mixed_kept.wait(pe, b, r + 1)
                    if r >= 1:
                        mixed_turned_kept.wait(pe, b, 2 * r)
                    pe.transpose(bank[0:C, 6, 0:P], at[:, r % 2, 0:C], ident[0:P, 0:P])
                    pe.transpose(bank[0:E1, 6, 128:128 + P], at[:, r % 2, C:E], ident[0:P, 0:P]).then_inc(mixed_turned_mm.sem, 1)
                if 0 <= s - 4 < R:
                    r = s - 4
                    mixed_turned_kept.wait(pe, b, 2 * r + 2)
                    mixed_kept.wait(pe, b, min(R, r + 3))
                    if r >= 1:
                        attn_out_kept.wait(pe, b, r)
                    mm(bank[0:P, 7, 256:256 + E], [(atT[k][:, r % 2, :], wpr[k][:, :]) for k in range(2)], attn_out_mm)
                forward(f, FILL[s])

        def forward(f, work):
            if f is None:
                return
            for what, half, n in work:
                if what == "turn":
                    if half == 1 or not is_zero(f):
                        ffn_out_done.wait(pe, f, 3 * half)
                    turn(f, normed2, turned2_mm, half, FORWARD_BANKS)
                if what == "hidden":
                    if n == 0:
                        turned2_low.wait(pe, f, 2 * half + 2)
                    if n >= 2:
                        hidden_kept.wait(pe, f, HT * half + n - 1)
                    mm(bank[:, FORWARD_BANKS[n % 2], 0:HALF], 
                       [op for k in range(2) for op in parts(lambda s: w0T[k][:, s, n * C:(n + 1) * C], lambda s: xc[k][:, s, half * HALF:(half + 1) * HALF])], hidden_mm)
                if what == "out":
                    if n == 0:
                        hidden_kept.wait(pe, f, HT * (half + 1))
                    if n == 2:
                        ffn_out_done.wait(pe, f, 3 * half + 1)
                    mm(bank[0:P, FORWARD_BANKS[n % 2], 0:E], [(hid[:, t, n * P:(n + 1) * P], w1T[:, t, :]) for t in range(HT)], ffn_out_mm)

        attend(0, None)
        with pe.Fori(0, B - 1) as f:
            attend(f + 1, f)
        for work in [BEFORE] + FILL:
            forward(B - 1, work)


_CONV = [f"L0_tok_{k}{n}" for n in range(6) for k in ("cw", "cb", "gw", "gb")]
_REST = ["tok_pw", "tok_pb", "attn_W_qkv", "attn_W_proj", "attn_b_proj", "attn_proj_mat", "ffn_w_fc", "ffn_b_fc",
         "ffn_w_proj", "ffn_b_proj", "ffn_alpha_e", "ffn_alpha_r"]


def kernel(**inputs):
    import numpy as _np
    import concourse.bacc as _bacc
    from concourse import mybir as _mybir
    from concourse.bass_utils import run_bass_kernel_spmd as _run

    nc = _bacc.Bacc("TRN2", target_bir_lowering=False, num_devices=1)
    arrays, args = {}, {}
    for name in ["x"] + _CONV + ["L0_" + n for n in _REST]:
        a = _np.ascontiguousarray(inputs[name])
        if name.startswith("L0_tok_cw"):
            a = a.reshape(a.shape[0], -1)
        arrays[f"in_{name}"] = a
        args[name] = nc.dram_tensor(f"in_{name}", a.shape, _mybir.dt.from_np(a.dtype), kind="ExternalInput").ap()
    out = nc.dram_tensor("out", (B, R * P - 1, E), _mybir.dt.float32, kind="ExternalOutput").ap()
    audio_tower(nc, args["x"], [args[f"L0_tok_cw{n}"] for n in range(6)],
                [[args[f"L0_tok_{k}{n}"] for k in ("cb", "gw", "gb")] for n in range(6)],
                {n: args["L0_" + n] for n in _REST}, out)
    r = _run(nc, [arrays], core_ids=[0])
    return r.results[0]["out"]
```
